# Optimizing a Trainium2 kernel written in Bass

```python
import numpy as np
import jax
import jax.numpy as jnp

def _softmax(x, axis=-1):
    return jax.nn.softmax(x, axis=axis)

def _gelu(x):
    return jax.nn.gelu(x, approximate=True)

def _silu(x):
    return jax.nn.silu(x)

def _sigmoid(x):
    return jax.nn.sigmoid(x)

def _layernorm(x, axis=-1, eps=1e-05):
    m = jnp.mean(x, axis=axis, keepdims=True)
    v = jnp.var(x, axis=axis, keepdims=True)
    return (x - m) / jnp.sqrt(v + eps)

def _scatter_add(tgt, idx, src, axis=0):
    return tgt.at[idx].add(src)

def _segment_sum(src, seg, n):
    return jax.ops.segment_sum(src, seg, n)
kernel_name = 'mk_seq_postln_d2_jaxref_r8_03eb90'

def setup_inputs(seed: int=0):
    np.random.seed(seed)
    _w = jnp.asarray

    def _L0_attn_setup():
        import jax, jax.numpy as jnp
        import numpy as np
        B, N, DIM = (4, 128, 128)
        H, DH = (16, 64)
        NUM_MEM = 64
        TOPK = 64
        SCALE = DH ** (-0.5)

        def _split_heads(t):
            b, n, _ = t.shape
            return t.reshape(b, n, H, DH).transpose(0, 2, 1, 3)
        key = jax.random.key(seed)
        ks = jax.random.split(key, 10)
        d_inner = H * DH
        return {'x': jax.random.normal(ks[0], (B, N, DIM), dtype=jnp.float32), 'Wq': jax.random.normal(ks[1], (d_inner, DIM), dtype=jnp.float32) * 0.02, 'Wk': jax.random.normal(ks[2], (d_inner, DIM), dtype=jnp.float32) * 0.02, 'Wv': jax.random.normal(ks[3], (d_inner, DIM), dtype=jnp.float32) * 0.02, 'pre_proj': jax.random.normal(ks[4], (H, H), dtype=jnp.float32) * 0.1, 'post_proj': jax.random.normal(ks[5], (H, H), dtype=jnp.float32) * 0.1, 'mem_k': jax.random.normal(ks[6], (H, NUM_MEM, DH), dtype=jnp.float32), 'mem_v': jax.random.normal(ks[7], (H, NUM_MEM, DH), dtype=jnp.float32), 'Wout': jax.random.normal(ks[8], (DIM, d_inner), dtype=jnp.float32) * 0.02, 'bout': jnp.zeros((DIM,), dtype=jnp.float32)}
    _L0_attn_in = _L0_attn_setup()

    def _L0_ffn_setup():
        import jax, jax.numpy as jnp
        import numpy as np
        DIM = 128

        def _reference_tuple_inner(x, W_r, W_k, W_v, mu_r, mu_k):
            B, T, C = x.shape
            x_prev = jnp.concatenate([jnp.zeros((B, 1, C), x.dtype), x[:, :-1, :]], axis=1)
            xr = mu_r * x + (1.0 - mu_r) * x_prev
            xk = mu_k * x + (1.0 - mu_k) * x_prev
            r = jax.nn.sigmoid(jnp.einsum('btc,dc->btd', xr, W_r))
            k = jnp.einsum('btc,dc->btd', xk, W_k)
            k_act = jnp.square(jax.nn.relu(k))
            out = r * jnp.einsum('btc,dc->btd', k_act, W_v)
            new_state = x[:, -1, :]
            return (out, new_state)
        key = jax.random.key(seed)
        ks = jax.random.split(key, 6)
        B, T, C = (8, 256, DIM)
        x = jax.random.normal(ks[0], (B, T, C), dtype=jnp.float32)
        s = 1.0 / np.sqrt(C)
        W_r = jax.random.uniform(ks[1], (C, C), jnp.float32, -s, s)
        W_k = jax.random.uniform(ks[2], (C, C), jnp.float32, -s, s)
        W_v = jax.random.uniform(ks[3], (C, C), jnp.float32, -s, s)
        mu_r = jax.random.uniform(ks[4], (C,), jnp.float32)
        mu_k = jax.random.uniform(ks[5], (C,), jnp.float32)
        return {'x': x, 'W_r': W_r, 'W_k': W_k, 'W_v': W_v, 'mu_r': mu_r, 'mu_k': mu_k}
    _L0_ffn_in = _L0_ffn_setup()

    def _L1_attn_setup():
        import jax, jax.numpy as jnp
        import numpy as np
        NUM_HEADS = 16

        def _rope_tables(seq_len, head_dim, dtype):
            pos = jnp.arange(seq_len, dtype=jnp.float32)
            inv = jnp.power(10000.0, -2.0 * jnp.arange(head_dim // 2, dtype=jnp.float32) / head_dim)
            ang = pos[:, None] * inv[None, :]
            cos = jnp.repeat(jnp.cos(ang), 2, axis=-1).astype(dtype)
            sin = jnp.repeat(jnp.sin(ang), 2, axis=-1).astype(dtype)
            return (cos[None, None], sin[None, None])

        def _rotate_half_interleaved(x):
            x2 = jnp.stack([-x[..., 1::2], x[..., ::2]], axis=-1)
            return x2.reshape(x.shape)
        key = jax.random.key(seed)
        k0, k1, k2, k3 = jax.random.split(key, 4)
        B, N, C = (2, 256, 128)
        s = 1.0 / np.sqrt(C)
        return {'x': jax.random.normal(k0, (B, N, C), dtype=jnp.float32), 'Wq': jax.random.normal(k1, (C, C), dtype=jnp.float32) * s, 'Wk': jax.random.normal(k2, (C, C), dtype=jnp.float32) * s, 'Wv': jax.random.normal(k3, (C, C), dtype=jnp.float32) * s}
    _L1_attn_in = _L1_attn_setup()

    def _L1_ffn_setup():
        import jax, jax.numpy as jnp
        import numpy as np
        D_MODEL = 128
        D_FF = 512
        N_EXPERTS = 8
        INIT_SCALE = 0.1

        def _trunc_normal(key, shape, std):
            return std * jax.random.truncated_normal(key, -2.0, 2.0, shape, dtype=jnp.float32)
        key = jax.random.key(seed)
        ks = jax.random.split(key, 5)
        x = jax.random.normal(ks[0], (4, 128, D_MODEL), dtype=jnp.float32)
        router_W = _trunc_normal(ks[1], (D_MODEL, N_EXPERTS), INIT_SCALE / np.sqrt(D_MODEL))
        router_b = jnp.zeros((N_EXPERTS,), dtype=jnp.float32)
        W1 = _trunc_normal(ks[2], (N_EXPERTS, D_MODEL, D_FF), INIT_SCALE / np.sqrt(D_MODEL))
        b1 = jnp.zeros((N_EXPERTS, D_FF), dtype=jnp.float32)
        W2 = _trunc_normal(ks[3], (N_EXPERTS, D_FF, D_MODEL), INIT_SCALE / np.sqrt(D_FF))
        b2 = jnp.zeros((N_EXPERTS, D_MODEL), dtype=jnp.float32)
        return {'x': x, 'router_W': router_W, 'router_b': router_b, 'W1': W1, 'b1': b1, 'W2': W2, 'b2': b2}
    _L1_ffn_in = _L1_ffn_setup()
    _d = {'L0_attn_x': _L0_attn_in['x'], 'L0_attn_Wq': _L0_attn_in['Wq'], 'L0_attn_Wk': _L0_attn_in['Wk'], 'L0_attn_Wv': _L0_attn_in['Wv'], 'L0_attn_pre_proj': _L0_attn_in['pre_proj'], 'L0_attn_post_proj': _L0_attn_in['post_proj'], 'L0_attn_mem_k': _L0_attn_in['mem_k'], 'L0_attn_mem_v': _L0_attn_in['mem_v'], 'L0_attn_Wout': _L0_attn_in['Wout'], 'L0_attn_bout': _L0_attn_in['bout'], 'L0_ffn_W_r': _L0_ffn_in['W_r'], 'L0_ffn_W_k': _L0_ffn_in['W_k'], 'L0_ffn_W_v': _L0_ffn_in['W_v'], 'L0_ffn_mu_r': _L0_ffn_in['mu_r'], 'L0_ffn_mu_k': _L0_ffn_in['mu_k'], 'L1_attn_Wq': _L1_attn_in['Wq'], 'L1_attn_Wk': _L1_attn_in['Wk'], 'L1_attn_Wv': _L1_attn_in['Wv'], 'L1_ffn_router_W': _L1_ffn_in['router_W'], 'L1_ffn_router_b': _L1_ffn_in['router_b'], 'L1_ffn_W1': _L1_ffn_in['W1'], 'L1_ffn_b1': _L1_ffn_in['b1'], 'L1_ffn_W2': _L1_ffn_in['W2'], 'L1_ffn_b2': _L1_ffn_in['b2']}
    _x0 = _d['L0_attn_x']
    _d['L0_attn_x'] = jax.random.normal(jax.random.fold_in(jax.random.key(seed), 1), (32, 256, 128), dtype=_x0.dtype)
    del _x0
    return _d

def reference(L0_attn_x, L0_attn_Wq, L0_attn_Wk, L0_attn_Wv, L0_attn_pre_proj, L0_attn_post_proj, L0_attn_mem_k, L0_attn_mem_v, L0_attn_Wout, L0_attn_bout, L0_ffn_W_r, L0_ffn_W_k, L0_ffn_W_v, L0_ffn_mu_r, L0_ffn_mu_k, L1_attn_Wq, L1_attn_Wk, L1_attn_Wv, L1_ffn_router_W, L1_ffn_router_b, L1_ffn_W1, L1_ffn_b1, L1_ffn_W2, L1_ffn_b2):

    def _L0_attn_ref(x, Wq, Wk, Wv, pre_proj, post_proj, mem_k, mem_v, Wout, bout):
        import jax, jax.numpy as jnp
        import numpy as np
        B, N, DIM = (4, 128, 128)
        H, DH = (16, 64)
        NUM_MEM = 64
        TOPK = 64
        SCALE = DH ** (-0.5)

        def _split_heads(t):
            b, n, _ = t.shape
            return t.reshape(b, n, H, DH).transpose(0, 2, 1, 3)
        b, n, _ = x.shape
        q = _split_heads(x @ Wq.T)
        k = _split_heads(x @ Wk.T)
        v = _split_heads(x @ Wv.T)
        mk = jnp.broadcast_to(mem_k[None], (b, H, NUM_MEM, DH))
        mv = jnp.broadcast_to(mem_v[None], (b, H, NUM_MEM, DH))
        k = jnp.concatenate([mk, k], axis=2)
        v = jnp.concatenate([mv, v], axis=2)
        j_len = n + NUM_MEM
        dots = jnp.einsum('bhid,bhjd->bhij', q, k) * SCALE
        dots = jnp.einsum('bhij,hk->bkij', dots, pre_proj)
        mask_value = -jnp.finfo(dots.dtype).max
        offset = j_len - n
        i_idx = jnp.arange(n)[:, None]
        j_idx = jnp.arange(j_len)[None, :]
        causal = j_idx > i_idx + offset
        dots = jnp.where(causal[None, None], mask_value, dots)
        kth = jax.lax.top_k(dots, TOPK)[0][..., -1:]
        dots = jnp.where(dots < kth, mask_value, dots)
        attn = jax.nn.softmax(dots, axis=-1)
        attn = jnp.einsum('bhij,hk->bkij', attn, post_proj)
        out = jnp.einsum('bhij,bhjd->bhid', attn, v)
        out = out.transpose(0, 2, 1, 3).reshape(b, n, H * DH)
        return out @ Wout.T + bout

    def _L0_ffn_ref(x, W_r, W_k, W_v, mu_r, mu_k):
        import jax, jax.numpy as jnp
        import numpy as np
        DIM = 128

        def _reference_tuple_inner(x, W_r, W_k, W_v, mu_r, mu_k):
            B, T, C = x.shape
            x_prev = jnp.concatenate([jnp.zeros((B, 1, C), x.dtype), x[:, :-1, :]], axis=1)
            xr = mu_r * x + (1.0 - mu_r) * x_prev
            xk = mu_k * x + (1.0 - mu_k) * x_prev
            r = jax.nn.sigmoid(jnp.einsum('btc,dc->btd', xr, W_r))
            k = jnp.einsum('btc,dc->btd', xk, W_k)
            k_act = jnp.square(jax.nn.relu(k))
            out = r * jnp.einsum('btc,dc->btd', k_act, W_v)
            new_state = x[:, -1, :]
            return (out, new_state)
        return _reference_tuple_inner(x, W_r, W_k, W_v, mu_r, mu_k)[0]

    def _L1_attn_ref(x, Wq, Wk, Wv):
        import jax, jax.numpy as jnp
        import numpy as np
        NUM_HEADS = 16

        def _rope_tables(seq_len, head_dim, dtype):
            pos = jnp.arange(seq_len, dtype=jnp.float32)
            inv = jnp.power(10000.0, -2.0 * jnp.arange(head_dim // 2, dtype=jnp.float32) / head_dim)
            ang = pos[:, None] * inv[None, :]
            cos = jnp.repeat(jnp.cos(ang), 2, axis=-1).astype(dtype)
            sin = jnp.repeat(jnp.sin(ang), 2, axis=-1).astype(dtype)
            return (cos[None, None], sin[None, None])

        def _rotate_half_interleaved(x):
            x2 = jnp.stack([-x[..., 1::2], x[..., ::2]], axis=-1)
            return x2.reshape(x.shape)
        B, N, C = x.shape
        H = NUM_HEADS
        D = C // H
        scale = D ** (-0.5)

        def heads(y):
            return y.reshape(B, N, H, D).transpose(0, 2, 1, 3)
        q = heads(x @ Wq.T)
        k = heads(x @ Wk.T)
        v = heads(x @ Wv.T)
        cos, sin = _rope_tables(N, D, x.dtype)
        q = q * cos + _rotate_half_interleaved(q) * sin
        k = k * cos + _rotate_half_interleaved(k) * sin
        attn = jnp.einsum('bhnd,bhmd->bhnm', q, k) * scale
        attn = jax.nn.softmax(attn, axis=-1)
        out = jnp.einsum('bhnm,bhmd->bhnd', attn, v)
        return out.transpose(0, 2, 1, 3).reshape(B, N, C)

    def _L1_ffn_ref(x, router_W, router_b, W1, b1, W2, b2):
        import jax, jax.numpy as jnp
        import numpy as np
        D_MODEL = 128
        D_FF = 512
        N_EXPERTS = 8
        INIT_SCALE = 0.1

        def _trunc_normal(key, shape, std):
            return std * jax.random.truncated_normal(key, -2.0, 2.0, shape, dtype=jnp.float32)
        logits = jnp.einsum('bsd,de->bse', x.astype(jnp.float32), router_W) + router_b
        probs = jax.nn.softmax(logits, axis=-1)
        top1 = jnp.argmax(probs, axis=-1)
        mask = jax.nn.one_hot(top1, N_EXPERTS, dtype=x.dtype)
        gates = mask * probs.astype(x.dtype)
        h = jax.nn.relu(jnp.einsum('bsd,edf->besf', x, W1) + b1[:, None, :])
        y = jnp.einsum('besf,efd->besd', h, W2) + b2[:, None, :]
        out = jnp.einsum('bse,besd->bsd', gates, y)
        return out
    x = L0_attn_x
    x = _layernorm(x + _L0_attn_ref(x, L0_attn_Wq, L0_attn_Wk, L0_attn_Wv, L0_attn_pre_proj, L0_attn_post_proj, L0_attn_mem_k, L0_attn_mem_v, L0_attn_Wout, L0_attn_bout), axis=-1)
    x = _layernorm(x + _L0_ffn_ref(x, L0_ffn_W_r, L0_ffn_W_k, L0_ffn_W_v, L0_ffn_mu_r, L0_ffn_mu_k), axis=-1)
    x = _layernorm(x + _L1_attn_ref(x, L1_attn_Wq, L1_attn_Wk, L1_attn_Wv), axis=-1)
    x = _layernorm(x + _L1_ffn_ref(x, L1_ffn_router_W, L1_ffn_router_b, L1_ffn_W1, L1_ffn_b1, L1_ffn_W2, L1_ffn_b2), axis=-1)
    return x

_drawn_inputs = setup_inputs


def setup_inputs(seed=0):
    import zlib

    import numpy as np

    out = dict(_drawn_inputs(seed))
    spreads = {'L0_attn_bout': (0.0, 0.1),
     'L1_ffn_router_b': (0.0, 0.459),
     'L1_ffn_b1': (0.0, 0.8),
     'L1_ffn_b2': (0.0, 0.502)}
    factors = {'L0_attn_Wq': 3.386,
     'L0_attn_Wk': 8.0,
     'L0_attn_Wv': 8.0,
     'L0_attn_pre_proj': 3.336,
     'L0_attn_mem_k': 3.571,
     'L0_ffn_W_r': 3.086,
     'L0_ffn_mu_r': 6.108,
     'L1_ffn_router_W': 4.769,
     'L1_ffn_W1': 8.0,
     'L1_ffn_W2': 8.0}
    for name, (base, spread) in spreads.items():
        noise = np.random.default_rng([zlib.crc32(name.encode()), seed]).standard_normal(out[name].shape)
        drawn = base * np.exp(spread * noise) if base else spread * noise
        out[name] = jnp.asarray(drawn.astype(out[name].dtype))
    for name, factor in factors.items():
        out[name] = (out[name] * factor).astype(out[name].dtype)
    return out
```

```python
from contextlib import ExitStack

import concourse.bass as bass
from concourse import mybir

F32 = mybir.dt.float32
ALU = mybir.AluOpType
ACT = mybir.ActivationFunctionType
AX = mybir.AxisListType

P = 128
T = 2
TOK = T * P
H = 16
MEM = 64
DH = 64
TOPK = 64
CH = H * DH // P
D1 = P // H
EXP = 8
FF = 512
STEPS = 8
RING = STEPS + 2
W0 = MEM + P
W1 = MEM + TOK
COLS = ((0, W0), (W0, W0 + W1))
BIG = 3.4028234663852886e38
EPS = 1e-5

USES = ("s1_0", "s1_1", "s_0", "s_1", "pg", "pu", "ptm", "pt_0", "pt_1", "h_0", "h_1", "p1_0", "p1_1", "y")
NBANK = 6
EXTRA = {"xt": 3, "x3t": 4, "lg": 5, "gt": 4, "base": 5,
         "x1t": 4, "kr": 5, "v": 0, "x2t": 1, "q": 2, "k": 3, "vv": 4}


def bank_of(use, par=0):
    return EXTRA[use] if use in EXTRA else (USES.index(use) + 2 * par) % NBANK


class Count:

    def __init__(self):
        self.n = 0

    def up(self):
        self.n += 1
        return 1

    def reset(self):
        n, self.n = self.n, 0
        return n


def flags(it, nb):
    lag = {"L": -2, "P": -1, "A": 0, "F": 1, "B": 2, "C": 3, "D": 4}
    return {s for s, n in lag.items() if 0 <= it - n < nb}


def build(nc, a, nb):
    with ExitStack() as ctx:
        def sb(name, *shape):
            return ctx.enter_context(nc.sbuf_tensor(name, [shape[0], *shape[1:]], F32))

        def sem(name):
            return ctx.enter_context(nc.semaphore(name))

        ident = sb("ident", P, P)
        ones = sb("ones", P, P)
        A_all = sb("A_all", P, H, P)
        B_all = sb("B_all", P, H, P)
        UM = sb("UM", MEM, H, P)
        keys = sb("keys", P, STEPS, 2, MEM + TOK)
        vals = sb("vals", P, RING, T, 2, P)
        WkT, WrT, WvT = (sb(n, P, P) for n in ("WkT", "WrT", "WvT"))
        qW, qWr, kW, kWr, vW = (sb(n, P, P) for n in ("qW", "qWr", "kW", "kWr", "vW"))
        cosT, sinT = sb("cosT", P, TOK), sb("sinT", P, TOK)
        hmask = sb("hmask", P, H)
        mu_r, mu_k = sb("mu_r", P, 1), sb("mu_k", P, 1)
        brow = sb("brow", 1, P)
        rW = sb("rW", P, EXP)
        rb = sb("rb", 1, EXP)
        b1c = sb("b1c", P, EXP, FF // P)
        W2 = sb("W2", P, EXP, FF // P, P)
        b2 = sb("b2", EXP, P)
        first = sb("first", P, EXP)
        minus_half = sb("minus_half", P, 3 * T)
        A_st = [sb(f"A_st{i}", P, 2, P) for i in range(2)]
        W1_st = [sb(f"W1_st{i}", P, FF) for i in range(2)]
        xload = sb("xload", P, T, P)
        xres = sb("xres", P, T, P)
        xT_next = sb("xT_next", P, TOK)
        xT = sb("xT", P, TOK)
        S = [sb(f"S{i}", P, 2, W0 + W1) for i in range(2)]
        work = sb("work", P, 2, W0 + W1)
        E = sb("E", P, 2, W0 + W1)
        Pr = [sb(f"Pr{i}", P, 2, W0 + W1) for i in range(2)]
        top = sb("top", P, 4, 8)
        best = sb("best", P, 4, 8)
        negmax = sb("negmax", P, 4)
        psumA = sb("psumA", P, 4)
        rsumA = [sb(f"rsumA{i}", P, 4) for i in range(2)]
        PTm = sb("PTm", MEM, 4, P)
        PT = [sb(f"PT{i}", P, 3, P) for i in range(2)]
        x1 = sb("x1", P, T, P)
        x1T = sb("x1T", P, 1 + TOK)
        dT, xrT, xkT = sb("dT", P, TOK), sb("xrT", P, TOK), sb("xkT", P, TOK)
        th = sb("th", P, T, P)
        rk = sb("rk", P, TOK)
        kact = sb("kact", P, TOK)
        x2 = sb("x2", P, T, P)
        x2res = sb("x2res", P, T, P)
        x2pre = sb("x2pre", P, T, P)
        x2T = sb("x2T", P, TOK)
        rope = sb("rope", P, 4, TOK)
        qT, kT = sb("qT", P, TOK), sb("kT", P, TOK)
        keys1 = sb("keys1", P, H, TOK)
        vals1 = sb("vals1", P, T, H, D1 + 1)
        negmax1 = sb("negmax1", P, T, 2)
        max1 = sb("max1", P, T, 2)
        E1 = sb("E1", P, T, 2, TOK)
        E1T = [sb(f"E1T{i}", P, T, T, P) for i in range(2)]
        rsum1 = sb("rsum1", P, T, H)
        o1 = sb("o1", P, T, P)
        x3pre = sb("x3pre", P, T, P)
        x3 = sb("x3", P, T, P)
        x3T = sb("x3T", P, TOK)
        lg = sb("lg", P, 6, T, EXP)
        lgs = sb("lgs", P, 4, T)
        gates = sb("gates", P, T, EXP)
        gT = sb("gT", EXP, TOK)
        hT = [sb(f"hT{i}", P, 2, TOK) for i in range(2)]
        yacc = sb("yacc", P, T, P)
        yout = sb("yout", P, T, P)
        stats = sb("stats", P, 3, T, 6)
        mv = sb("mv", P, 3, T, 2)
        rstd = sb("rstd", P, 3, T)
        var = sb("var", P, 3, T)
        stats2, mv2, rstd2, var2 = sb("stats2", P, T, 6), sb("mv2", P, T, 2), sb("rstd2", P, T), sb("var2", P, T)

        bank = [ctx.enter_context(nc.psum_tensor(f"bank{i}", [P, 512], F32)) for i in range(NBANK)]
        acc_bank = ctx.enter_context(nc.psum_tensor("acc_bank", [P, 512], F32))
        pv_bank = ctx.enter_context(nc.psum_tensor("pv_bank", [P, 512], F32))
        acc = acc_bank[:, 0:TOK].rearrange("p (t c) -> p t c", t=T)
        pv = pv_bank[:, 0:T * H * (D1 + 1)].rearrange("p (t h e) -> p t h e", t=T, h=H)

        nat = keys1[:, :, :].rearrange("p h j -> p (h j)")
        WqN, WkN, WvN, WoN = (nat[:, i * CH * P:(i + 1) * CH * P].rearrange("p (c k) -> p c k", c=CH) for i in range(4))
        slab = [vals[:, :, :, :, :].rearrange("p r t h c -> p (r t h c)")[:, i * H * P:(i + 1) * H * P] for i in range(2)]
        mkN = work[0:MEM, :, :].rearrange("p h j -> p (h j)")
        mvN = E[0:MEM, :, :].rearrange("p h j -> p (h j)")
        WoT = S[0][:, :, :].rearrange("p h j -> p (h j)")
        mkT = S[1][:, 0, :]
        mvT = S[1][:, 1, :]
        preB, postB = rope[:, 0, :], rope[:, 1, :]
        preX = rope[:, 2, 0:CH * H].rearrange("p (c k) -> p c k", c=CH)
        postX = rope[:, 3, 0:CH * H].rearrange("p (c k) -> p c k", c=CH)
        smallN = E1[:, :, :, :].rearrange("p t h j -> p (t h j)")

        w_big = sem("w_big")
        w_small = sem("w_small")
        consts_ready = sem("consts_ready")
        turned = sem("turned")
        turned_out = sem("turned_out")
        slab_ready = sem("slab_ready")
        slab_free = sem("slab_free")
        fold_full = sem("fold_full")
        fold_out = sem("fold_out")
        setup_done = sem("setup_done")
        bank_free = [sem(f"bank{i}_free") for i in range(NBANK)]
        A_full, A_free = [sem(f"A_full{i}") for i in range(2)], [sem(f"A_free{i}") for i in range(2)]
        W1_full, W1_free = [sem(f"W1_full{i}") for i in range(2)], [sem(f"W1_free{i}") for i in range(2)]
        xload_full = sem("xload_full")
        xload_free = sem("xload_free")
        xres_full = sem("xres_full")
        xres_free = sem("xres_free")
        xt_full = sem("xt_full")
        xt_ready = sem("xt_ready")
        xT_ready = sem("xT_ready")
        pg_full = sem("pg_full")
        pu_full = sem("pu_full")
        s_full = sem("s_full")
        s_out = sem("s_out")
        s_masked = sem("s_masked")
        S_free = sem("S_free")
        negmax_ready = sem("negmax_ready")
        E_ready = sem("E_ready")
        P_free = sem("P_free")
        kept_ready = sem("kept_ready")
        probs_ready = sem("probs_ready")
        pt_full = sem("pt_full")
        pt_ready = sem("pt_ready")
        acc_full = sem("acc_full")
        var_ready = sem("var_ready")
        rstd_ready = sem("rstd_ready")
        x1_ready = sem("x1_ready")
        x1t_full = sem("x1t_full")
        x1T_ready = sem("x1T_ready")
        mixed_ready = sem("mixed_ready")
        kr_full = sem("kr_full")
        kact_ready = sem("kact_ready")
        v_full = sem("v_full")
        x2_ready = sem("x2_ready")
        x2t_full = sem("x2t_full")
        x2T_ready = sem("x2T_ready")
        x2_saved = sem("x2_saved")
        q_full = sem("q_full")
        k_full = sem("k_full")
        vv_full = sem("vv_full")
        kT_ready = sem("kT_ready")
        keys1_ready = sem("keys1_ready")
        vals1_ready = sem("vals1_ready")
        s1_full = sem("s1_full")
        negmax1_ready = sem("negmax1_ready")
        E1_ready = sem("E1_ready")
        p1_full = sem("p1_full")
        p1_ready = sem("p1_ready")
        pv_full = sem("pv_full")
        x3_ready = sem("x3_ready")
        x3t_full = sem("x3t_full")
        x3T_ready = sem("x3T_ready")
        lg_full = sem("lg_full")
        lg_shifted = sem("lg_shifted")
        lg_exp = sem("lg_exp")
        gates_ready = sem("gates_ready")
        gt_full = sem("gt_full")
        gT_ready = sem("gT_ready")
        base_full = sem("base_full")
        h_full = sem("h_full")
        h_ready = sem("h_ready")
        y_full = sem("y_full")
        yout_full = sem("yout_full")
        yout_free = sem("yout_free")
        dve_did = sem("dve_did")
        pool_did = sem("pool_did")
        act_did = sem("act_did")

        def iterations(eng, iteration):
            for it in range(-1, 4):
                iteration(it, flags(it, nb))
            with eng.Fori(4, nb - 2) as it:
                iteration(it, set("LPAFBCD"))
            for it in range(nb - 2, nb + 4):
                iteration(it, flags(it, nb))

        def middle_steps(eng, step):
            with eng.Fori(0, (STEPS - 2) // 2) as q:
                step(2 * q + 1, 1)
                step(2 * q + 2, 0)

        def psum(use, par=0):
            return bank[bank_of(use, par)]

        block = ctx.enter_context(nc.Block())

        @block.sync
        def _(sp):
            for dst, w in ((WqN, "L0_attn_Wq"), (WkN, "L0_attn_Wk"), (WvN, "L0_attn_Wv")):
                sp.dma_start(dst, a[w].rearrange("(c p) k -> p c k", p=P)).then_inc(w_big, 16)
            sp.dma_start(WoN, a["L0_attn_Wout"].rearrange("p (c k) -> p c k", c=CH)).then_inc(w_big, 16)
            for dst, w in ((mkN, "L0_attn_mem_k"), (mvN, "L0_attn_mem_v")):
                sp.dma_start(dst.rearrange("j (h d) -> j h d", h=H), a[w].rearrange("h j d -> j h d")).then_inc(w_big, 16)
            for dst, w in ((preB, "L0_attn_pre_proj"), (postB, "L0_attn_post_proj")):
                sp.dma_start(dst, a[w].rearrange("h k -> (h k)").partition_broadcast(P)).then_inc(w_big, 16)
            for n, w in enumerate(("L0_ffn_W_r", "L0_ffn_W_k", "L0_ffn_W_v", "L1_attn_Wq", "L1_attn_Wk", "L1_attn_Wv")):
                sp.dma_start(smallN[:, n * P:(n + 1) * P], a[w]).then_inc(w_big, 16)
            x_in = a["L0_attn_x"].rearrange("b (t p) c -> b p t c", p=P)
            out = a["out"].rearrange("b (t p) c -> b p t c", p=P)
            sp.dma_start(xload[:, :, :], x_in[0]).then_inc(xload_full, 16)
            sp.dma_start(xres[:, :, :], x_in[0]).then_inc(xres_full, 16)
            for dst, w in ((mu_r, "L0_ffn_mu_r"), (mu_k, "L0_ffn_mu_k")):
                sp.dma_start(dst[:, :], a[w].rearrange("(p o) -> p o", o=1)).then_inc(w_small, 16)
            for dst, w in ((brow, "L0_attn_bout"), (rb, "L1_ffn_router_b")):
                sp.dma_start(dst[:, :], a[w].rearrange("(o c) -> o c", o=1)).then_inc(w_small, 16)
            sp.dma_start(rW[:, :], a["L1_ffn_router_W"]).then_inc(w_small, 16)
            with nc.allow_non_contiguous_dma(reason="4096 biases, once"):
                for e in range(EXP):
                    sp.dma_start(b1c[:, e, :], a["L1_ffn_b1"][e].rearrange("(f p) -> p f", p=P)).then_inc(w_small, 16)
            for e in range(EXP):
                sp.dma_start(W2[:, e, :, :], a["L1_ffn_W2"][e].rearrange("(f p) d -> p f d", p=P)).then_inc(w_small, 16)
            for dst, w in ((b2, "L1_ffn_b2"), (cosT, "cosT"), (sinT, "sinT")):
                sp.dma_start(dst[:, :], a[w]).then_inc(w_small, 16)
            sp.wait_ge(setup_done, 1)
            for f in (*A_free, *W1_free):
                sp.sem_inc(f, 1)

            def stage_weights(n, par, on):
                if "P" in on:
                    sp.wait_ge(A_free[par], 1)
                    sp.sem_inc(A_free[par], -1)
                    sp.dma_start(A_st[par][:, :, :], A_all[:, bass.ds(2 * n, 2), :]).then_inc(A_full[par], 16)
                if "C" in on:
                    sp.wait_ge(W1_free[par], 1)
                    sp.sem_inc(W1_free[par], -1)
                    sp.dma_start(W1_st[par][:, :], a["L1_ffn_W1"][n]).then_inc(W1_full[par], 16)

            def iteration(it, on):
                stage_weights(0, 0, on)
                if on & {"P", "C"}:
                    middle_steps(sp, lambda n, par: stage_weights(n, par, on))
                stage_weights(STEPS - 1, 1, on)
                if {"A", "P"} <= on:
                    sp.wait_ge(xres_free, 1)
                    sp.sem_inc(xres_free, -1)
                    sp.dma_start(xres[:, :, :], x_in[it + 1]).then_inc(xres_full, 16)
                if "L" in on:
                    sp.wait_ge(xload_free, 1)
                    sp.sem_inc(xload_free, -1)
                    sp.dma_start(xload[:, :, :], x_in[it + 2]).then_inc(xload_full, 16)
                if "D" in on:
                    sp.wait_ge(yout_full, 1)
                    sp.sem_inc(yout_full, -1)
                    sp.dma_start(out[it - 4], yout[:, :, :]).then_inc(yout_free, 16)

            iterations(sp, iteration)
            sp.wait_ge(yout_free, 16)

        @block.gpsimd
        def _(pool):
            seq = Count()
            for dst, value in ((ones[:, :], 1.0), (ident[:, :], 0.0), (hmask[:, :], 1.0), (minus_half[:, :], -0.5),
                               (x1T[:, 0:1], 0.0), (vals1[:, :, :, :], 1.0)):
                pool.memset(dst, value).then_inc(pool_did, seq.up())
            for e in range(EXP):
                pool.memset(first[:, e:e + 1], float(EXP - e)).then_inc(pool_did, seq.up())
            pool.wait_ge(pool_did, seq.n)
            pool.affine_select(out=ident[:, :], in_=ident[:, :], compare_op=ALU.not_equal, fill=1.0, base=0,
                               pattern=[[-1, P]], channel_multiplier=1).then_inc(pool_did, seq.up())
            pool.affine_select(out=hmask[:, :], in_=hmask[:, :], compare_op=ALU.is_ge, fill=0.0, base=0,
                               pattern=[[-D1, H]], channel_multiplier=1).then_inc(pool_did, seq.up())
            pool.wait_ge(pool_did, seq.n)
            pool.affine_select(out=hmask[:, :], in_=hmask[:, :], compare_op=ALU.is_ge, fill=0.0, base=D1 - 1,
                               pattern=[[D1, H]], channel_multiplier=-1).then_inc(pool_did, seq.up())
            pool.wait_ge(pool_did, seq.n)
            pool.sem_inc(pool_did, -seq.reset())
            pool.sem_inc(consts_ready, 2)
            pool.wait_ge(setup_done, 1)

            def mask(par, nxt):
                for h in range(2):
                    pool.wait_ge(s_out, 1)
                    pool.sem_inc(s_out, -1)
                    pool.sem_inc(bank_free[bank_of(f"s_{h}", par)], 1)
                    for c0, c1 in COLS:
                        diag = S[nxt][:, h, c1 - P:c1]
                        last = pool.affine_select(out=diag, in_=diag, compare_op=ALU.is_ge, fill=-BIG, base=0,
                                                  pattern=[[-1, P]], channel_multiplier=1)
                last.then_inc(s_masked, 1)

            def normalise(par):
                pool.wait_ge(kept_ready, 1)
                pool.sem_inc(kept_ready, -1)
                pool.sem_inc(S_free, 1)
                for h in range(2):
                    for t, (c0, c1) in enumerate(COLS):
                        u = 2 * h + t
                        last = pool.tensor_scalar(Pr[par][:, h, c0:c1], Pr[par][:, h, c0:c1], rsumA[par][:, u:u + 1], 1.0,
                                                  ALU.mult, ALU.mult)
                last.then_inc(probs_ready, 1)

            def rstd_of(out_, scratch, v, half):
                pool.wait_ge(var_ready, 1)
                pool.sem_inc(var_ready, -1)
                pool.tensor_scalar(scratch, v, EPS, 1.0, ALU.add, ALU.mult).then_inc(pool_did, seq.up())
                pool.wait_ge(pool_did, seq.n)
                pool.tensor_tensor(out_, scratch, half, ALU.pow).then_inc(rstd_ready, 1)
                pool.wait_ge(pool_did, seq.n)
                pool.sem_inc(pool_did, -seq.reset())

            def step(n, par, on, last=False):
                if ("P" if last else "A") in on:
                    mask(par, 1 - par)
                if "A" in on:
                    normalise(par)

            def iteration(it, on):
                cols = [i for i, s in enumerate("FCD") if s in on]
                if cols:
                    lo, hi = cols[0], cols[-1] + 1
                    rstd_of(rstd[:, lo:hi, :], var[:, lo:hi, :], mv[:, lo:hi, :, 1],
                            minus_half[:, 0:(hi - lo) * T].rearrange("p (a t) -> p a t", t=T))
                if "B" in on:
                    pool.tensor_copy(x2res[:, :, :], x2[:, :, :]).then_inc(x2_saved, 1)
                step(0, 0, on)
                if "A" in on:
                    middle_steps(pool, lambda n, par: step(n, par, on))
                step(STEPS - 1, 1, on, last=True)
                if "F" in on:
                    rstd_of(rstd2[:, :], var2[:, :], mv2[:, :, 1], minus_half[:, 0:T])
                    pool.wait_ge(kT_ready, 1)
                    pool.sem_inc(kT_ready, -1)
                    pool.tensor_tensor(keys1[:, :, :], kT[:, :].unsqueeze(1).broadcast_to([P, H, TOK]),
                                       hmask[:, :].unsqueeze(2).broadcast_to([P, H, TOK]), ALU.mult).then_inc(keys1_ready, 1)

            iterations(pool, iteration)

        @block.scalar
        def _(act):
            act.preload_act_table_set("exp_and_others")
            seq = Count()

            def copy(dst, src, **kw):
                return act.activation(dst, src, ACT.Copy, **kw)

            act.wait_ge(turned, 1)
            copy(WoT[:, 0:512], bank[0][:, :])
            copy(WoT[:, 512:1024], bank[1][:, :])
            copy(mkT, bank[2][:, :])
            copy(mvT, bank[3][:, :])
            for i, w in enumerate((WrT, WkT, WvT, qW)):
                copy(w[:, :], bank[4][:, i * P:(i + 1) * P])
            for i, w in enumerate((kW, vW)):
                last = copy(w[:, :], bank[5][:, i * P:(i + 1) * P])
            last.then_inc(turned_out, 2)
            act.wait_ge(fold_full, 1)
            scale = float(DH) ** -0.5
            A_flat = A_all[:, :, :].rearrange("p k c -> p (k c)")
            for b in range(4):
                copy(A_flat[:, b * 512:(b + 1) * 512], bank[b][:, :], scale=scale)
            for s in range(STEPS):
                last = copy(keys[:, s, :, 0:MEM],
                            bank[4 + s // 4][:, (s % 4) * P:(s % 4 + 1) * P].rearrange("p (h j) -> p h j", h=2), scale=scale)
            last.then_inc(fold_out, 1)
            act.wait_ge(fold_full, 2)
            B_flat = B_all[:, :, :].rearrange("p k c -> p (k c)")
            U_flat = UM[:, :, :].rearrange("p k c -> p (k c)")
            for b, mem in enumerate((bank[4], bank[5], acc_bank, pv_bank)):
                copy(B_flat[:, b * 512:(b + 1) * 512], bank[b][:, :])
                last = copy(U_flat[:, b * 512:(b + 1) * 512], mem[0:MEM, :])
            last.then_inc(act_did, seq.up())
            act.wait_ge(act_did, seq.n)
            act.sem_inc(act_did, -seq.reset())
            act.wait_ge(consts_ready, 3)
            act.wait_ge(w_small, 24 * 16)
            act.sem_inc(setup_done, 1)
            act.sem_inc(S_free, 2)

            def exp1(n, par):
                act.wait_ge(negmax1_ready, 1)
                act.sem_inc(negmax1_ready, -1)
                for t in range(T):
                    for h in range(2):
                        last = act.activation(E1[:, t, h, :], psum(f"s1_{t}", par)[:, h * TOK:(h + 1) * TOK], ACT.Exp,
                                              bias=negmax1[:, t, h:h + 1], scale=float(D1) ** -0.5)
                last.then_inc(act_did, seq.up())
                act.wait_ge(act_did, seq.n)
                act.sem_inc(act_did, -seq.reset())
                act.sem_inc(E1_ready, 1)
                act.sem_inc(bank_free[bank_of("s1_0", par)], 1)
                act.sem_inc(bank_free[bank_of("s1_1", par)], 1)

            def scores_out(par):
                act.wait_ge(S_free, 1)
                act.sem_inc(S_free, -1)
                for h in range(2):
                    act.wait_ge(s_full, 1)
                    act.sem_inc(s_full, -1)
                    copy(S[1 - par][:, h, :], psum(f"s_{h}", par)[:, :]).then_inc(s_out, 1)

            def projections_out(it, n, par):
                act.wait_ge(pg_full, 1)
                act.sem_inc(pg_full, -1)
                copy(keys[:, n, :, MEM:MEM + TOK], psum("pg", par)[:, :].rearrange("p (h j) -> p h j", h=2))\
                    .then_inc(bank_free[bank_of("pg", par)], 1)
                act.wait_ge(pu_full, 1)
                act.sem_inc(pu_full, -1)
                act.sem_inc(A_free[par], 1)
                copy(vals[:, (STEPS * (it + 1) + n) % RING, :, :, :].rearrange("p t h c -> p (t h c)"), psum("pu", par)[:, :])\
                    .then_inc(bank_free[bank_of("pu", par)], 1)

            def probs_out(par):
                act.wait_ge(pt_full, 1)
                act.sem_inc(pt_full, -1)
                copy(PTm[:, :, :].rearrange("p u i -> p (u i)"), psum("ptm", par)[0:MEM, :])
                for h in range(2):
                    act.wait_ge(pt_full, 1)
                    act.sem_inc(pt_full, -1)
                    if h == 1:
                        act.sem_inc(P_free, 1)
                    copy(PT[h][:, :, :].rearrange("p u i -> p (u i)"), psum(f"pt_{h}", par)[:, 0:3 * P]).then_inc(pt_ready, 1)

            def hidden_out(n, par):
                for b in range(2):
                    act.wait_ge(h_full, 1)
                    act.sem_inc(h_full, -1)
                    if b == 1:
                        act.sem_inc(W1_free[par], 1)
                    for f in range(2):
                        last = act.activation(hT[b][:, f, :], psum(f"h_{b}", par)[:, f * TOK:(f + 1) * TOK], ACT.Relu,
                                              bias=b1c[:, n, 2 * b + f:2 * b + f + 1])
                    last.then_inc(h_ready, 1)

            def probs1_out(par):
                for h in range(2):
                    act.wait_ge(p1_full, 1)
                    act.sem_inc(p1_full, -1)
                    copy(E1T[h][:, :, :, :].rearrange("p a b i -> p (a b i)"), psum(f"p1_{h}", par)[:, :]).then_inc(p1_ready, 1)

            def exp_scores(par):
                act.wait_ge(negmax_ready, 1)
                act.sem_inc(negmax_ready, -1)
                for h in range(2):
                    for t, (c0, c1) in enumerate(COLS):
                        u = 2 * h + t
                        last = act.activation(E[:, h, c0:c1], S[par][:, h, c0:c1], ACT.Exp, bias=negmax[:, u:u + 1])
                last.then_inc(E_ready, 1)

            def step(it, n, par, on, first=False, last=False):
                if "B" in on:
                    exp1(n, par)
                if ("P" if last else "A") in on:
                    scores_out(par)
                if first and {"A", "P"} <= on:
                    act.sem_inc(xres_free, 1)
                if "P" in on:
                    projections_out(it, n, par)
                if "A" in on and not first:
                    probs_out(par)
                if "C" in on:
                    hidden_out(n, par)
                if "B" in on:
                    probs1_out(par)
                if "A" in on:
                    exp_scores(par)

            def bank_out(dst, src, full, ready):
                act.wait_ge(full, 1)
                act.sem_inc(full, -1)
                copy(dst, src).then_inc(ready, 1)

            def iteration(it, on):
                if "F" in on:
                    probs_out(0)
                if "C" in on:
                    bank_out(x3T[:, :], psum("x3t")[:, 0:TOK], x3t_full, x3T_ready)
                    act.wait_ge(lg_shifted, 1)
                    act.sem_inc(lg_shifted, -1)
                    act.activation(lg[:, 1, :, :], lg[:, 0, :, :], ACT.Exp).then_inc(lg_exp, 1)
                    bank_out(gT[:, :], psum("gt")[0:EXP, 0:TOK], gt_full, gT_ready)
                if "P" in on:
                    bank_out(xT_next[:, :], psum("xt")[:, 0:TOK], xt_full, xt_ready)
                    if "L" in on:
                        act.sem_inc(xload_free, 1)
                step(it, 0, 0, on, first=True)
                if on & {"A", "P", "B", "C"}:
                    middle_steps(act, lambda n, par: step(it, n, par, on))
                if "P" in on:
                    copy(xT[:, :], xT_next[:, :]).then_inc(xT_ready, 1)
                step(it, STEPS - 1, 1, on, last=True)
                if "F" in on:
                    bank_out(x1T[:, 1:1 + TOK], psum("x1t")[:, 0:TOK], x1t_full, x1T_ready)
                    act.wait_ge(kr_full, 1)
                    act.sem_inc(kr_full, -1)
                    act.activation(rk[:, :], psum("kr")[:, 0:TOK], ACT.Relu).then_inc(act_did, seq.up())
                    act.activation(th[:, :, :].rearrange("p t c -> p (t c)"), psum("kr")[:, TOK:2 * TOK], ACT.Tanh, scale=0.5)
                    act.wait_ge(act_did, seq.n)
                    act.activation(kact[:, :], rk[:, :], ACT.Square).then_inc(kact_ready, 1)
                    act.wait_ge(act_did, seq.n)
                    act.sem_inc(act_did, -seq.reset())
                    bank_out(x2T[:, :], psum("x2t")[:, 0:TOK], x2t_full, x2T_ready)
                    bank_out(vals1[:, :, :, 0:D1], psum("vv")[:, 0:TOK].rearrange("p (t h d) -> p t h d", t=T, h=H),
                             vv_full, vals1_ready)

            iterations(act, iteration)

        @block.vector
        def _(dve):
            seq = Count()
            dve.wait_ge(w_big, 14 * 16)
            pre_hk = preB.rearrange("p (h k) -> p h k", h=H)
            post_hk = postB.rearrange("p (k h) -> p h k", h=H)
            for half in range(2):
                rows = slice(half * DH, (half + 1) * DH)
                dve.tensor_copy(preX[rows, :, :], pre_hk[rows, half:H:2, :]).then_inc(dve_did, seq.up())
                dve.tensor_copy(postX[rows, :, :], post_hk[rows, half:H:2, :]).then_inc(dve_did, seq.up())
            dve.wait_ge(dve_did, seq.n)

            def make_slab(n, w, mix):
                if n >= 2:
                    dve.wait_ge(slab_free, n - 1)
                dve.tensor_tensor(slab[n % 2].rearrange("p (k c) -> p k c", k=H), w.unsqueeze(1).broadcast_to([P, H, P]),
                                  mix.unsqueeze(2).broadcast_to([P, H, P]), ALU.mult).then_inc(slab_ready, 1)

            for c in range(CH):
                make_slab(c, WqN[:, c, :], preX[:, c, :])
            dve.wait_ge(turned_out, 2)
            for w, wr in ((qW, qWr), (kW, kWr)):
                dve.tensor_scalar(wr[:, 0:P:2], w[:, 1:P:2], -1.0, None, ALU.mult).then_inc(dve_did, seq.up())
                dve.tensor_copy(wr[:, 1:P:2], w[:, 0:P:2]).then_inc(dve_did, seq.up())
            dve.wait_ge(dve_did, seq.n)
            dve.sem_inc(dve_did, -seq.reset())
            dve.sem_inc(consts_ready, 1)
            for c in range(CH):
                make_slab(CH + c, WoT[:, c * P:(c + 1) * P], postX[:, c, :])
            dve.wait_ge(setup_done, 1)
            dve.sem_inc(P_free, 2)
            dve.sem_inc(yout_free, 16)

            def max1_of(par):
                for t in range(T):
                    dve.wait_ge(s1_full, 1)
                    dve.sem_inc(s1_full, -1)
                    dve.tensor_reduce(max1[:, t, :], psum(f"s1_{t}", par)[:, :].rearrange("p (h j) -> p h j", h=2),
                                      AX.X, ALU.max).then_inc(dve_did, seq.up())
                dve.wait_ge(dve_did, seq.n)
                dve.tensor_scalar(negmax1[:, :, :], max1[:, :, :], -float(D1) ** -0.5, None, ALU.mult).then_inc(negmax1_ready, 1)
                dve.wait_ge(dve_did, seq.n)
                dve.sem_inc(dve_did, -seq.reset())

            def top_64(par):
                units = [(2 * h + t, h, c0, c1) for h in range(2) for t, (c0, c1) in enumerate(COLS)]
                dve.wait_ge(s_masked, 1)
                dve.sem_inc(s_masked, -1)
                for u, h, c0, c1 in units:
                    dve.max(best[:, u, :], S[par][:, h, c0:c1]).then_inc(dve_did, seq.up())
                seen = {u: u + 1 for u, _, _, _ in units}
                dve.wait_ge(dve_did, seq.n)
                dve.tensor_scalar(negmax[:, :], best[:, :, 0], -1.0, None, ALU.mult).then_inc(negmax_ready, 1)
                for r in range(1, TOPK // 8):
                    src, eight = (S[par], best) if r == 1 else (work, top)
                    for u, h, c0, c1 in units:
                        dve.wait_ge(dve_did, seen[u])
                        dve.match_replace(work[:, h, c0:c1], eight[:, u, :], src[:, h, c0:c1], -BIG).then_inc(dve_did, seq.up())
                        seen[u] = seq.n
                    for u, h, c0, c1 in units:
                        dve.wait_ge(dve_did, seen[u])
                        dve.max(top[:, u, :], work[:, h, c0:c1]).then_inc(dve_did, seq.up())
                        seen[u] = seq.n
                dve.wait_ge(dve_did, seq.n)
                dve.wait_ge(E_ready, 1)
                dve.sem_inc(E_ready, -1)
                dve.wait_ge(P_free, 1)
                dve.sem_inc(P_free, -1)
                for u, h, c0, c1 in units:
                    dve.scalar_tensor_tensor(out=Pr[par][:, h, c0:c1], in0=S[par][:, h, c0:c1], scalar=top[:, u, 7:8],
                                             in1=E[:, h, c0:c1], op0=ALU.is_ge, op1=ALU.mult,
                                             accum_out=psumA[:, u:u + 1]).then_inc(dve_did, seq.up())
                dve.wait_ge(dve_did, seq.n)
                dve.reciprocal(rsumA[par][:, :], psumA[:, :]).then_inc(kept_ready, 1)
                dve.wait_ge(dve_did, seq.n)
                dve.sem_inc(dve_did, -seq.reset())

            def add_expert(n, par):
                dve.wait_ge(y_full, 1)
                dve.sem_inc(y_full, -1)
                for t in range(T):
                    dve.scalar_tensor_tensor(out=yacc[:, t, :], in0=psum("y", par)[:, t * P:(t + 1) * P],
                                             scalar=gates[:, t, bass.ds(n, 1)], in1=yacc[:, t, :],
                                             op0=ALU.mult, op1=ALU.add).then_inc(dve_did, seq.up())
                dve.wait_ge(dve_did, seq.n)
                dve.sem_inc(dve_did, -seq.reset())
                dve.sem_inc(bank_free[bank_of("y", par)], 1)

            def statistics(src, st, m):
                for t in range(T):
                    dve.bn_stats(st[:, t, :], src[:, t, :]).then_inc(dve_did, seq.up())
                dve.wait_ge(dve_did, seq.n)
                for t in range(T):
                    last = dve.bn_aggr(m[:, t, :], st[:, t, :])
                    last.then_inc(dve_did, seq.up())

            def normalised(dst, src, m, r, done):
                for t in range(T):
                    last = dve.tensor_scalar(dst[:, t, :], src[:, t, :], m[:, t, 0:1], r[:, t:t + 1], ALU.subtract, ALU.mult)
                last.then_inc(done, 1)

            def over_experts(x):
                return x.unsqueeze(2).broadcast_to([P, T, EXP])

            def route():
                dve.wait_ge(lg_full, 1)
                dve.sem_inc(lg_full, -1)
                raw = psum("lg")[:, 0:T * EXP].rearrange("p (t e) -> p t e", t=T)
                dve.tensor_reduce(lgs[:, 0, :], raw, AX.X, ALU.max).then_inc(dve_did, seq.up())
                dve.wait_ge(dve_did, seq.n)
                dve.tensor_tensor(lg[:, 0, :, :], raw, over_experts(lgs[:, 0, :]), ALU.subtract).then_inc(lg_shifted, 1)
                dve.wait_ge(lg_exp, 1)
                dve.sem_inc(lg_exp, -1)
                dve.tensor_reduce(lgs[:, 1, :], lg[:, 1, :, :], AX.X, ALU.add).then_inc(dve_did, seq.up())
                dve.wait_ge(dve_did, seq.n)
                dve.reciprocal(lgs[:, 2, :], lgs[:, 1, :]).then_inc(dve_did, seq.up())
                dve.wait_ge(dve_did, seq.n)
                dve.tensor_tensor(lg[:, 2, :, :], lg[:, 1, :, :], over_experts(lgs[:, 2, :]), ALU.mult).then_inc(dve_did, seq.up())
                dve.wait_ge(dve_did, seq.n)
                dve.tensor_reduce(lgs[:, 3, :], lg[:, 2, :, :], AX.X, ALU.max).then_inc(dve_did, seq.up())
                dve.wait_ge(dve_did, seq.n)
                dve.tensor_tensor(lg[:, 3, :, :], lg[:, 2, :, :], over_experts(lgs[:, 3, :]), ALU.is_ge).then_inc(dve_did, seq.up())
                dve.wait_ge(dve_did, seq.n)
                dve.tensor_tensor(lg[:, 4, :, :], lg[:, 3, :, :], first[:, :].unsqueeze(1).broadcast_to([P, T, EXP]),
                                  ALU.mult).then_inc(dve_did, seq.up())
                dve.wait_ge(dve_did, seq.n)
                dve.tensor_reduce(lgs[:, 0, :], lg[:, 4, :, :], AX.X, ALU.max).then_inc(dve_did, seq.up())
                dve.wait_ge(dve_did, seq.n)
                dve.tensor_tensor(lg[:, 5, :, :], lg[:, 4, :, :], over_experts(lgs[:, 0, :]), ALU.is_ge).then_inc(dve_did, seq.up())
                dve.wait_ge(dve_did, seq.n)
                dve.tensor_tensor(gates[:, :, :], lg[:, 5, :, :], lg[:, 2, :, :], ALU.mult).then_inc(gates_ready, 1)
                dve.wait_ge(base_full, 1)
                dve.sem_inc(base_full, -1)
                dve.tensor_tensor(yacc[:, :, :], psum("base")[:, 0:TOK].rearrange("p (t c) -> p t c", t=T), x3[:, :, :],
                                  ALU.add).then_inc(dve_did, seq.up())
                dve.wait_ge(dve_did, seq.n)
                dve.sem_inc(dve_did, -seq.reset())
                dve.sem_inc(bank_free[bank_of("base")], 1)

            def step(n, par, on):
                if "B" in on:
                    max1_of(par)
                if "A" in on:
                    top_64(par)
                if "C" in on:
                    add_expert(n, par)

            def iteration(it, on):
                if "D" in on:
                    statistics(yacc, stats[:, 2, :, :], mv[:, 2, :, :])
                if "C" in on:
                    dve.wait_ge(pv_full, 1)
                    dve.sem_inc(pv_full, -1)
                    dve.reciprocal(rsum1[:, :, :], pv[:, :, :, D1]).then_inc(dve_did, seq.up())
                    dve.wait_ge(dve_did, seq.n)
                    o1_h = o1[:, :, :].rearrange("p t (h d) -> p t h d", h=H)
                    dve.tensor_tensor(o1_h, pv[:, :, :, 0:D1], rsum1[:, :, :].unsqueeze(3).broadcast_to([P, T, H, D1]),
                                      ALU.mult).then_inc(dve_did, seq.up())
                    dve.wait_ge(dve_did, seq.n)
                    dve.tensor_tensor(x3pre[:, :, :], o1[:, :, :], x2res[:, :, :], ALU.add).then_inc(dve_did, seq.up())
                    dve.wait_ge(dve_did, seq.n)
                    statistics(x3pre, stats[:, 1, :, :], mv[:, 1, :, :])
                if "F" in on:
                    dve.wait_ge(acc_full, 1)
                    dve.sem_inc(acc_full, -1)
                    statistics(acc, stats[:, 0, :, :], mv[:, 0, :, :])
                if on & {"F", "C", "D"}:
                    dve.wait_ge(dve_did, seq.n)
                    dve.sem_inc(dve_did, -seq.reset())
                    dve.sem_inc(var_ready, 1)
                    dve.wait_ge(rstd_ready, 1)
                    dve.sem_inc(rstd_ready, -1)
                if "C" in on:
                    normalised(x3, x3pre, mv[:, 1, :, :], rstd[:, 1, :], x3_ready)
                if "F" in on:
                    normalised(x1, acc, mv[:, 0, :, :], rstd[:, 0, :], x1_ready)
                if "D" in on:
                    dve.wait_ge(yout_free, 16)
                    dve.sem_inc(yout_free, -16)
                    normalised(yout, yacc, mv[:, 2, :, :], rstd[:, 2, :], yout_full)
                if "C" in on:
                    route()
                step(0, 0, on)
                if on & {"A", "B", "C"}:
                    middle_steps(dve, lambda n, par: step(n, par, on))
                step(STEPS - 1, 1, on)
                if "B" in on:
                    dve.wait_ge(x2_saved, 1)
                    dve.sem_inc(x2_saved, -1)
                if "F" in on:
                    channel_mix()
                    project1()

            def channel_mix():
                dve.wait_ge(x1T_ready, 1)
                dve.sem_inc(x1T_ready, -1)
                dve.tensor_tensor(dT[:, :], x1T[:, 1:1 + TOK], x1T[:, 0:TOK], ALU.subtract).then_inc(dve_did, seq.up())
                dve.wait_ge(dve_did, seq.n)
                for dst, mu in ((xrT, mu_r), (xkT, mu_k)):
                    last = dve.scalar_tensor_tensor(out=dst[:, :], in0=dT[:, :], scalar=mu[:, 0:1], in1=x1T[:, 0:TOK],
                                                    op0=ALU.mult, op1=ALU.add)
                last.then_inc(mixed_ready, 1)
                dve.wait_ge(v_full, 1)
                dve.sem_inc(v_full, -1)
                v = psum("v")[:, 0:TOK].rearrange("p (t c) -> p t c", t=T)
                dve.scalar_tensor_tensor(out=x2pre[:, :, :], in0=th[:, :, :], scalar=1.0, in1=v, op0=ALU.add, op1=ALU.mult).then_inc(dve_did, seq.up())
                dve.wait_ge(dve_did, seq.n)
                dve.sem_inc(bank_free[bank_of("v")], 1)
                dve.scalar_tensor_tensor(out=x2pre[:, :, :], in0=x2pre[:, :, :], scalar=0.5, in1=x1[:, :, :],
                                         op0=ALU.mult, op1=ALU.add).then_inc(dve_did, seq.up())
                dve.wait_ge(dve_did, seq.n)
                statistics(x2pre, stats2, mv2)
                dve.wait_ge(dve_did, seq.n)
                dve.sem_inc(dve_did, -seq.reset())
                dve.sem_inc(var_ready, 1)
                dve.wait_ge(rstd_ready, 1)
                dve.sem_inc(rstd_ready, -1)
                normalised(x2, x2pre, mv2, rstd2, x2_ready)

            def project1():
                for i, (use, full, dst) in enumerate((("q", q_full, qT), ("k", k_full, kT))):
                    dve.wait_ge(full, 1)
                    dve.sem_inc(full, -1)
                    for j, table in enumerate((cosT, sinT)):
                        dve.tensor_tensor(rope[:, 2 * i + j, :], psum(use)[:, j * TOK:(j + 1) * TOK], table[:, :], ALU.mult).then_inc(dve_did, seq.up())
                    dve.wait_ge(dve_did, seq.n)
                    dve.sem_inc(bank_free[bank_of(use)], 1)
                    last = dve.tensor_tensor(dst[:, :], rope[:, 2 * i, :], rope[:, 2 * i + 1, :], ALU.add)
                last.then_inc(kT_ready, 1)
                dve.wait_ge(dve_did, seq.n)
                dve.sem_inc(dve_did, -seq.reset())

            iterations(dve, iteration)

        @block.tensor
        def _(pe):
            pe.wait_ge(consts_ready, 2)
            pe.wait_ge(w_big, 14 * 16)
            for c in range(CH):
                pe.transpose(bank[c // 4][:, (c % 4) * P:(c % 4 + 1) * P], WoN[:, c, :], ident[:, :])
                pe.transpose(bank[2][:, c * MEM:(c + 1) * MEM], mkN[:, c * P:(c + 1) * P], ident[0:MEM, 0:MEM])
                pe.transpose(bank[3][:, c * MEM:(c + 1) * MEM], mvN[:, c * P:(c + 1) * P], ident[0:MEM, 0:MEM])
            for i, (b, k) in enumerate(((4, 0), (4, 1), (4, 2), (4, 3), (5, 0), (5, 1))):
                last = pe.transpose(bank[b][:, k * P:(k + 1) * P], smallN[:, i * P:(i + 1) * P], ident[:, :])
            last.then_inc(turned, 1)
            pe.wait_ge(turned_out, 2)
            for c in range(CH):
                pe.wait_ge(slab_ready, c + 1)
                for b in range(4):
                    pe.matmul(bank[b][:, :], WkN[:, c, :], slab[c % 2][:, b * 512:(b + 1) * 512], start=(c == 0), stop=(c == CH - 1))
                for k in range(H):
                    last = pe.matmul(bank[4 + k // 8][:, (k % 8) * MEM:(k % 8 + 1) * MEM], slab[c % 2][:, k * P:(k + 1) * P],
                                     mkT[:, c * MEM:(c + 1) * MEM], start=(c == 0 and k % 8 == 0), stop=(c == CH - 1),
                                     skip_group_check=True)
                last.then_inc(slab_free, 1)
            pe.drain().then_inc(fold_full, 1)
            pe.wait_ge(fold_out, 1)
            for c in range(CH):
                pe.wait_ge(slab_ready, CH + c + 1)
                for b, mem in enumerate((bank[4], bank[5], acc_bank, pv_bank)):
                    sl = slab[c % 2][:, b * 512:(b + 1) * 512]
                    pe.matmul(bank[b][:, :], WvN[:, c, :], sl, start=(c == 0), stop=(c == CH - 1))
                    last = pe.matmul(mem[0:MEM, :], mvT[:, c * MEM:(c + 1) * MEM], sl, start=(c == 0), stop=(c == CH - 1))
                last.then_inc(slab_free, 1)
            pe.drain().then_inc(fold_full, 1)
            pe.wait_ge(setup_done, 1)
            for f in bank_free:
                pe.sem_inc(f, 1)

            def take_bank(use, par=0):
                pe.wait_ge(bank_free[bank_of(use, par)], 1)
                pe.sem_inc(bank_free[bank_of(use, par)], -1)
                return psum(use, par)

            def give_bank(use, par=0):
                pe.sem_inc(bank_free[bank_of(use, par)], 1)

            def scores1(n, par):
                for t in range(T):
                    b = take_bank(f"s1_{t}", par)
                    pe.matmul(b[:, :].rearrange("p (h j) -> p h j", h=2), qT[:, t * P:(t + 1) * P],
                              keys1[:, bass.ds(2 * n, 2), :], start=True, stop=True).then_inc(s1_full, 1)

            def scores(n, par):
                for h in range(2):
                    b = take_bank(f"s_{h}", par)
                    pe.matmul(b[:, 0:W0], xT[:, 0:P], keys[:, n, h, 0:W0], start=True, stop=True)
                    pe.matmul(b[:, W0:W0 + W1], xT[:, P:TOK], keys[:, n, h, :], start=True, stop=True).then_inc(s_full, 1)

            def project(n, par):
                pe.wait_ge(A_full[par], 16)
                pe.sem_inc(A_full[par], -16)
                b = take_bank("pg", par)
                for h in range(2):
                    last = pe.matmul(b[:, h * TOK:(h + 1) * TOK], A_st[par][:, h, :], xT_next[:, :], start=True, stop=True)
                last.then_inc(pg_full, 1)
                b = take_bank("pu", par)
                for t in range(T):
                    last = pe.matmul(b[:, t * TOK:(t + 1) * TOK].rearrange("p (h c) -> p h c", h=2),
                                     xT_next[:, t * P:(t + 1) * P], B_all[:, bass.ds(2 * n, 2), :], start=True, stop=True)
                last.then_inc(pu_full, 1)

            def attend(prev, head0, ring, par, last_of_batch=False):
                pe.wait_ge(probs_ready, 1)
                pe.sem_inc(probs_ready, -1)
                b = take_bank("ptm", par)
                for h in range(2):
                    for t, (c0, c1) in enumerate(COLS):
                        last = pe.transpose(b[0:MEM, (2 * h + t) * P:(2 * h + t + 1) * P], Pr[prev][:, h, c0:c0 + MEM], ident[:, :])
                last.then_inc(pt_full, 1)
                for h in range(2):
                    b = take_bank(f"pt_{h}", par)
                    for i, c0 in enumerate((MEM, W0 + MEM, W0 + MEM + P)):
                        last = pe.transpose(b[:, i * P:(i + 1) * P], Pr[prev][:, h, c0:c0 + P], ident[:, :])
                    last.then_inc(pt_full, 1)
                for h in range(2):
                    pe.wait_ge(pt_ready, 1)
                    pe.sem_inc(pt_ready, -1)
                    if h == 0:
                        give_bank("ptm", par)
                    give_bank(f"pt_{h}", par)
                    for t in range(T):
                        pe.matmul(acc[:, t, :], PTm[:, 2 * h + t, :], UM[:, head0 + h, :], start=False, stop=False,
                                  skip_group_check=True)
                    for i, (t, jt) in enumerate(((0, 0), (1, 0), (1, 1))):
                        last = pe.matmul(acc[:, t, :], PT[h][:, i, :], vals[:, ring, jt, h, :], start=False,
                                         stop=last_of_batch and h == 1 and i != 1, skip_group_check=True)
                if last_of_batch:
                    last.then_inc(acc_full, 1)

            def hidden(n, par):
                pe.wait_ge(W1_full[par], 16)
                pe.sem_inc(W1_full[par], -16)
                for i in range(2):
                    b = take_bank(f"h_{i}", par)
                    for f in range(2):
                        c = 2 * i + f
                        last = pe.matmul(b[:, f * TOK:(f + 1) * TOK], W1_st[par][:, c * P:(c + 1) * P], x3T[:, :], start=True, stop=True)
                    last.then_inc(h_full, 1)

            def attend1(n, par, last_of_batch):
                pe.wait_ge(E1_ready, 1)
                pe.sem_inc(E1_ready, -1)
                for h in range(2):
                    b = take_bank(f"p1_{h}", par)
                    for jt in range(T):
                        for t in range(T):
                            last = pe.transpose(b[:, (2 * jt + t) * P:(2 * jt + t + 1) * P], E1[:, t, h, jt * P:(jt + 1) * P], ident[:, :])
                    last.then_inc(p1_full, 1)
                for h in range(2):
                    pe.wait_ge(p1_ready, 1)
                    pe.sem_inc(p1_ready, -1)
                    give_bank(f"p1_{h}", par)
                    for t in range(T):
                        for jt in range(T):
                            last = pe.matmul(pv[:, t, 2 * n + h, :], E1T[h][:, jt, t, :], vals1[:, jt, 2 * n + h, :],
                                             start=(jt == 0), stop=(jt == T - 1))
                if last_of_batch:
                    last.then_inc(pv_full, 1)

            def experts_out(n, par):
                b = take_bank("y", par)
                for i in range(2):
                    pe.wait_ge(h_ready, 1)
                    pe.sem_inc(h_ready, -1)
                    give_bank(f"h_{i}", par)
                for t in range(T):
                    for f in range(FF // P):
                        last = pe.matmul(b[:, t * P:(t + 1) * P], hT[f // 2][:, f % 2, t * P:(t + 1) * P], W2[:, n, f, :],
                                         start=(f == 0), stop=(f == FF // P - 1))
                last.then_inc(y_full, 1)

            def step(it, n, par, on, first=False, last=False):
                if "B" in on:
                    scores1(n, par)
                if "A" in on and not last:
                    scores(n + 1, par)
                if "P" in on and last:
                    pe.wait_ge(xT_ready, 1)
                    pe.sem_inc(xT_ready, -1)
                    scores(0, par)
                if "P" in on:
                    project(n, par)
                if "A" in on and not first:
                    attend(1 - par, 2 * n - 2, (STEPS * it + n - 1) % RING, par)
                if "C" in on:
                    hidden(n, par)
                if "B" in on:
                    attend1(n, par, last)
                if "C" in on:
                    experts_out(n, par)

            def turn(use, src, full):
                b = take_bank(use)
                for t in range(T):
                    last = pe.transpose(b[:, t * P:(t + 1) * P], src[:, t, :], ident[:, :])
                last.then_inc(full, 1)

            def per_tile(b, c0, lhsT, w):
                for t in range(T):
                    last = pe.matmul(b[:, c0 + t * P:c0 + (t + 1) * P], lhsT[:, t * P:(t + 1) * P], w[:, :], start=True, stop=True)
                return last

            def iteration(it, on):
                if "B" in on:
                    pe.wait_ge(vals1_ready, 1)
                    pe.sem_inc(vals1_ready, -1)
                    give_bank("vv")
                if "F" in on:
                    attend(1, H - 2, (STEPS * it - 1) % RING, 0, last_of_batch=True)
                if "C" in on:
                    pe.wait_ge(x3_ready, 1)
                    pe.sem_inc(x3_ready, -1)
                    turn("x3t", x3, x3t_full)
                    pe.wait_ge(x3T_ready, 1)
                    pe.sem_inc(x3T_ready, -1)
                    give_bank("x3t")
                    b = take_bank("lg")
                    for t in range(T):
                        pe.matmul(b[:, t * EXP:(t + 1) * EXP], x3T[:, t * P:(t + 1) * P], rW[:, :], start=True, stop=False)
                        last = pe.matmul(b[:, t * EXP:(t + 1) * EXP], ones[0:1, :], rb[:, :], start=False, stop=True)
                    last.then_inc(lg_full, 1)
                    pe.wait_ge(gates_ready, 1)
                    pe.sem_inc(gates_ready, -1)
                    give_bank("lg")
                    b = take_bank("gt")
                    for t in range(T):
                        last = pe.transpose(b[0:EXP, t * P:(t + 1) * P], gates[:, t, :], ident[:, :])
                    last.then_inc(gt_full, 1)
                    pe.wait_ge(gT_ready, 1)
                    pe.sem_inc(gT_ready, -1)
                    give_bank("gt")
                    per_tile(take_bank("base"), 0, gT, b2).then_inc(base_full, 1)
                if "P" in on:
                    pe.wait_ge(xload_full, 16)
                    pe.sem_inc(xload_full, -16)
                    turn("xt", xload, xt_full)
                    pe.wait_ge(xt_ready, 1)
                    pe.sem_inc(xt_ready, -1)
                    give_bank("xt")
                if "B" in on:
                    pe.wait_ge(keys1_ready, 1)
                    pe.sem_inc(keys1_ready, -1)
                if "F" in on:
                    pe.wait_ge(x1_ready, 1)
                    pe.sem_inc(x1_ready, -1)
                if "A" in on:
                    pe.wait_ge(xres_full, 16)
                    pe.sem_inc(xres_full, -16)
                    pe.matmul(acc_bank[:, 0:TOK], ident[:, :], xres[:, :, :].rearrange("p t c -> p (t c)"), start=True, stop=False,
                              skip_group_check=True)
                    for t in range(T):
                        pe.matmul(acc[:, t, :], ones[0:1, :], brow[:, :], start=False, stop=False, skip_group_check=True)
                step(it, 0, 0, on, first=True)
                if on & {"A", "P", "B", "C"}:
                    middle_steps(pe, lambda n, par: step(it, n, par, on))
                step(it, STEPS - 1, 1, on, last=True)
                if "F" in on:
                    turn("x1t", x1, x1t_full)
                    pe.wait_ge(mixed_ready, 1)
                    pe.sem_inc(mixed_ready, -1)
                    give_bank("x1t")
                    b = take_bank("kr")
                    pe.matmul(b[:, 0:TOK], WkT[:, :], xkT[:, :], start=True, stop=True)
                    per_tile(b, TOK, xrT, WrT).then_inc(kr_full, 1)
                    pe.wait_ge(kact_ready, 1)
                    pe.sem_inc(kact_ready, -1)
                    give_bank("kr")
                    per_tile(take_bank("v"), 0, kact, WvT).then_inc(v_full, 1)
                    pe.wait_ge(x2_ready, 1)
                    pe.sem_inc(x2_ready, -1)
                    turn("x2t", x2, x2t_full)
                    pe.wait_ge(x2T_ready, 1)
                    pe.sem_inc(x2T_ready, -1)
                    give_bank("x2t")
                    for use, w, wr, full in (("q", qW, qWr, q_full), ("k", kW, kWr, k_full)):
                        b = take_bank(use)
                        pe.matmul(b[:, 0:TOK], w[:, :], x2T[:, :], start=True, stop=True)
                        pe.matmul(b[:, TOK:2 * TOK], wr[:, :], x2T[:, :], start=True, stop=True).then_inc(full, 1)
                    per_tile(take_bank("vv"), 0, x2T, vW).then_inc(vv_full, 1)

            iterations(pe, iteration)


INPUTS = ("L0_attn_x", "L0_attn_Wq", "L0_attn_Wk", "L0_attn_Wv", "L0_attn_pre_proj", "L0_attn_post_proj", "L0_attn_mem_k",
          "L0_attn_mem_v", "L0_attn_Wout", "L0_attn_bout", "L0_ffn_W_r", "L0_ffn_W_k", "L0_ffn_W_v", "L0_ffn_mu_r",
          "L0_ffn_mu_k", "L1_attn_Wq", "L1_attn_Wk", "L1_attn_Wv", "L1_ffn_router_W", "L1_ffn_router_b", "L1_ffn_W1",
          "L1_ffn_b1", "L1_ffn_W2", "L1_ffn_b2")


def kernel(**inputs):
    import numpy as np
    import concourse.bacc as bacc
    from concourse.bass_utils import run_bass_kernel_spmd

    arrays = {n: np.ascontiguousarray(inputs[n]) for n in INPUTS}
    pos = np.arange(TOK, dtype=np.float32)
    inv = np.power(np.float32(10000.0), -2.0 * np.arange(D1 // 2, dtype=np.float32) / D1).astype(np.float32)
    angle = np.tile(np.repeat(inv[:, None] * pos[None, :], 2, axis=0), (H, 1))
    arrays["cosT"] = np.cos(angle).astype(np.float32)
    arrays["sinT"] = np.sin(angle).astype(np.float32)
    nc = bacc.Bacc("TRN2", target_bir_lowering=False, num_devices=1)
    a = {n: nc.dram_tensor(f"{n}_dram", v.shape, F32, kind="ExternalInput").ap() for n, v in arrays.items()}
    shape = arrays["L0_attn_x"].shape
    a["out"] = nc.dram_tensor("out_dram", shape, F32, kind="ExternalOutput").ap()
    build(nc, a, shape[0])
    r = run_bass_kernel_spmd(nc, [{f"{n}_dram": v for n, v in arrays.items()}], core_ids=[0])
    return r.results[0]["out_dram"]
```

```python
from contextlib import ExitStack

import concourse.bass as bass
from concourse import mybir

F32 = mybir.dt.float32
ALU = mybir.AluOpType
ACT = mybir.ActivationFunctionType
AX = mybir.AxisListType

P = 128
T = 2
TOK = T * P
H = 16
MEM = 64
DH = 64
TOPK = 64
CH = H * DH // P
D1 = P // H
EXP = 8
FF = 512
STEPS = 8
RING = STEPS + 2
W0 = MEM + P
W1 = MEM + TOK
COLS = ((0, W0), (W0, W0 + W1))
KEYS = (((P, W1), (0, W1)), ((W1, W1 + W0), (W1, 2 * W1)))
PROBS = ((0, 2 * W0), (W0, 2 * W0 + W1))
MEM_AT = (P, 2 * W0 + TOK)
TOKENS_AT = ((0, 2 * W0 + P, 2 * W0), (2 * P, 2 * W0 + W1 + MEM, 2 * W0 + W1 + MEM + P))
TAKEN = -2.0 ** 118
WINDOW = 16
BIG = 3.4028234663852886e38
EPS = 1e-5

USES = ("s1_0", "s1_1", "h_0", "h_1", "ptm", "pt_0", "pt_1", "s_0", "s_1", "pg", "pu", "miss", "p1_0", "p1_1", "y")
NBANK = 6
EXTRA = {"xt": 3, "x1t": 0, "x3t": 3, "lg": 0, "kr": 1, "v": 0, "gt": 2, "base": 5, "x2t": 0, "q": 0, "k": 1, "vv": 4}


def bank_of(use, par=0):
    return EXTRA[use] if use in EXTRA else (USES.index(use) + len(USES) * par) % NBANK


def threshold_tables():
    import math
    import numpy as np

    table = np.zeros((P, 5, 2 * T), np.float32)
    for t, (c0, c1) in enumerate(COLS):
        width = c1 - c0
        shift = width - 2 * (TOPK - 0.5 - WINDOW / 2)
        for p in range(P):
            seen = MEM + 1 + t * P + p
            share = (TOPK - 0.5 - WINDOW / 2) / seen
            low, z = -9.0, 9.0
            for _ in range(60):
                middle = (low + z) / 2
                low, z = (middle, z) if 0.5 * math.erfc(middle / 2 ** 0.5) > share else (low, middle)
            density = math.exp(-z * z / 2) / (2 * math.pi) ** 0.5
            sigma = (np.pi / 2) ** 0.5 / width
            g1, g2 = (damp * sigma / (2 * seen * density) for damp in (0.95, 0.55))
            for h in range(2):
                table[p, :, 2 * h + t] = -z * sigma, -z * sigma - g1 * shift, -g1, g2, -g2 * shift
    return table


class Count:

    def __init__(self):
        self.n = 0

    def up(self):
        self.n += 1
        return 1

    def reset(self):
        n, self.n = self.n, 0
        return n


def flags(it, nb):
    lag = {"L": -2, "P": -1, "A": 0, "F": 1, "B": 2, "C": 3, "D": 4}
    return {s for s, n in lag.items() if 0 <= it - n < nb}


def build(nc, a, nb):
    with ExitStack() as ctx:
        def sb(name, *shape):
            return ctx.enter_context(nc.sbuf_tensor(name, [shape[0], *shape[1:]], F32))

        def sem(name):
            return ctx.enter_context(nc.semaphore(name))

        ident = sb("ident", P, P)
        ones = sb("ones", P, P)
        A_all = sb("A_all", P, H, P)
        B_all = sb("B_all", P, H, P)
        UM = sb("UM", P, STEPS, P)
        keys = sb("keys", P, STEPS, 2, P + TOK)
        vals = sb("vals", P, RING, T, 2, P)
        WkT, WrT, WvT = (sb(n, P, P) for n in ("WkT", "WrT", "WvT"))
        qW, qWr, kW, kWr, vW = (sb(n, P, P) for n in ("qW", "qWr", "kW", "kWr", "vW"))
        cosT, sinT = sb("cosT", P, TOK), sb("sinT", P, TOK)
        hmask = sb("hmask", P, H)
        mu_r, mu_k = sb("mu_r", P, 1), sb("mu_k", P, 1)
        brow = sb("brow", 1, P)
        rW = sb("rW", P, EXP)
        rb = sb("rb", 1, EXP)
        b1c = sb("b1c", P, EXP, FF // P)
        W2 = sb("W2", P, EXP, FF // P, P)
        b2 = sb("b2", EXP, P)
        first = sb("first", P, EXP)
        guess = sb("guess", P, 5, 4)
        place = sb("place", P, WINDOW)
        taken = sb("taken", P, 1)
        minus_half = sb("minus_half", P, 2 * T)
        A_st = [sb(f"A_st{i}", P, 2, P) for i in range(2)]
        W1_st = [sb(f"W1_st{i}", P, FF) for i in range(2)]
        xload = sb("xload", P, T, P)
        xres = sb("xres", P, T, P)
        xT_next = sb("xT_next", P, TOK)
        xT = sb("xT", P, TOK)
        S = [sb(f"S{i}", P, 2, W0 + W1) for i in range(2)]
        work = sb("work", P, 2, W0 + W1)
        E = sb("E", P, 2, W0 + W1)
        Pr = [sb(f"Pr{i}", P, 2 * (W0 + W1)) for i in range(2)]
        signs = sb("signs", P, 2, W0 + W1)
        sizes = sb("sizes", P, 2, T)
        fit = sb("fit", P, 5, 4)
        signsum = [sb(f"signsum{i}", P, 4) for i in range(2)]
        moved = sb("moved", P, 4)
        neg_t = sb("neg_t", P, 4)
        neg_t_next = sb("neg_t_next", P, 4)
        threshold = sb("threshold", P, 4)
        above = sb("above", P, 4)
        rank = sb("rank", P, 4)
        deep = sb("deep", P, 4)
        missed = sb("missed", P, 4)
        missed_n = ctx.enter_context(nc.sbuf_tensor("missed_n", [1, 1], mybir.dt.int32))
        window = sb("window", P, 4, WINDOW)
        chosen = sb("chosen", P, 4, WINDOW)
        kth = sb("kth", P, 4)
        top = sb("top", P, 4, 8)
        negmax = [sb(f"neg_top{i}", P, 2, T) for i in range(2)]
        psumA = sb("psumA", P, 4)
        rsumA = [sb(f"rsumA{i}", P, 4) for i in range(2)]
        PTm = sb("PTm", P, T, P)
        PT = [sb(f"PT{i}", P, 3, P) for i in range(2)]
        x1 = sb("x1", P, T, P)
        x1T = sb("x1T", P, 1 + TOK)
        dT, xrT, xkT = sb("dT", P, TOK), sb("xrT", P, TOK), sb("xkT", P, TOK)
        th = sb("th", P, T, P)
        rk = sb("rk", P, TOK)
        kact = sb("kact", P, TOK)
        x2 = sb("x2", P, T, P)
        x2res = sb("x2res", P, T, P)
        x2pre = sb("x2pre", P, T, P)
        x2T = sb("x2T", P, TOK)
        rope = sb("rope", P, 4, TOK)
        qT, kT = sb("qT", P, TOK), sb("kT", P, TOK)
        keys1 = sb("keys1", P, H, TOK)
        vals1 = sb("vals1", P, T, H, D1 + 1)
        negmax1 = sb("negmax1", P, T, 2)
        max1 = sb("max1", P, T, 2)
        E1 = sb("E1", P, T, 2, TOK)
        E1T = [sb(f"E1T{i}", P, T, T, P) for i in range(2)]
        rsum1 = sb("rsum1", P, T, H)
        o1 = sb("o1", P, T, P)
        x3pre = sb("x3pre", P, T, P)
        x3 = sb("x3", P, T, P)
        x3T = sb("x3T", P, TOK)
        lg_raw = sb("lg_raw", P, T, EXP)
        lg = sb("lg", P, 6, T, EXP)
        lgs = sb("lgs", P, 4, T)
        gates = sb("gates", P, T, EXP)
        gT = sb("gT", EXP, TOK)
        hT = [sb(f"hT{i}", P, 2, TOK) for i in range(2)]
        yacc = sb("yacc", P, T, P)
        yout = sb("yout", P, T, P)
        stats = sb("stats", P, 4, T, 6)
        mv = sb("mv", P, 4, T, 2)
        rstd = sb("rstd", P, 4, T)
        var = sb("var", P, 4, T)

        bank = [ctx.enter_context(nc.psum_tensor(f"bank{i}", [P, 512], F32)) for i in range(NBANK)]
        acc_bank = ctx.enter_context(nc.psum_tensor("acc_bank", [P, 512], F32))
        pv_bank = ctx.enter_context(nc.psum_tensor("pv_bank", [P, 512], F32))
        acc = acc_bank[:, 0:TOK].rearrange("p (t c) -> p t c", t=T)
        pv = pv_bank[:, 0:T * H * (D1 + 1)].rearrange("p (t h e) -> p t h e", t=T, h=H)

        nat = keys1[:, :, :].rearrange("p h j -> p (h j)")
        WqN, WkN, WvN, WoN = (nat[:, i * CH * P:(i + 1) * CH * P].rearrange("p (c k) -> p c k", c=CH) for i in range(4))
        slab = [vals[:, :, :, :, :].rearrange("p r t h c -> p (r t h c)")[:, i * H * P:(i + 1) * H * P] for i in range(2)]
        mkN = work[0:MEM, :, :].rearrange("p h j -> p (h j)")
        mvN = E[0:MEM, :, :].rearrange("p h j -> p (h j)")
        WoT = S[0][:, :, :].rearrange("p h j -> p (h j)")
        mkT = S[1][:, 0, :]
        mvT = Pr[0][:, :].rearrange("p (c r m) -> p c r m", c=CH, r=2)
        preB, postB = rope[:, 0, :], rope[:, 1, :]
        preX = rope[:, 2, 0:CH * H].rearrange("p (c k) -> p c k", c=CH)
        postX = rope[:, 3, 0:CH * H].rearrange("p (c k) -> p c k", c=CH)
        smallN = E1[:, :, :, :].rearrange("p t h j -> p (t h j)")

        w_big = sem("w_big")
        w_small = sem("w_small")
        consts_ready = sem("consts_ready")
        turned = sem("turned")
        turned_out = sem("turned_out")
        slab_ready = sem("slab_ready")
        slab_free = sem("slab_free")
        fold_full = sem("fold_full")
        fold_out = sem("fold_out")
        setup_done = sem("setup_done")
        bank_free = [sem(f"bank{i}_free") for i in range(NBANK)]
        A_full, A_free = [sem(f"A_full{i}") for i in range(2)], [sem(f"A_free{i}") for i in range(2)]
        W1_full, W1_free = [sem(f"W1_full{i}") for i in range(2)], [sem(f"W1_free{i}") for i in range(2)]
        xload_full = sem("xload_full")
        xload_free = sem("xload_free")
        xres_full = sem("xres_full")
        xres_free = sem("xres_free")
        xt_full = sem("xt_full")
        xt_ready = sem("xt_ready")
        xT_ready = sem("xT_ready")
        pg_full = sem("pg_full")
        pu_full = sem("pu_full")
        s_full = sem("s_full")
        s_out = sem("s_out")
        s_copied = sem("s_copied")
        sizes_ready = sem("sizes_ready")
        s_masked = sem("s_masked")
        neg_t_ready = sem("neg_t_ready")
        signs_ready = sem("signs_ready")
        threshold_ready = sem("threshold_ready")
        above_ready = sem("above_ready")
        below_ready = sem("below_ready")
        missed_ready = sem("missed_ready")
        missed_full = sem("missed_full")
        E_free = sem("E_free")
        S_free = sem("S_free")
        negmax_ready = sem("negmax_ready")
        E_ready = sem("E_ready")
        P_free = sem("P_free")
        kept_ready = sem("kept_ready")
        probs_ready = sem("probs_ready")
        pt_full = sem("pt_full")
        pt_ready = sem("pt_ready")
        acc_full = sem("acc_full")
        var_ready = sem("var_ready")
        rstd_ready = sem("rstd_ready")
        x1_ready = sem("x1_ready")
        x1t_full = sem("x1t_full")
        x1T_ready = sem("x1T_ready")
        mixed_ready = sem("mixed_ready")
        kr_full = sem("kr_full")
        kact_ready = sem("kact_ready")
        v_full = sem("v_full")
        x2_ready = sem("x2_ready")
        x2t_full = sem("x2t_full")
        x2T_ready = sem("x2T_ready")
        x2_saved = sem("x2_saved")
        q_full = sem("q_full")
        k_full = sem("k_full")
        vv_full = sem("vv_full")
        kT_ready = sem("kT_ready")
        keys1_ready = sem("keys1_ready")
        s1_full = sem("s1_full")
        negmax1_ready = sem("negmax1_ready")
        E1_ready = sem("E1_ready")
        p1_full = sem("p1_full")
        p1_ready = sem("p1_ready")
        pv_full = sem("pv_full")
        pv_free = sem("pv_free")
        x3_ready = sem("x3_ready")
        x3t_full = sem("x3t_full")
        x3T_ready = sem("x3T_ready")
        lg_full = sem("lg_full")
        lg_ready = sem("lg_ready")
        lg_shifted = sem("lg_shifted")
        lg_exp = sem("lg_exp")
        gates_ready = sem("gates_ready")
        gt_full = sem("gt_full")
        gT_ready = sem("gT_ready")
        base_full = sem("base_full")
        h_full = sem("h_full")
        h_ready = sem("h_ready")
        y_full = sem("y_full")
        yout_full = sem("yout_full")
        yout_free = sem("yout_free")
        dve_did = sem("dve_did")
        pool_did = sem("pool_did")
        act_did = sem("act_did")

        def iterations(eng, iteration):
            for it in range(-1, 4):
                iteration(it, flags(it, nb))
            with eng.Fori(4, nb - 2) as it:
                iteration(it, set("LPAFBCD"))
            for it in range(nb - 2, nb + 4):
                iteration(it, flags(it, nb))

        def steps(eng, step, on):
            for n in range(3):
                step(n, n % 2, n)
            if on & {"A", "P", "B", "C"}:
                with eng.Fori(0, 2) as q:
                    step(2 * q + 3, 1, None)
                    step(2 * q + 4, 0, None)
            step(STEPS - 1, 1, STEPS - 1)

        def expert_of(n, at, on):
            if at in (0, 1):
                return n + EXP - 2 if "D" in on else None
            return n - 2 if "C" in on else None

        def psum(use, par=0):
            return bank[bank_of(use, par)]

        block = ctx.enter_context(nc.Block())

        @block.sync
        def _(sp):
            for dst, w in ((WqN, "L0_attn_Wq"), (WkN, "L0_attn_Wk"), (WvN, "L0_attn_Wv")):
                sp.dma_start(dst, a[w].rearrange("(c p) k -> p c k", p=P)).then_inc(w_big, 16)
            sp.dma_start(WoN, a["L0_attn_Wout"].rearrange("p (c k) -> p c k", c=CH)).then_inc(w_big, 16)
            for dst, w in ((mkN, "L0_attn_mem_k"), (mvN, "L0_attn_mem_v")):
                sp.dma_start(dst.rearrange("j (h d) -> j h d", h=H), a[w].rearrange("h j d -> j h d")).then_inc(w_big, 16)
            for dst, w in ((preB, "L0_attn_pre_proj"), (postB, "L0_attn_post_proj")):
                sp.dma_start(dst, a[w].rearrange("h k -> (h k)").partition_broadcast(P)).then_inc(w_big, 16)
            for n, w in enumerate(("L0_ffn_W_r", "L0_ffn_W_k", "L0_ffn_W_v", "L1_attn_Wq", "L1_attn_Wk", "L1_attn_Wv")):
                sp.dma_start(smallN[:, n * P:(n + 1) * P], a[w]).then_inc(w_big, 16)
            x_in = a["L0_attn_x"].rearrange("b (t p) c -> b p t c", p=P)
            out = a["out"].rearrange("b (t p) c -> b p t c", p=P)
            sp.dma_start(xload[:, :, :], x_in[0]).then_inc(xload_full, 16)
            sp.dma_start(xres[:, :, :], x_in[0]).then_inc(xres_full, 16)
            for dst, w in ((mu_r, "L0_ffn_mu_r"), (mu_k, "L0_ffn_mu_k")):
                sp.dma_start(dst[:, :], a[w].rearrange("(p o) -> p o", o=1)).then_inc(w_small, 16)
            for dst, w in ((brow, "L0_attn_bout"), (rb, "L1_ffn_router_b")):
                sp.dma_start(dst[:, :], a[w].rearrange("(o c) -> o c", o=1)).then_inc(w_small, 16)
            sp.dma_start(rW[:, :], a["L1_ffn_router_W"]).then_inc(w_small, 16)
            with nc.allow_non_contiguous_dma(reason="4096 biases, once"):
                for e in range(EXP):
                    sp.dma_start(b1c[:, e, :], a["L1_ffn_b1"][e].rearrange("(f p) -> p f", p=P)).then_inc(w_small, 16)
            for e in range(EXP):
                sp.dma_start(W2[:, e, :, :], a["L1_ffn_W2"][e].rearrange("(f p) d -> p f d", p=P)).then_inc(w_small, 16)
            for dst, w in ((b2, "L1_ffn_b2"), (cosT, "cosT"), (sinT, "sinT")):
                sp.dma_start(dst[:, :], a[w]).then_inc(w_small, 16)
            sp.dma_start(guess[:, :, :], a["guess"]).then_inc(w_small, 16)
            sp.wait_ge(setup_done, 1)
            for f in (*A_free, *W1_free):
                sp.sem_inc(f, 1)

            def stage_weights(n, par, at, on):
                if "P" in on:
                    sp.wait_ge(A_free[par], 1)
                    sp.sem_inc(A_free[par], -1)
                    sp.dma_start(A_st[par][:, :, :], A_all[:, bass.ds(2 * n, 2), :]).then_inc(A_full[par], 16)
                e = expert_of(n, at, on)
                if e is not None:
                    sp.wait_ge(W1_free[par], 1)
                    sp.sem_inc(W1_free[par], -1)
                    sp.dma_start(W1_st[par][:, :], a["L1_ffn_W1"][e]).then_inc(W1_full[par], 16)

            def iteration(it, on):
                steps(sp, lambda n, par, at: stage_weights(n, par, at, on), on)
                if {"A", "P"} <= on:
                    sp.wait_ge(xres_free, 1)
                    sp.sem_inc(xres_free, -1)
                    sp.dma_start(xres[:, :, :], x_in[it + 1]).then_inc(xres_full, 16)
                if "L" in on:
                    sp.wait_ge(xload_free, 1)
                    sp.sem_inc(xload_free, -1)
                    sp.dma_start(xload[:, :, :], x_in[it + 2]).then_inc(xload_full, 16)
                if "D" in on:
                    sp.wait_ge(yout_full, 1)
                    sp.sem_inc(yout_full, -1)
                    sp.dma_start(out[it - 4], yout[:, :, :]).then_inc(yout_free, 16)

            iterations(sp, iteration)
            sp.wait_ge(yout_free, 16)

        @block.gpsimd
        def _(pool):
            seq = Count()
            for dst, value in ((ones[:, :], 1.0), (ident[:, :], 0.0), (hmask[:, :], 1.0), (minus_half[:, :], -0.5),
                               (x1T[:, 0:1], 0.0), (vals1[:, :, :, :], 1.0), (taken[:, :], TAKEN)):
                pool.memset(dst, value).then_inc(pool_did, seq.up())
            for e in range(EXP):
                pool.memset(first[:, e:e + 1], float(EXP - e)).then_inc(pool_did, seq.up())
            for i in range(WINDOW):
                pool.memset(place[:, i:i + 1], float(i)).then_inc(pool_did, seq.up())
            pool.wait_ge(pool_did, seq.n)
            pool.affine_select(out=ident[:, :], in_=ident[:, :], compare_op=ALU.not_equal, fill=1.0, base=0,
                               pattern=[[-1, P]], channel_multiplier=1).then_inc(pool_did, seq.up())
            pool.affine_select(out=hmask[:, :], in_=hmask[:, :], compare_op=ALU.is_ge, fill=0.0, base=0,
                               pattern=[[-D1, H]], channel_multiplier=1).then_inc(pool_did, seq.up())
            pool.wait_ge(pool_did, seq.n)
            pool.affine_select(out=hmask[:, :], in_=hmask[:, :], compare_op=ALU.is_ge, fill=0.0, base=D1 - 1,
                               pattern=[[D1, H]], channel_multiplier=-1).then_inc(pool_did, seq.up())
            pool.wait_ge(pool_did, seq.n)
            pool.sem_inc(pool_did, -seq.reset())
            pool.sem_inc(consts_ready, 2)
            pool.wait_ge(setup_done, 1)

            def below(par):
                for h in range(2):
                    pool.wait_ge(above_ready, 1)
                    pool.sem_inc(above_ready, -1)
                    pool.tensor_tensor(work[:, h, :], work[:, h, :], S[par][:, h, :], ALU.add).then_inc(below_ready, 1)

            def mask(par, nxt):
                for h in range(2):
                    pool.wait_ge(s_out, 1)
                    pool.sem_inc(s_out, -1)
                    pool.sem_inc(bank_free[bank_of(f"s_{h}", par)], 1)
                pool.sem_inc(s_copied, 1)
                pool.wait_ge(sizes_ready, 1)
                pool.sem_inc(sizes_ready, -1)
                for h in range(2):
                    for c0, c1 in COLS:
                        diag = S[nxt][:, h, c0:c0 + P] if h == 0 else S[nxt][:, h, c1 - P:c1]
                        last = pool.affine_select(out=diag, in_=diag, compare_op=ALU.is_ge, fill=-BIG, base=0,
                                                  pattern=[[-1, P]], channel_multiplier=1)
                last.then_inc(s_masked, 1)

            def first_guess():
                pool.tensor_tensor(fit[:, :, :], guess[:, :, :],
                                   sizes[:, :, :].rearrange("p h t -> p (h t)").unsqueeze(1).broadcast_to([P, 5, 4]),
                                   ALU.mult).then_inc(pool_did, seq.up())
                pool.wait_ge(pool_did, seq.n)
                pool.sem_inc(pool_did, -seq.reset())
                pool.sem_inc(neg_t_ready, 1)

            def first_correction():
                pool.wait_ge(signs_ready, 1)
                pool.sem_inc(signs_ready, -1)
                pool.tensor_tensor(moved[:, :], fit[:, 2, :], signsum[0][:, :], ALU.mult).then_inc(pool_did, seq.up())
                pool.wait_ge(pool_did, seq.n)
                pool.tensor_tensor(neg_t[:, :], moved[:, :], fit[:, 1, :], ALU.add).then_inc(pool_did, seq.up())
                pool.wait_ge(pool_did, seq.n)
                pool.sem_inc(neg_t_ready, 1)
                pool.tensor_tensor(neg_t_next[:, :], neg_t[:, :], fit[:, 4, :], ALU.add).then_inc(pool_did, seq.up())
                pool.wait_ge(pool_did, seq.n)
                pool.sem_inc(pool_did, -seq.reset())

            def second_correction():
                pool.wait_ge(signs_ready, 1)
                pool.sem_inc(signs_ready, -1)
                pool.tensor_tensor(moved[:, :], fit[:, 3, :], signsum[1][:, :], ALU.mult).then_inc(pool_did, seq.up())
                pool.wait_ge(pool_did, seq.n)
                pool.tensor_tensor(threshold[:, :], moved[:, :], neg_t_next[:, :], ALU.subtract).then_inc(threshold_ready, 1)
                pool.sem_inc(pool_did, -seq.reset())

            def normalise(par):
                pool.wait_ge(kept_ready, 1)
                pool.sem_inc(kept_ready, -1)
                pool.sem_inc(S_free, 1)
                pool.sem_inc(E_free, 1)
                for h in range(2):
                    for t, (c0, c1) in enumerate(COLS):
                        u = 2 * h + t
                        probs = Pr[par][:, PROBS[h][t]:PROBS[h][t] + c1 - c0]
                        last = pool.tensor_scalar(probs, probs, rsumA[par][:, u:u + 1], 1.0,
                                                  ALU.mult, ALU.mult)
                last.then_inc(probs_ready, 1)

            def rstd_of(a0, present):
                cols = [a0 + i for i, p in enumerate(present) if p]
                if cols:
                    lo, hi = cols[0], cols[-1] + 1
                    pool.wait_ge(var_ready, 1)
                    pool.sem_inc(var_ready, -1)
                    pool.tensor_scalar(var[:, lo:hi, :], mv[:, lo:hi, :, 1], EPS, 1.0, ALU.add, ALU.mult).then_inc(pool_did, seq.up())
                    pool.wait_ge(pool_did, seq.n)
                    pool.tensor_tensor(rstd[:, lo:hi, :], var[:, lo:hi, :],
                                       minus_half[:, 0:(hi - lo) * T].rearrange("p (a t) -> p a t", t=T), ALU.pow).then_inc(rstd_ready, 1)
                    pool.sem_inc(pool_did, -seq.reset())

            def spread_keys(h0, h1):
                pool.tensor_tensor(keys1[:, h0:h1, :], kT[:, :].unsqueeze(1).broadcast_to([P, h1 - h0, TOK]),
                                   hmask[:, h0:h1].unsqueeze(2).broadcast_to([P, h1 - h0, TOK]), ALU.mult).then_inc(keys1_ready, 1)

            def step(n, par, at, on):
                front = ("P" if at == STEPS - 1 else "A") in on
                if "A" in on:
                    below(par)
                if at == 1 and "B" in on:
                    pool.tensor_copy(x2res[:, :, :], x2[:, :, :]).then_inc(x2_saved, 1)
                if front:
                    mask(par, 1 - par)
                    first_guess()
                if at == 0:
                    rstd_of(0, ("F" in on, "C" in on))
                if at == 2:
                    rstd_of(2, ("F" in on, "D" in on))
                if front:
                    first_correction()
                if at == 0 and "B" in on:
                    spread_keys(4, 8)
                if at == 1 and "B" in on:
                    spread_keys(8, 12)
                    spread_keys(12, 16)
                if front:
                    second_correction()
                if at == STEPS - 1 and "F" in on:
                    pool.wait_ge(kT_ready, 1)
                    pool.sem_inc(kT_ready, -1)
                    spread_keys(0, 4)
                if "A" in on:
                    normalise(par)

            def iteration(it, on):
                steps(pool, lambda n, par, at: step(n, par, at, on), on)

            iterations(pool, iteration)

        @block.scalar
        def _(act):
            act.preload_act_table_set("exp_and_others")
            seq = Count()

            def copy(dst, src, **kw):
                return act.activation(dst, src, ACT.Copy, **kw)

            act.wait_ge(turned, 1)
            copy(WoT[:, 0:512], bank[0][:, :])
            copy(WoT[:, 512:1024], bank[1][:, :])
            copy(mkT, bank[2][:, :])
            for r in range(2):
                copy(mvT[:, :, r, :], bank[3][:, :].rearrange("p (c m) -> p c m", c=CH))
            for i, w in enumerate((WrT, WkT, WvT, qW)):
                copy(w[:, :], bank[4][:, i * P:(i + 1) * P])
            for i, w in enumerate((kW, vW)):
                last = copy(w[:, :], bank[5][:, i * P:(i + 1) * P])
            last.then_inc(turned_out, 2)
            act.wait_ge(fold_full, 1)
            scale = float(DH) ** -0.5
            A_flat = A_all[:, :, :].rearrange("p k c -> p (k c)")
            for b in range(4):
                copy(A_flat[:, b * 512:(b + 1) * 512], bank[b][:, :], scale=scale)
            for s in range(STEPS):
                last = copy(keys[:, s, 0, TOK:TOK + P], bank[4 + s // 4][:, (s % 4) * P:(s % 4 + 1) * P], scale=scale)
            last.then_inc(fold_out, 1)
            act.wait_ge(fold_full, 2)
            B_flat = B_all[:, :, :].rearrange("p k c -> p (k c)")
            for b, mem in enumerate((bank[4], bank[5], acc_bank, pv_bank)):
                copy(B_flat[:, b * 512:(b + 1) * 512], bank[b][:, :])
                for r in range(2):
                    rows = slice(r * MEM, (r + 1) * MEM)
                    last = copy(UM[rows, 2 * b:2 * b + 2, :], mem[rows, :].rearrange("p (s r c) -> p s r c", s=2, r=2)[:, :, r, :])
            last.then_inc(act_did, seq.up())
            act.wait_ge(act_did, seq.n)
            act.sem_inc(act_did, -seq.reset())
            act.wait_ge(consts_ready, 3)
            act.wait_ge(w_small, 25 * 16)
            act.sem_inc(setup_done, 1)
            act.sem_inc(S_free, 2)
            act.sem_inc(E_free, 1)

            def exp1(n, par):
                act.wait_ge(negmax1_ready, 1)
                act.sem_inc(negmax1_ready, -1)
                for t in range(T):
                    for h in range(2):
                        last = act.activation(E1[:, t, h, :], psum(f"s1_{t}", par)[:, h * TOK:(h + 1) * TOK], ACT.Exp,
                                              bias=negmax1[:, t, h:h + 1], scale=float(D1) ** -0.5)
                last.then_inc(act_did, seq.up())
                act.wait_ge(act_did, seq.n)
                act.sem_inc(act_did, -seq.reset())
                act.sem_inc(E1_ready, 1)
                act.sem_inc(bank_free[bank_of("s1_0", par)], 1)
                act.sem_inc(bank_free[bank_of("s1_1", par)], 1)

            def scores_out(par):
                act.wait_ge(S_free, 1)
                act.sem_inc(S_free, -1)
                for h in range(2):
                    act.wait_ge(s_full, 1)
                    act.sem_inc(s_full, -1)
                    copy(S[1 - par][:, h, :], psum(f"s_{h}", par)[:, :]).then_inc(s_out, 1)

            def projections_out(it, n, par):
                act.wait_ge(pg_full, 1)
                act.sem_inc(pg_full, -1)
                copy(keys[:, n, :, 0:TOK], psum("pg", par)[:, :].rearrange("p (h j) -> p h j", h=2))\
                    .then_inc(bank_free[bank_of("pg", par)], 1)
                act.wait_ge(pu_full, 1)
                act.sem_inc(pu_full, -1)
                act.sem_inc(A_free[par], 1)
                copy(vals[:, (STEPS * (it + 1) + n) % RING, :, :, :].rearrange("p t h c -> p (t h c)"), psum("pu", par)[:, :])\
                    .then_inc(bank_free[bank_of("pu", par)], 1)

            def probs_out(par):
                act.wait_ge(pt_full, 1)
                act.sem_inc(pt_full, -1)
                copy(PTm[:, :, :].rearrange("p t i -> p (t i)"), psum("ptm", par)[:, 0:TOK])
                for h in range(2):
                    act.wait_ge(pt_full, 1)
                    act.sem_inc(pt_full, -1)
                    if h == 1:
                        act.sem_inc(P_free, 1)
                    copy(PT[h][:, :, :].rearrange("p u i -> p (u i)"), psum(f"pt_{h}", par)[:, 0:3 * P]).then_inc(pt_ready, 1)

            def hidden_out(e, par):
                for b in range(2):
                    act.wait_ge(h_full, 1)
                    act.sem_inc(h_full, -1)
                    if b == 1:
                        act.sem_inc(W1_free[par], 1)
                    for f in range(2):
                        last = act.activation(hT[b][:, f, :], psum(f"h_{b}", par)[:, f * TOK:(f + 1) * TOK], ACT.Relu,
                                              bias=b1c[:, e, 2 * b + f:2 * b + f + 1])
                    last.then_inc(h_ready, 1)

            def probs1_out(par):
                for h in range(2):
                    act.wait_ge(p1_full, 1)
                    act.sem_inc(p1_full, -1)
                    copy(E1T[h][:, :, :, :].rearrange("p a b i -> p (a b i)"), psum(f"p1_{h}", par)[:, :]).then_inc(p1_ready, 1)

            def exp_scores(par):
                act.wait_ge(negmax_ready, 1)
                act.sem_inc(negmax_ready, -1)
                act.wait_ge(E_free, 1)
                act.sem_inc(E_free, -1)
                for h in range(2):
                    for t, (c0, c1) in enumerate(COLS):
                        last = act.activation(E[:, h, c0:c1], S[par][:, h, c0:c1], ACT.Exp, bias=negmax[par][:, h, t:t + 1])
                last.then_inc(E_ready, 1)

            def count(nxt, neg_t, out):
                act.wait_ge(neg_t_ready, 1)
                act.sem_inc(neg_t_ready, -1)
                for h in range(2):
                    for t, (c0, c1) in enumerate(COLS):
                        u = 2 * h + t
                        last = act.activation(signs[:, h, c0:c1], S[nxt][:, h, c0:c1], ACT.Sign, bias=neg_t[:, u:u + 1],
                                              accum_out=out[:, u:u + 1])
                last.then_inc(signs_ready, 1)

            def bank_out(use, cols, dst, full, ready):
                act.wait_ge(full, 1)
                act.sem_inc(full, -1)
                src = psum(use)[0:dst.shape[0], 0:cols]
                if len(dst.shape) == 3:
                    src = src.rearrange("p (t e) -> p t e", t=T)
                copy(dst, src).then_inc(act_did, seq.up())
                act.wait_ge(act_did, seq.n)
                act.sem_inc(act_did, -seq.reset())
                act.sem_inc(ready, 1)
                act.sem_inc(bank_free[bank_of(use)], 1)

            def step(it, n, par, at, on):
                front = ("P" if at == STEPS - 1 else "A") in on
                e = expert_of(n, at, on)
                if at == STEPS - 1 and "P" in on:
                    copy(xT[:, :], xT_next[:, :]).then_inc(xT_ready, 1)
                if at == 0 and "P" in on:
                    bank_out("xt", TOK, xT_next[:, :], xt_full, xt_ready)
                    if "L" in on:
                        act.sem_inc(xload_free, 1)
                if at == 1 and "F" in on:
                    bank_out("x1t", TOK, x1T[:, 1:1 + TOK], x1t_full, x1T_ready)
                if "B" in on:
                    exp1(n, par)
                if at == 0 and "B" in on:
                    act.wait_ge(vv_full, 1)
                    act.sem_inc(vv_full, -1)
                    copy(vals1[:, :, :, 0:D1], psum("vv")[:, 0:TOK].rearrange("p (t h d) -> p t h d", t=T, h=H))\
                        .then_inc(bank_free[bank_of("vv")], 1)
                if e is not None:
                    hidden_out(e, par)
                if at == 2 and "C" in on:
                    act.wait_ge(lg_shifted, 1)
                    act.sem_inc(lg_shifted, -1)
                    act.activation(lg[:, 1, :, :], lg[:, 0, :, :], ACT.Exp).then_inc(lg_exp, 1)
                if ("F" if at == 0 else "A") in on:
                    probs_out(par)
                if front:
                    scores_out(par)
                if at == 1 and "C" in on:
                    bank_out("x3t", TOK, x3T[:, :], x3t_full, x3T_ready)
                if "A" in on:
                    exp_scores(par)
                if "P" in on:
                    projections_out(it, n, par)
                if at == 1 and {"A", "P"} <= on:
                    act.sem_inc(xres_free, 1)
                if at == 2 and "C" in on:
                    bank_out("gt", TOK, gT[:, :], gt_full, gT_ready)
                if front:
                    count(1 - par, fit[:, 0, :], signsum[0])
                if "B" in on:
                    probs1_out(par)
                if at == 1 and "F" in on:
                    act.wait_ge(kr_full, 1)
                    act.sem_inc(kr_full, -1)
                    act.activation(rk[:, :], psum("kr")[:, 0:TOK], ACT.Relu).then_inc(act_did, seq.up())
                    act.activation(th[:, :, :].rearrange("p t c -> p (t c)"), psum("kr")[:, TOK:2 * TOK], ACT.Tanh,
                                   scale=0.5).then_inc(act_did, seq.up())
                    act.wait_ge(act_did, seq.n)
                    act.activation(kact[:, :], rk[:, :], ACT.Square).then_inc(kact_ready, 1)
                    act.sem_inc(act_did, -seq.reset())
                    act.sem_inc(bank_free[bank_of("kr")], 1)
                if at == 1 and "C" in on:
                    bank_out("lg", T * EXP, lg_raw[:, :, :], lg_full, lg_ready)
                if front:
                    count(1 - par, neg_t, signsum[1])
                if at == 2 and "F" in on:
                    bank_out("x2t", TOK, x2T[:, :], x2t_full, x2T_ready)

            def iteration(it, on):
                steps(act, lambda n, par, at: step(it, n, par, at, on), on)

            iterations(act, iteration)

        @block.vector
        def _(dve):
            seq = Count()
            dve.wait_ge(w_big, 14 * 16)
            pre_hk = preB.rearrange("p (h k) -> p h k", h=H)
            post_hk = postB.rearrange("p (k h) -> p h k", h=H)
            for half in range(2):
                rows = slice(half * DH, (half + 1) * DH)
                dve.tensor_copy(preX[rows, :, :], pre_hk[rows, half:H:2, :]).then_inc(dve_did, seq.up())
                dve.tensor_copy(postX[rows, :, :], post_hk[rows, half:H:2, :]).then_inc(dve_did, seq.up())
            dve.wait_ge(dve_did, seq.n)

            def make_slab(n, w, mix):
                if n >= 2:
                    dve.wait_ge(slab_free, n - 1)
                dve.tensor_tensor(slab[n % 2].rearrange("p (k c) -> p k c", k=H), w.unsqueeze(1).broadcast_to([P, H, P]),
                                  mix.unsqueeze(2).broadcast_to([P, H, P]), ALU.mult).then_inc(slab_ready, 1)

            for c in range(CH):
                make_slab(c, WqN[:, c, :], preX[:, c, :])
            dve.wait_ge(turned_out, 2)
            for w, wr in ((qW, qWr), (kW, kWr)):
                dve.tensor_scalar(wr[:, 0:P:2], w[:, 1:P:2], -1.0, None, ALU.mult).then_inc(dve_did, seq.up())
                dve.tensor_copy(wr[:, 1:P:2], w[:, 0:P:2]).then_inc(dve_did, seq.up())
            dve.wait_ge(dve_did, seq.n)
            dve.sem_inc(dve_did, -seq.reset())
            dve.sem_inc(consts_ready, 1)
            for c in range(CH):
                make_slab(CH + c, WoT[:, c * P:(c + 1) * P], postX[:, c, :])
            dve.wait_ge(setup_done, 1)
            dve.sem_inc(P_free, 2)
            dve.sem_inc(yout_free, 16)

            def max1_of(par):
                for t in range(T):
                    dve.wait_ge(s1_full, 1)
                    dve.sem_inc(s1_full, -1)
                    dve.tensor_reduce(max1[:, t, :], psum(f"s1_{t}", par)[:, :].rearrange("p (h j) -> p h j", h=2),
                                      AX.X, ALU.max).then_inc(dve_did, seq.up())
                dve.wait_ge(dve_did, seq.n)
                dve.tensor_scalar(negmax1[:, :, :], max1[:, :, :], -float(D1) ** -0.5, None, ALU.mult).then_inc(negmax1_ready, 1)
                dve.wait_ge(dve_did, seq.n)
                dve.sem_inc(dve_did, -seq.reset())

            units = [(2 * h + t, h, c0, c1) for h in range(2) for t, (c0, c1) in enumerate(COLS)]

            def count_above(par):
                dve.wait_ge(threshold_ready, 1)
                dve.sem_inc(threshold_ready, -1)
                for u, h, c0, c1 in units:
                    last = dve.scalar_tensor_tensor(out=work[:, h, c0:c1], in0=S[par][:, h, c0:c1], scalar=threshold[:, u:u + 1],
                                                    in1=taken[:, 0:1].broadcast_to([P, c1 - c0]), op0=ALU.is_ge, op1=ALU.mult,
                                                    accum_out=above[:, u:u + 1])
                    last.then_inc(dve_did, seq.up())
                    if u % 2:
                        dve.wait_ge(dve_did, seq.n)
                        dve.sem_inc(above_ready, 1)
                dve.tensor_scalar(rank[:, :], above[:, :], 1 / TAKEN * -1.0, float(TOPK - 1), ALU.mult, ALU.add).then_inc(dve_did, seq.up())
                dve.wait_ge(dve_did, seq.n)
                dve.tensor_scalar(deep[:, :], rank[:, :], WINDOW - 0.5, None, ALU.is_gt).then_inc(dve_did, seq.up())
                dve.wait_ge(dve_did, seq.n)
                dve.scalar_tensor_tensor(out=missed[:, :], in0=rank[:, :], scalar=-0.5, in1=deep[:, :], op0=ALU.is_lt,
                                         op1=ALU.add).then_inc(missed_ready, 1)
                dve.wait_ge(dve_did, seq.n)
                dve.sem_inc(dve_did, -seq.reset())

            def upper_eight(par):
                got = {}
                for u, h, c0, c1 in units:
                    if u % 2 == 0:
                        dve.wait_ge(below_ready, 1)
                        dve.sem_inc(below_ready, -1)
                    dve.max(window[:, u, 0:8], work[:, h, c0:c1]).then_inc(dve_did, seq.up())
                    got[u] = seq.n
                for u, h, c0, c1 in units:
                    dve.wait_ge(dve_did, got[u])
                    dve.match_replace(work[:, h, c0:c1], window[:, u, 0:8], work[:, h, c0:c1], -BIG).then_inc(dve_did, seq.up())
                    got[u] = seq.n
                return got

            def lower_eight(par, got):
                for u, h, c0, c1 in units:
                    dve.wait_ge(dve_did, got[u])
                    dve.max(window[:, u, 8:WINDOW], work[:, h, c0:c1]).then_inc(dve_did, seq.up())
                dve.tensor_tensor(chosen[:, :, :], place[:, :].unsqueeze(1).broadcast_to([P, 4, WINDOW]),
                                  rank[:, :].unsqueeze(2).broadcast_to([P, 4, WINDOW]), ALU.is_equal).then_inc(dve_did, seq.up())
                dve.wait_ge(dve_did, seq.n)
                dve.tensor_tensor(chosen[:, :, :], chosen[:, :, :], window[:, :, :], ALU.mult).then_inc(dve_did, seq.up())
                dve.wait_ge(dve_did, seq.n)
                dve.tensor_reduce(kth[:, :], chosen[:, :, :], AX.X, ALU.add).then_inc(dve_did, seq.up())
                dve.wait_ge(dve_did, seq.n)
                dve.sem_inc(dve_did, -seq.reset())

            def all_eights(par):
                for r in range(TOPK // 8):
                    src = S[par] if r <= 1 else work
                    if r > 0:
                        for u, h, c0, c1 in units:
                            dve.match_replace(work[:, h, c0:c1], top[:, u, :], src[:, h, c0:c1], -BIG).then_inc(dve_did, seq.up())
                        dve.wait_ge(dve_did, seq.n)
                        src = work
                    for u, h, c0, c1 in units:
                        dve.max(top[:, u, :], src[:, h, c0:c1]).then_inc(dve_did, seq.up())
                    dve.wait_ge(dve_did, seq.n)
                dve.tensor_copy(kth[:, :], top[:, :, 7]).then_inc(dve_did, seq.up())
                dve.wait_ge(dve_did, seq.n)
                dve.sem_inc(dve_did, -seq.reset())

            def count_missed(par):
                dve.wait_ge(missed_full, 1)
                dve.sem_inc(missed_full, -1)
                dve.tensor_reduce(missed_n[:, :], psum("miss", par)[0:1, 0:4], AX.X, ALU.max).then_inc(dve_did, seq.up())
                dve.wait_ge(dve_did, seq.n)
                dve.sem_inc(bank_free[bank_of("miss", par)], 1)

            def repair(par):
                if seq.n:
                    dve.wait_ge(dve_did, seq.n)
                    dve.sem_inc(dve_did, -seq.reset())
                n_missed = dve.value_load(missed_n[0:1, 0:1])
                with dve.If(n_missed > 0):
                    all_eights(par)

            def sum_sizes(nxt):
                dve.wait_ge(s_copied, 1)
                dve.sem_inc(s_copied, -1)
                for t, (c0, c1) in enumerate(COLS):
                    last = dve.tensor_reduce(sizes[:, :, t], S[nxt][:, :, c0:c1], AX.X, ALU.add, apply_absolute_value=True)
                last.then_inc(sizes_ready, 1)

            def maxima(nxt):
                dve.wait_ge(s_masked, 1)
                dve.sem_inc(s_masked, -1)
                for t, (c0, c1) in enumerate(COLS):
                    last = dve.tensor_reduce(negmax[nxt][:, :, t], S[nxt][:, :, c0:c1], AX.X, ALU.max, negate=True)
                last.then_inc(negmax_ready, 1)

            def keep(par):
                dve.wait_ge(E_ready, 1)
                dve.sem_inc(E_ready, -1)
                dve.wait_ge(P_free, 1)
                dve.sem_inc(P_free, -1)
                for u, h, c0, c1 in units:
                    dve.scalar_tensor_tensor(out=Pr[par][:, PROBS[h][u % T]:PROBS[h][u % T] + c1 - c0], in0=S[par][:, h, c0:c1], scalar=kth[:, u:u + 1],
                                             in1=E[:, h, c0:c1], op0=ALU.is_ge, op1=ALU.mult,
                                             accum_out=psumA[:, u:u + 1]).then_inc(dve_did, seq.up())
                dve.wait_ge(dve_did, seq.n)
                dve.reciprocal(rsumA[par][:, :], psumA[:, :]).then_inc(kept_ready, 1)
                dve.wait_ge(dve_did, seq.n)
                dve.sem_inc(dve_did, -seq.reset())

            def add_expert(e, par):
                dve.wait_ge(y_full, 1)
                dve.sem_inc(y_full, -1)
                for t in range(T):
                    dve.scalar_tensor_tensor(out=yacc[:, t, :], in0=psum("y", par)[:, t * P:(t + 1) * P],
                                             scalar=gates[:, t, bass.ds(e, 1)], in1=yacc[:, t, :],
                                             op0=ALU.mult, op1=ALU.add).then_inc(dve_did, seq.up())
                dve.wait_ge(dve_did, seq.n)
                dve.sem_inc(dve_did, -seq.reset())
                dve.sem_inc(bank_free[bank_of("y", par)], 1)

            def statistics(src, i):
                for t in range(T):
                    dve.bn_stats(stats[:, i, t, :], src[:, t, :]).then_inc(dve_did, seq.up())
                dve.wait_ge(dve_did, seq.n)
                for t in range(T):
                    dve.bn_aggr(mv[:, i, t, :], stats[:, i, t, :]).then_inc(dve_did, seq.up())

            def normalised(dst, src, i, done):
                for t in range(T):
                    dve.tensor_scalar(dst[:, t, :], src[:, t, :], mv[:, i, t, 0:1], rstd[:, i, t:t + 1], ALU.subtract,
                                      ALU.mult).then_inc(dve_did, seq.up())
                dve.wait_ge(dve_did, seq.n)
                dve.sem_inc(done, 1)

            def over_experts(x):
                return x.unsqueeze(2).broadcast_to([P, T, EXP])

            def route():
                dve.wait_ge(lg_ready, 1)
                dve.sem_inc(lg_ready, -1)
                dve.tensor_reduce(lgs[:, 0, :], lg_raw[:, :, :], AX.X, ALU.max).then_inc(dve_did, seq.up())
                dve.wait_ge(dve_did, seq.n)
                dve.tensor_tensor(lg[:, 0, :, :], lg_raw[:, :, :], over_experts(lgs[:, 0, :]), ALU.subtract).then_inc(lg_shifted, 1)
                dve.wait_ge(lg_exp, 1)
                dve.sem_inc(lg_exp, -1)
                dve.tensor_reduce(lgs[:, 1, :], lg[:, 1, :, :], AX.X, ALU.add).then_inc(dve_did, seq.up())
                dve.wait_ge(dve_did, seq.n)
                dve.reciprocal(lgs[:, 2, :], lgs[:, 1, :]).then_inc(dve_did, seq.up())
                dve.wait_ge(dve_did, seq.n)
                dve.tensor_tensor(lg[:, 2, :, :], lg[:, 1, :, :], over_experts(lgs[:, 2, :]), ALU.mult).then_inc(dve_did, seq.up())
                dve.wait_ge(dve_did, seq.n)
                dve.tensor_reduce(lgs[:, 3, :], lg[:, 2, :, :], AX.X, ALU.max).then_inc(dve_did, seq.up())
                dve.wait_ge(dve_did, seq.n)
                dve.tensor_tensor(lg[:, 3, :, :], lg[:, 2, :, :], over_experts(lgs[:, 3, :]), ALU.is_ge).then_inc(dve_did, seq.up())
                dve.wait_ge(dve_did, seq.n)
                dve.tensor_tensor(lg[:, 4, :, :], lg[:, 3, :, :], first[:, :].unsqueeze(1).broadcast_to([P, T, EXP]),
                                  ALU.mult).then_inc(dve_did, seq.up())
                dve.wait_ge(dve_did, seq.n)
                dve.tensor_reduce(lgs[:, 0, :], lg[:, 4, :, :], AX.X, ALU.max).then_inc(dve_did, seq.up())
                dve.wait_ge(dve_did, seq.n)
                dve.tensor_tensor(lg[:, 5, :, :], lg[:, 4, :, :], over_experts(lgs[:, 0, :]), ALU.is_ge).then_inc(dve_did, seq.up())
                dve.wait_ge(dve_did, seq.n)
                dve.tensor_tensor(gates[:, :, :], lg[:, 5, :, :], lg[:, 2, :, :], ALU.mult).then_inc(gates_ready, 1)

            def start_sum():
                dve.wait_ge(base_full, 1)
                dve.sem_inc(base_full, -1)
                dve.tensor_tensor(yacc[:, :, :], psum("base")[:, 0:TOK].rearrange("p (t c) -> p t c", t=T), x3[:, :, :],
                                  ALU.add).then_inc(dve_did, seq.up())
                dve.wait_ge(dve_did, seq.n)
                dve.sem_inc(dve_did, -seq.reset())
                dve.sem_inc(bank_free[bank_of("base")], 1)

            def end_attention1():
                dve.wait_ge(pv_full, 1)
                dve.sem_inc(pv_full, -1)
                dve.reciprocal(rsum1[:, :, :], pv[:, :, :, D1]).then_inc(dve_did, seq.up())
                dve.wait_ge(dve_did, seq.n)
                o1_h = o1[:, :, :].rearrange("p t (h d) -> p t h d", h=H)
                dve.tensor_tensor(o1_h, pv[:, :, :, 0:D1], rsum1[:, :, :].unsqueeze(3).broadcast_to([P, T, H, D1]),
                                  ALU.mult).then_inc(dve_did, seq.up())
                dve.wait_ge(dve_did, seq.n)
                dve.sem_inc(pv_free, 1)
                dve.tensor_tensor(x3pre[:, :, :], o1[:, :, :], x2res[:, :, :], ALU.add).then_inc(dve_did, seq.up())
                dve.wait_ge(dve_did, seq.n)
                statistics(x3pre, 1)

            def mix_tokens():
                dve.wait_ge(x1T_ready, 1)
                dve.sem_inc(x1T_ready, -1)
                dve.tensor_tensor(dT[:, :], x1T[:, 1:1 + TOK], x1T[:, 0:TOK], ALU.subtract).then_inc(dve_did, seq.up())
                dve.wait_ge(dve_did, seq.n)
                for dst, mu in ((xrT, mu_r), (xkT, mu_k)):
                    last = dve.scalar_tensor_tensor(out=dst[:, :], in0=dT[:, :], scalar=mu[:, 0:1], in1=x1T[:, 0:TOK],
                                                    op0=ALU.mult, op1=ALU.add)
                last.then_inc(mixed_ready, 1)

            def end_channel_mix():
                dve.wait_ge(v_full, 1)
                dve.sem_inc(v_full, -1)
                v = psum("v")[:, 0:TOK].rearrange("p (t c) -> p t c", t=T)
                dve.scalar_tensor_tensor(out=x2pre[:, :, :], in0=th[:, :, :], scalar=1.0, in1=v, op0=ALU.add, op1=ALU.mult).then_inc(dve_did, seq.up())
                dve.wait_ge(dve_did, seq.n)
                dve.sem_inc(bank_free[bank_of("v")], 1)
                dve.scalar_tensor_tensor(out=x2pre[:, :, :], in0=x2pre[:, :, :], scalar=0.5, in1=x1[:, :, :],
                                         op0=ALU.mult, op1=ALU.add).then_inc(dve_did, seq.up())
                dve.wait_ge(dve_did, seq.n)
                statistics(x2pre, 2)

            def rotate():
                for i, (use, full, dst) in enumerate((("q", q_full, qT), ("k", k_full, kT))):
                    dve.wait_ge(full, 1)
                    dve.sem_inc(full, -1)
                    for j, table in enumerate((cosT, sinT)):
                        dve.tensor_tensor(rope[:, 2 * i + j, :], psum(use)[:, j * TOK:(j + 1) * TOK], table[:, :], ALU.mult).then_inc(dve_did, seq.up())
                    dve.wait_ge(dve_did, seq.n)
                    dve.sem_inc(bank_free[bank_of(use)], 1)
                    last = dve.tensor_tensor(dst[:, :], rope[:, 2 * i, :], rope[:, 2 * i + 1, :], ALU.add)
                last.then_inc(kT_ready, 1)

            def step(n, par, at, on):
                front = ("P" if at == STEPS - 1 else "A") in on
                e = expert_of(n, at, on)
                if "B" in on:
                    max1_of(par)
                if "A" in on:
                    count_above(par)
                if at == 0 and "C" in on:
                    end_attention1()
                if at == 2 and "D" in on:
                    statistics(yacc, 3)
                if at == 2 and "C" in on:
                    route()
                if "A" in on:
                    got = upper_eight(par)
                if front:
                    sum_sizes(1 - par)
                if at == 0 and "F" in on:
                    dve.wait_ge(acc_full, 1)
                    dve.sem_inc(acc_full, -1)
                    statistics(acc, 0)
                if at == 1 and "F" in on:
                    mix_tokens()
                if at == 2 and "F" in on:
                    end_channel_mix()
                if (at == 0 and on & {"F", "C"}) or (at == 2 and on & {"F", "D"}):
                    dve.wait_ge(dve_did, seq.n)
                    dve.sem_inc(var_ready, 1)
                if "A" in on:
                    count_missed(par)
                    lower_eight(par, got)
                if front:
                    maxima(1 - par)
                if (at == 0 and on & {"F", "C"}) or (at == 2 and on & {"F", "D"}):
                    dve.wait_ge(rstd_ready, 1)
                    dve.sem_inc(rstd_ready, -1)
                if at == 0 and "F" in on:
                    normalised(x1, acc, 0, x1_ready)
                if at == 0 and "C" in on:
                    normalised(x3, x3pre, 1, x3_ready)
                if at == 2 and "B" in on:
                    dve.wait_ge(x2_saved, 1)
                    dve.sem_inc(x2_saved, -1)
                if at == 2 and "F" in on:
                    normalised(x2, x2pre, 2, x2_ready)
                if at == 2 and "D" in on:
                    dve.wait_ge(yout_free, 16)
                    dve.sem_inc(yout_free, -16)
                    normalised(yout, yacc, 3, yout_full)
                if at == STEPS - 1 and "F" in on:
                    rotate()
                if "A" in on:
                    repair(par)
                    keep(par)
                if at == 2 and "C" in on:
                    start_sum()
                if e is not None:
                    add_expert(e, par)
                if seq.n:
                    dve.wait_ge(dve_did, seq.n)
                    dve.sem_inc(dve_did, -seq.reset())

            def iteration(it, on):
                steps(dve, lambda n, par, at: step(n, par, at, on), on)

            iterations(dve, iteration)

        @block.tensor
        def _(pe):
            pe.wait_ge(consts_ready, 2)
            pe.wait_ge(w_big, 14 * 16)
            for c in range(CH):
                pe.transpose(bank[c // 4][:, (c % 4) * P:(c % 4 + 1) * P], WoN[:, c, :], ident[:, :])
                pe.transpose(bank[2][:, c * MEM:(c + 1) * MEM], mkN[:, c * P:(c + 1) * P], ident[0:MEM, 0:MEM])
                pe.transpose(bank[3][:, c * MEM:(c + 1) * MEM], mvN[:, c * P:(c + 1) * P], ident[0:MEM, 0:MEM])
            for i, (b, k) in enumerate(((4, 0), (4, 1), (4, 2), (4, 3), (5, 0), (5, 1))):
                last = pe.transpose(bank[b][:, k * P:(k + 1) * P], smallN[:, i * P:(i + 1) * P], ident[:, :])
            last.then_inc(turned, 1)
            pe.wait_ge(turned_out, 2)
            for c in range(CH):
                pe.wait_ge(slab_ready, c + 1)
                for b in range(4):
                    pe.matmul(bank[b][:, :], WkN[:, c, :], slab[c % 2][:, b * 512:(b + 1) * 512], start=(c == 0), stop=(c == CH - 1))
                for k in range(H):
                    last = pe.matmul(bank[4 + k // 8][:, (k % 8) * MEM:(k % 8 + 1) * MEM], slab[c % 2][:, k * P:(k + 1) * P],
                                     mkT[:, c * MEM:(c + 1) * MEM], start=(c == 0 and k % 8 == 0), stop=(c == CH - 1),
                                     skip_group_check=True)
                last.then_inc(slab_free, 1)
            pe.drain().then_inc(fold_full, 1)
            pe.wait_ge(fold_out, 1)
            for c in range(CH):
                pe.wait_ge(slab_ready, CH + c + 1)
                for b, mem in enumerate((bank[4], bank[5], acc_bank, pv_bank)):
                    sl = slab[c % 2][:, b * 512:(b + 1) * 512]
                    pe.matmul(bank[b][:, :], WvN[:, c, :], sl, start=(c == 0), stop=(c == CH - 1))
                    last = pe.matmul(mem[:, :], mvT[:, c, :, :], sl, start=(c == 0), stop=(c == CH - 1))
                last.then_inc(slab_free, 1)
            pe.drain().then_inc(fold_full, 1)
            pe.wait_ge(setup_done, 1)
            for f in bank_free:
                pe.sem_inc(f, 1)

            def take_bank(use, par=0):
                pe.wait_ge(bank_free[bank_of(use, par)], 1)
                pe.sem_inc(bank_free[bank_of(use, par)], -1)
                return psum(use, par)

            def give_bank(use, par=0):
                pe.sem_inc(bank_free[bank_of(use, par)], 1)

            keys_flat = keys[:, :, :, :].rearrange("p s a j -> p s (a j)")

            def scores1(n, par):
                for t in range(T):
                    b = take_bank(f"s1_{t}", par)
                    pe.matmul(b[:, :].rearrange("p (h j) -> p h j", h=2), qT[:, t * P:(t + 1) * P],
                              keys1[:, bass.ds(2 * n, 2), :], start=True, stop=True).then_inc(s1_full, 1)

            def scores(n, h, par):
                b = take_bank(f"s_{h}", par)
                for t, (c0, c1) in enumerate(COLS):
                    last = pe.matmul(b[:, c0:c1], xT[:, t * P:(t + 1) * P], keys_flat[:, n, KEYS[h][t][0]:KEYS[h][t][1]],
                                     start=True, stop=True)
                last.then_inc(s_full, 1)

            def project(n, par):
                pe.wait_ge(A_full[par], 16)
                pe.sem_inc(A_full[par], -16)
                b = take_bank("pg", par)
                for t in range(T):
                    pe.matmul(b[:, t * P:(t + 1) * P], A_st[par][:, 0, :], xT_next[:, (1 - t) * P:(2 - t) * P], start=True, stop=True)
                last = pe.matmul(b[:, TOK:2 * TOK], A_st[par][:, 1, :], xT_next[:, :], start=True, stop=True)
                last.then_inc(pg_full, 1)
                b = take_bank("pu", par)
                for t in range(T):
                    last = pe.matmul(b[:, t * TOK:(t + 1) * TOK].rearrange("p (h c) -> p h c", h=2),
                                     xT_next[:, t * P:(t + 1) * P], B_all[:, bass.ds(2 * n, 2), :], start=True, stop=True)
                last.then_inc(pu_full, 1)

            def turn_probs(prev, par):
                pe.wait_ge(probs_ready, 1)
                pe.sem_inc(probs_ready, -1)
                b = take_bank("ptm", par)
                for t in range(T):
                    last = pe.transpose(b[:, t * P:(t + 1) * P], Pr[prev][:, MEM_AT[t]:MEM_AT[t] + 2 * MEM], ident[:, :])
                last.then_inc(pt_full, 1)
                for h in range(2):
                    b = take_bank(f"pt_{h}", par)
                    for i, c0 in enumerate(TOKENS_AT[h]):
                        last = pe.transpose(b[:, i * P:(i + 1) * P], Pr[prev][:, c0:c0 + P], ident[:, :])
                    last.then_inc(pt_full, 1)

            def attend(n, ring, par, last_of_batch=False):
                for h in range(2):
                    pe.wait_ge(pt_ready, 1)
                    pe.sem_inc(pt_ready, -1)
                    if h == 0:
                        give_bank("ptm", par)
                        for t in range(T):
                            pe.matmul(acc[:, t, :], PTm[:, t, :], UM[:, n, :], start=False, stop=False, skip_group_check=True)
                    give_bank(f"pt_{h}", par)
                    for i, (t, jt) in enumerate(((0, 0), (1, 0), (1, 1))):
                        last = pe.matmul(acc[:, t, :], PT[h][:, i, :], vals[:, ring, jt, h, :], start=False,
                                         stop=last_of_batch and h == 1 and i != 1, skip_group_check=True)
                if last_of_batch:
                    last.then_inc(acc_full, 1)

            def hidden(par):
                pe.wait_ge(W1_full[par], 16)
                pe.sem_inc(W1_full[par], -16)
                for i in range(2):
                    b = take_bank(f"h_{i}", par)
                    for f in range(2):
                        c = 2 * i + f
                        last = pe.matmul(b[:, f * TOK:(f + 1) * TOK], W1_st[par][:, c * P:(c + 1) * P], x3T[:, :], start=True, stop=True)
                    last.then_inc(h_full, 1)

            def turn_probs1(par):
                pe.wait_ge(E1_ready, 1)
                pe.sem_inc(E1_ready, -1)
                for h in range(2):
                    b = take_bank(f"p1_{h}", par)
                    for jt in range(T):
                        for t in range(T):
                            last = pe.transpose(b[:, (2 * jt + t) * P:(2 * jt + t + 1) * P], E1[:, t, h, jt * P:(jt + 1) * P], ident[:, :])
                    last.then_inc(p1_full, 1)

            def attend1(n, par, last_of_batch):
                for h in range(2):
                    pe.wait_ge(p1_ready, 1)
                    pe.sem_inc(p1_ready, -1)
                    give_bank(f"p1_{h}", par)
                    for t in range(T):
                        for jt in range(T):
                            last = pe.matmul(pv[:, t, 2 * n + h, :], E1T[h][:, jt, t, :], vals1[:, jt, 2 * n + h, :],
                                             start=(jt == 0), stop=(jt == T - 1))
                if last_of_batch:
                    last.then_inc(pv_full, 1)

            def experts_out(e, par):
                b = take_bank("y", par)
                for t in range(T):
                    for f in range(FF // P):
                        last = pe.matmul(b[:, t * P:(t + 1) * P], hT[f // 2][:, f % 2, t * P:(t + 1) * P], W2[:, e, f, :],
                                         start=(f == 0), stop=(f == FF // P - 1))
                last.then_inc(y_full, 1)

            def turn(use, src, full):
                b = take_bank(use)
                for t in range(T):
                    last = pe.transpose(b[:, t * P:(t + 1) * P], src[:, t, :], ident[:, :])
                last.then_inc(full, 1)

            def per_tile(b, c0, lhsT, w):
                for t in range(T):
                    last = pe.matmul(b[:, c0 + t * P:c0 + (t + 1) * P], lhsT[:, t * P:(t + 1) * P], w[:, :], start=True, stop=True)
                return last

            def step(it, n, par, at, on):
                last = at == STEPS - 1
                e = expert_of(n, at, on)
                if "B" in on:
                    for _ in range({0: 1, 2: 3}.get(at, 0)):
                        pe.wait_ge(keys1_ready, 1)
                        pe.sem_inc(keys1_ready, -1)
                    scores1(n, par)
                if at == 0 and "P" in on:
                    pe.wait_ge(xload_full, 16)
                    pe.sem_inc(xload_full, -16)
                    turn("xt", xload, xt_full)
                if at == 1 and "F" in on:
                    pe.wait_ge(x1_ready, 1)
                    pe.sem_inc(x1_ready, -1)
                    turn("x1t", x1, x1t_full)
                if e is not None:
                    hidden(par)
                if ("F" if at == 0 else "A") in on:
                    turn_probs(1 - par, par)
                if last and "P" in on:
                    pe.wait_ge(xT_ready, 1)
                    pe.sem_inc(xT_ready, -1)
                for h in range(2):
                    if ("P" if last else "A") in on:
                        scores(0 if last else n + 1, h, par)
                    if e is not None:
                        pe.wait_ge(h_ready, 1)
                        pe.sem_inc(h_ready, -1)
                        give_bank(f"h_{h}", par)
                if at == 1 and "A" in on:
                    pe.wait_ge(xres_full, 16)
                    pe.sem_inc(xres_full, -16)
                    pe.matmul(acc_bank[:, 0:TOK], ident[:, :], xres[:, :, :].rearrange("p t c -> p (t c)"), start=True, stop=False,
                              skip_group_check=True)
                    for t in range(T):
                        pe.matmul(acc[:, t, :], ones[0:1, :], brow[:, :], start=False, stop=False, skip_group_check=True)
                if at == 0 and "F" in on:
                    attend(STEPS - 1, (STEPS * it - 1) % RING, par, last_of_batch=True)
                if at != 0 and "A" in on:
                    attend(n - 1, (STEPS * it + n - 1) % RING, par)
                if at == 1 and "C" in on:
                    pe.wait_ge(x3_ready, 1)
                    pe.sem_inc(x3_ready, -1)
                    turn("x3t", x3, x3t_full)
                if at == 2 and "F" in on:
                    pe.wait_ge(kact_ready, 1)
                    pe.sem_inc(kact_ready, -1)
                    per_tile(take_bank("v"), 0, kact, WvT).then_inc(v_full, 1)
                if "P" in on:
                    if at == 0:
                        pe.wait_ge(xt_ready, 1)
                        pe.sem_inc(xt_ready, -1)
                    project(n, par)
                if "A" in on:
                    pe.wait_ge(missed_ready, 1)
                    pe.sem_inc(missed_ready, -1)
                    pe.matmul(take_bank("miss", par)[0:1, 0:4], ones[:, 0:1], missed[:, :], start=True, stop=True).then_inc(missed_full, 1)
                if at == 2 and "C" in on:
                    pe.wait_ge(gates_ready, 1)
                    pe.sem_inc(gates_ready, -1)
                    b = take_bank("gt")
                    for t in range(T):
                        turned_gates = pe.transpose(b[0:EXP, t * P:(t + 1) * P], gates[:, t, :], ident[:, :])
                    turned_gates.then_inc(gt_full, 1)
                if "B" in on:
                    turn_probs1(par)
                if at == 1 and "F" in on:
                    pe.wait_ge(mixed_ready, 1)
                    pe.sem_inc(mixed_ready, -1)
                    b = take_bank("kr")
                    pe.matmul(b[:, 0:TOK], WkT[:, :], xkT[:, :], start=True, stop=True)
                    per_tile(b, TOK, xrT, WrT).then_inc(kr_full, 1)
                if at == 1 and "C" in on:
                    pe.wait_ge(x3T_ready, 1)
                    pe.sem_inc(x3T_ready, -1)
                    b = take_bank("lg")
                    for t in range(T):
                        pe.matmul(b[:, t * EXP:(t + 1) * EXP], x3T[:, t * P:(t + 1) * P], rW[:, :], start=True, stop=False)
                        logits = pe.matmul(b[:, t * EXP:(t + 1) * EXP], ones[0:1, :], rb[:, :], start=False, stop=True)
                    logits.then_inc(lg_full, 1)
                if last and "F" in on:
                    pe.wait_ge(x2T_ready, 1)
                    pe.sem_inc(x2T_ready, -1)
                    for use, w, wr, full in (("q", qW, qWr, q_full), ("k", kW, kWr, k_full)):
                        b = take_bank(use)
                        pe.matmul(b[:, 0:TOK], w[:, :], x2T[:, :], start=True, stop=True)
                        pe.matmul(b[:, TOK:2 * TOK], wr[:, :], x2T[:, :], start=True, stop=True).then_inc(full, 1)
                if e is not None:
                    experts_out(e, par)
                if at == 2 and "C" in on:
                    pe.wait_ge(gT_ready, 1)
                    pe.sem_inc(gT_ready, -1)
                    per_tile(take_bank("base"), 0, gT, b2).then_inc(base_full, 1)
                if at == 0 and "C" in on:
                    pe.wait_ge(pv_free, 1)
                    pe.sem_inc(pv_free, -1)
                if "B" in on:
                    attend1(n, par, last)
                if at == 2 and "F" in on:
                    pe.wait_ge(x2_ready, 1)
                    pe.sem_inc(x2_ready, -1)
                    turn("x2t", x2, x2t_full)
                if last and "F" in on:
                    per_tile(take_bank("vv"), 0, x2T, vW).then_inc(vv_full, 1)

            def iteration(it, on):
                steps(pe, lambda n, par, at: step(it, n, par, at, on), on)

            iterations(pe, iteration)


INPUTS = ("L0_attn_x", "L0_attn_Wq", "L0_attn_Wk", "L0_attn_Wv", "L0_attn_pre_proj", "L0_attn_post_proj", "L0_attn_mem_k",
          "L0_attn_mem_v", "L0_attn_Wout", "L0_attn_bout", "L0_ffn_W_r", "L0_ffn_W_k", "L0_ffn_W_v", "L0_ffn_mu_r",
          "L0_ffn_mu_k", "L1_attn_Wq", "L1_attn_Wk", "L1_attn_Wv", "L1_ffn_router_W", "L1_ffn_router_b", "L1_ffn_W1",
          "L1_ffn_b1", "L1_ffn_W2", "L1_ffn_b2")


def kernel(**inputs):
    import numpy as np
    import concourse.bacc as bacc
    from concourse.bass_utils import run_bass_kernel_spmd

    arrays = {n: np.ascontiguousarray(inputs[n]) for n in INPUTS}
    pos = np.arange(TOK, dtype=np.float32)
    inv = np.power(np.float32(10000.0), -2.0 * np.arange(D1 // 2, dtype=np.float32) / D1).astype(np.float32)
    angle = np.tile(np.repeat(inv[:, None] * pos[None, :], 2, axis=0), (H, 1))
    arrays["cosT"] = np.cos(angle).astype(np.float32)
    arrays["sinT"] = np.sin(angle).astype(np.float32)
    arrays["guess"] = threshold_tables()
    nc = bacc.Bacc("TRN2", target_bir_lowering=False, num_devices=1)
    a = {n: nc.dram_tensor(f"{n}_dram", v.shape, F32, kind="ExternalInput").ap() for n, v in arrays.items()}
    shape = arrays["L0_attn_x"].shape
    a["out"] = nc.dram_tensor("out_dram", shape, F32, kind="ExternalOutput").ap()
    build(nc, a, shape[0])
    r = run_bass_kernel_spmd(nc, [{f"{n}_dram": v for n, v in arrays.items()}], core_ids=[0])
    return r.results[0]["out_dram"]
```

```python
from contextlib import ExitStack

import concourse.bass as bass
from concourse import mybir

F32 = mybir.dt.float32
ALU = mybir.AluOpType
ACT = mybir.ActivationFunctionType
AX = mybir.AxisListType

P = 128
T = 2
TOK = T * P
H = 16
MEM = 64
DH = 64
TOPK = 64
CH = H * DH // P
D1 = P // H
EXP = 8
FF = 512
STEPS = 8
RING = STEPS + 2
W0 = MEM + P
W1 = MEM + TOK
COLS = ((0, W0), (W0, W0 + W1))
KEYS = (((P, W1), (0, W1)), ((W1, W1 + W0), (W1, 2 * W1)))
PROBS = ((0, 2 * W0), (W0, 2 * W0 + W1))
MEM_AT = (P, 2 * W0 + TOK)
TOKENS_AT = ((0, 2 * W0 + P, 2 * W0), (2 * P, 2 * W0 + W1 + MEM, 2 * W0 + W1 + MEM + P))
TAKEN = -2.0 ** 118
SAMPLE = 2
WINDOW = 16
BIG = 3.4028234663852886e38
EPS = 1e-5

BANK = {"s1_0": 0, "s1_1": 5, "h_0": 1, "h_1": 3, "pt_0": 4, "pt_1": 2, "s_0": 0, "s_1": 5, "miss": 1,
        "p1_0": 4, "p1_1": 3, "pg": 2, "pu": 1, "y": 2,
        "xt": 3, "x1t": 4, "x3t": 0, "kr": 4, "lg": 3, "v": 5, "gt": 1, "base": 1, "x2t": 4, "q": 0, "k": 5, "vv": 4}
NBANK = 6


def threshold_tables():
    import math
    import numpy as np

    table = np.zeros((P, 5, 2 * T), np.float32)
    for t, (c0, c1) in enumerate(COLS):
        width = c1 - c0
        shift = width - 2 * (TOPK - 0.5 - WINDOW / 2)
        for p in range(P):
            seen = MEM + 1 + t * P + p
            share = (TOPK - 0.5 - WINDOW / 2) / seen
            low, z = -9.0, 9.0
            for _ in range(60):
                middle = (low + z) / 2
                low, z = (middle, z) if 0.5 * math.erfc(middle / 2 ** 0.5) > share else (low, middle)
            density = math.exp(-z * z / 2) / (2 * math.pi) ** 0.5
            sigma = (np.pi / 2) ** 0.5 / (width / SAMPLE)
            g1, g2 = (damp * sigma / (2 * seen * density) for damp in (1.0, 0.55))
            for h in range(2):
                table[p, :, 2 * h + t] = -z * sigma, -z * sigma - g1 * shift, -g1, g2, -g2 * shift
    return table


class Count:

    def __init__(self):
        self.n = 0

    def up(self):
        self.n += 1
        return 1

    def reset(self):
        n, self.n = self.n, 0
        return n


def flags(it, nb):
    lag = {"L": -2, "P": -1, "A": 0, "F": 1, "B": 2, "C": 3, "D": 4}
    return {s for s, n in lag.items() if 0 <= it - n < nb}


def build(nc, a, nb):
    with ExitStack() as ctx:
        def sb(name, *shape):
            return ctx.enter_context(nc.sbuf_tensor(name, [shape[0], *shape[1:]], F32))

        def sem(name):
            return ctx.enter_context(nc.semaphore(name))

        ident = sb("ident", P, P)
        ones = sb("ones", P, P)
        A_all = sb("A_all", P, H, P)
        B_all = sb("B_all", P, H, P)
        UM = sb("UM", P, STEPS, P)
        keys = sb("keys", P, STEPS, 2, P + TOK)
        vals = sb("vals", P, RING, T, 2, P)
        WkT, WrT, WvT = (sb(n, P, P) for n in ("WkT", "WrT", "WvT"))
        qW, qWr, kW, kWr, vW = (sb(n, P, P) for n in ("qW", "qWr", "kW", "kWr", "vW"))
        cosT, sinT = sb("cosT", P, TOK), sb("sinT", P, TOK)
        hmask = sb("hmask", P, H)
        mu_r, mu_k = sb("mu_r", P, 1), sb("mu_k", P, 1)
        brow = sb("brow", 1, P)
        rW = sb("rW", P, EXP)
        rb = sb("rb", 1, EXP)
        b1c = sb("b1c", P, EXP, FF // P)
        W2 = sb("W2", P, EXP, FF // P, P)
        b2 = sb("b2", EXP, P)
        first = sb("first", P, EXP)
        guess = sb("guess", P, 5, 4)
        place = sb("place", P, WINDOW)
        taken = sb("taken", P, 1)
        minus_half = sb("minus_half", P, 2 * T)
        A_st = [sb(f"A_st{i}", P, 2, P) for i in range(2)]
        W1_st = [sb(f"W1_st{i}", P, FF) for i in range(2)]
        xload = sb("xload", P, T, P)
        xres = sb("xres", P, T, P)
        xT_next = sb("xT_next", P, TOK)
        xT = sb("xT", P, TOK)
        S = [sb(f"S{i}", P, 2, W0 + W1) for i in range(2)]
        work = sb("work", P, 2, W0 + W1)
        E = sb("E", P, 2, W0 + W1)
        Pr = [sb(f"Pr{i}", P, 2 * (W0 + W1)) for i in range(2)]
        signs = sb("signs", P, 2, W0 + W1)
        sizes = sb("sizes", P, 2, T)
        fit = sb("fit", P, 5, 4)
        signsum = [sb(f"signsum{i}", P, 4) for i in range(2)]
        moved = sb("moved", P, 4)
        neg_t = sb("neg_t", P, 4)
        neg_t_next = sb("neg_t_next", P, 4)
        threshold = sb("threshold", P, 4)
        above = sb("above", P, 4)
        rank = sb("rank", P, 4)
        deep = sb("deep", P, 4)
        missed = sb("missed", P, 4)
        missed_n = ctx.enter_context(nc.sbuf_tensor("missed_n", [1, 1], mybir.dt.int32))
        window = sb("window", P, 4, WINDOW)
        chosen = sb("chosen", P, 4, WINDOW)
        kth = sb("kth", P, 4)
        top = sb("top", P, 4, 8)
        negmax = [sb(f"neg_top{i}", P, 2, T) for i in range(2)]
        psumA = sb("psumA", P, 4)
        rsumA = [sb(f"rsumA{i}", P, 4) for i in range(2)]
        PT = sb("PT", P, 8, P)
        x1 = sb("x1", P, T, P)
        x1T = sb("x1T", P, 1 + TOK)
        dT, xrT, xkT = sb("dT", P, TOK), sb("xrT", P, TOK), sb("xkT", P, TOK)
        th = sb("th", P, T, P)
        rk = sb("rk", P, TOK)
        kact = sb("kact", P, TOK)
        x2 = sb("x2", P, T, P)
        x2res = sb("x2res", P, T, P)
        x2pre = sb("x2pre", P, T, P)
        x2T = sb("x2T", P, TOK)
        rope = sb("rope", P, 4, TOK)
        qT, kT = sb("qT", P, TOK), sb("kT", P, TOK)
        keys1 = sb("keys1", P, H, TOK)
        vals1 = sb("vals1", P, T, H, D1 + 1)
        negmax1 = sb("negmax1", P, T, 2)
        E1 = sb("E1", P, T, 2, TOK)
        E1T = [sb(f"E1T{i}", P, T, T, P) for i in range(2)]
        rsum1 = sb("rsum1", P, T, H)
        o1 = sb("o1", P, T, P)
        x3pre = sb("x3pre", P, T, P)
        x3 = sb("x3", P, T, P)
        x3T = sb("x3T", P, TOK)
        lg_raw = sb("lg_raw", P, T, EXP)
        lg = sb("lg", P, 4, T, EXP)
        lgs = sb("lgs", P, 4, T)
        gates = sb("gates", P, T, EXP)
        gT = sb("gT", EXP, TOK)
        hT = [sb(f"hT{i}", P, 2, TOK) for i in range(2)]
        yacc = sb("yacc", P, T, P)
        yout = sb("yout", P, T, P)
        stats = sb("stats", P, 4, T, 6)
        mv = sb("mv", P, 4, T, 2)
        rstd = sb("rstd", P, 4, T)
        var = sb("var", P, 4, T)

        bank = [ctx.enter_context(nc.psum_tensor(f"bank{i}", [P, 512], F32)) for i in range(NBANK)]
        acc_bank = ctx.enter_context(nc.psum_tensor("acc_bank", [P, 512], F32))
        pv_bank = ctx.enter_context(nc.psum_tensor("pv_bank", [P, 512], F32))
        acc = acc_bank[:, 0:TOK].rearrange("p (t c) -> p t c", t=T)
        pv = pv_bank[:, 0:T * H * (D1 + 1)].rearrange("p (t h e) -> p t h e", t=T, h=H)

        nat = keys1[:, :, :].rearrange("p h j -> p (h j)")
        WqN, WkN, WvN, WoN = (nat[:, i * CH * P:(i + 1) * CH * P].rearrange("p (c k) -> p c k", c=CH) for i in range(4))
        slab = [vals[:, :, :, :, :].rearrange("p r t h c -> p (r t h c)")[:, i * H * P:(i + 1) * H * P] for i in range(2)]
        mkN = work[0:MEM, :, :].rearrange("p h j -> p (h j)")
        mvN = E[0:MEM, :, :].rearrange("p h j -> p (h j)")
        WoT = S[0][:, :, :].rearrange("p h j -> p (h j)")
        mkT = S[1][:, 0, :]
        mvT = Pr[0][:, :].rearrange("p (c r m) -> p c r m", c=CH, r=2)
        preB, postB = rope[:, 0, :], rope[:, 1, :]
        preX = rope[:, 2, 0:CH * H].rearrange("p (c k) -> p c k", c=CH)
        postX = rope[:, 3, 0:CH * H].rearrange("p (c k) -> p c k", c=CH)
        smallN = E1[:, :, :, :].rearrange("p t h j -> p (t h j)")

        w_big = sem("w_big")
        w_small = sem("w_small")
        consts_ready = sem("consts_ready")
        turned = sem("turned")
        turned_out = sem("turned_out")
        slab_ready = sem("slab_ready")
        slab_free = sem("slab_free")
        fold_full = sem("fold_full")
        fold_out = sem("fold_out")
        setup_done = sem("setup_done")
        bank_free = [sem(f"bank{i}_free") for i in range(NBANK)]
        A_full, A_free = [sem(f"A_full{i}") for i in range(2)], [sem(f"A_free{i}") for i in range(2)]
        W1_full, W1_free = [sem(f"W1_full{i}") for i in range(2)], [sem(f"W1_free{i}") for i in range(2)]
        xload_full = sem("xload_full")
        xload_free = sem("xload_free")
        xres_full = sem("xres_full")
        xres_free = sem("xres_free")
        xt_full = sem("xt_full")
        xt_ready = sem("xt_ready")
        xT_ready = sem("xT_ready")
        pg_full = sem("pg_full")
        pu_full = sem("pu_full")
        s_full = sem("s_full")
        s_out = sem("s_out")
        s_copied = sem("s_copied")
        sizes_ready = sem("sizes_ready")
        s_masked = sem("s_masked")
        neg_t_ready = sem("neg_t_ready")
        signs_ready = sem("signs_ready")
        threshold_ready = sem("threshold_ready")
        above_ready = sem("above_ready")
        below_ready = sem("below_ready")
        missed_ready = sem("missed_ready")
        missed_full = sem("missed_full")
        E_free = sem("E_free")
        S_free = sem("S_free")
        negmax_ready = sem("negmax_ready")
        E_ready = sem("E_ready")
        P_free = sem("P_free")
        kept_ready = sem("kept_ready")
        probs_ready = sem("probs_ready")
        pt_full = sem("pt_full")
        pt_ready = sem("pt_ready")
        acc_full = sem("acc_full")
        var_ready = sem("var_ready")
        rstd_ready = sem("rstd_ready")
        x1_ready = sem("x1_ready")
        x1t_full = sem("x1t_full")
        x1T_ready = sem("x1T_ready")
        mixed_ready = sem("mixed_ready")
        kr_full = sem("kr_full")
        kact_ready = sem("kact_ready")
        v_full = sem("v_full")
        x2_ready = sem("x2_ready")
        x2t_full = sem("x2t_full")
        x2T_ready = sem("x2T_ready")
        q_full = sem("q_full")
        k_full = sem("k_full")
        vv_full = sem("vv_full")
        kT_ready = sem("kT_ready")
        keys1_ready = sem("keys1_ready")
        s1_full = sem("s1_full")
        negmax1_ready = sem("negmax1_ready")
        E1_ready = sem("E1_ready")
        p1_full = sem("p1_full")
        p1_ready = sem("p1_ready")
        pv_full = sem("pv_full")
        pv_free = sem("pv_free")
        x3_ready = sem("x3_ready")
        x3t_full = sem("x3t_full")
        x3T_ready = sem("x3T_ready")
        lg_full = sem("lg_full")
        lg_ready = sem("lg_ready")
        lg_shifted = sem("lg_shifted")
        lg_exp = sem("lg_exp")
        gates_ready = sem("gates_ready")
        gt_full = sem("gt_full")
        gT_ready = sem("gT_ready")
        base_full = sem("base_full")
        h_full = sem("h_full")
        h_ready = sem("h_ready")
        y_full = sem("y_full")
        yout_full = sem("yout_full")
        yout_free = sem("yout_free")
        dve_did = sem("dve_did")
        pool_did = sem("pool_did")
        act_did = sem("act_did")

        def iterations(eng, iteration):
            for it in range(-1, 4):
                iteration(it, flags(it, nb))
            with eng.Fori(4, nb - 2) as it:
                iteration(it, set("LPAFBCD"))
            for it in range(nb - 2, nb + 4):
                iteration(it, flags(it, nb))

        def steps(eng, step, on):
            for n in range(3):
                step(n, n % 2, n)
            if on & {"A", "P", "B", "C"}:
                with eng.Fori(0, 2) as q:
                    step(2 * q + 3, 1, None)
                    step(2 * q + 4, 0, None)
            step(STEPS - 1, 1, STEPS - 1)

        def expert_of(n, at, on):
            if at in (0, 1):
                return n + EXP - 2 if "D" in on else None
            return n - 2 if "C" in on else None

        def psum(use):
            return bank[BANK[use]]

        block = ctx.enter_context(nc.Block())

        @block.sync
        def _(sp):
            for dst, w in ((WqN, "L0_attn_Wq"), (WkN, "L0_attn_Wk"), (WvN, "L0_attn_Wv")):
                sp.dma_start(dst, a[w].rearrange("(c p) k -> p c k", p=P)).then_inc(w_big, 16)
            sp.dma_start(WoN, a["L0_attn_Wout"].rearrange("p (c k) -> p c k", c=CH)).then_inc(w_big, 16)
            for dst, w in ((mkN, "L0_attn_mem_k"), (mvN, "L0_attn_mem_v")):
                sp.dma_start(dst.rearrange("j (h d) -> j h d", h=H), a[w].rearrange("h j d -> j h d")).then_inc(w_big, 16)
            for dst, w in ((preB, "L0_attn_pre_proj"), (postB, "L0_attn_post_proj")):
                sp.dma_start(dst, a[w].rearrange("h k -> (h k)").partition_broadcast(P)).then_inc(w_big, 16)
            for n, w in enumerate(("L0_ffn_W_r", "L0_ffn_W_k", "L0_ffn_W_v", "L1_attn_Wq", "L1_attn_Wk", "L1_attn_Wv")):
                sp.dma_start(smallN[:, n * P:(n + 1) * P], a[w]).then_inc(w_big, 16)
            x_in = a["L0_attn_x"].rearrange("b (t p) c -> b p t c", p=P)
            out = a["out"].rearrange("b (t p) c -> b p t c", p=P)
            sp.dma_start(xload[:, :, :], x_in[0]).then_inc(xload_full, 16)
            sp.dma_start(xres[:, :, :], x_in[0]).then_inc(xres_full, 16)
            for dst, w in ((mu_r, "L0_ffn_mu_r"), (mu_k, "L0_ffn_mu_k")):
                sp.dma_start(dst[:, :], a[w].rearrange("(p o) -> p o", o=1)).then_inc(w_small, 16)
            for dst, w in ((brow, "L0_attn_bout"), (rb, "L1_ffn_router_b")):
                sp.dma_start(dst[:, :], a[w].rearrange("(o c) -> o c", o=1)).then_inc(w_small, 16)
            sp.dma_start(rW[:, :], a["L1_ffn_router_W"]).then_inc(w_small, 16)
            with nc.allow_non_contiguous_dma(reason="4096 biases, once"):
                for e in range(EXP):
                    sp.dma_start(b1c[:, e, :], a["L1_ffn_b1"][e].rearrange("(f p) -> p f", p=P)).then_inc(w_small, 16)
            for e in range(EXP):
                sp.dma_start(W2[:, e, :, :], a["L1_ffn_W2"][e].rearrange("(f p) d -> p f d", p=P)).then_inc(w_small, 16)
            for dst, w in ((b2, "L1_ffn_b2"), (cosT, "cosT"), (sinT, "sinT")):
                sp.dma_start(dst[:, :], a[w]).then_inc(w_small, 16)
            sp.dma_start(guess[:, :, :], a["guess"]).then_inc(w_small, 16)
            sp.wait_ge(setup_done, 1)
            for f in (*A_free, *W1_free):
                sp.sem_inc(f, 1)

            def stage_weights(n, par, at, on):
                if "P" in on:
                    sp.wait_ge(A_free[par], 1)
                    sp.sem_inc(A_free[par], -1)
                    sp.dma_start(A_st[par][:, :, :], A_all[:, bass.ds(2 * n, 2), :]).then_inc(A_full[par], 16)
                e = expert_of(n, at, on)
                if e is not None:
                    sp.wait_ge(W1_free[par], 1)
                    sp.sem_inc(W1_free[par], -1)
                    sp.dma_start(W1_st[par][:, :], a["L1_ffn_W1"][e]).then_inc(W1_full[par], 16)

            def iteration(it, on):
                steps(sp, lambda n, par, at: stage_weights(n, par, at, on), on)
                if {"A", "P"} <= on:
                    sp.wait_ge(xres_free, 1)
                    sp.sem_inc(xres_free, -1)
                    sp.dma_start(xres[:, :, :], x_in[it + 1]).then_inc(xres_full, 16)
                if "L" in on:
                    sp.wait_ge(xload_free, 1)
                    sp.sem_inc(xload_free, -1)
                    sp.dma_start(xload[:, :, :], x_in[it + 2]).then_inc(xload_full, 16)
                if "D" in on:
                    sp.wait_ge(yout_full, 1)
                    sp.sem_inc(yout_full, -1)
                    sp.dma_start(out[it - 4], yout[:, :, :]).then_inc(yout_free, 16)

            iterations(sp, iteration)
            sp.wait_ge(yout_free, 16)

        @block.gpsimd
        def _(pool):
            seq = Count()
            for dst, value in ((ones[:, :], 1.0), (ident[:, :], 0.0), (hmask[:, :], 1.0), (minus_half[:, :], -0.5),
                               (x1T[:, 0:1], 0.0), (vals1[:, :, :, :], 1.0), (taken[:, :], TAKEN)):
                pool.memset(dst, value).then_inc(pool_did, seq.up())
            for e in range(EXP):
                pool.memset(first[:, e:e + 1], float(EXP - e)).then_inc(pool_did, seq.up())
            for i in range(WINDOW):
                pool.memset(place[:, i:i + 1], float(i)).then_inc(pool_did, seq.up())
            pool.wait_ge(pool_did, seq.n)
            pool.affine_select(out=ident[:, :], in_=ident[:, :], compare_op=ALU.not_equal, fill=1.0, base=0,
                               pattern=[[-1, P]], channel_multiplier=1).then_inc(pool_did, seq.up())
            pool.affine_select(out=hmask[:, :], in_=hmask[:, :], compare_op=ALU.is_ge, fill=0.0, base=0,
                               pattern=[[-D1, H]], channel_multiplier=1).then_inc(pool_did, seq.up())
            pool.wait_ge(pool_did, seq.n)
            pool.affine_select(out=hmask[:, :], in_=hmask[:, :], compare_op=ALU.is_ge, fill=0.0, base=D1 - 1,
                               pattern=[[D1, H]], channel_multiplier=-1).then_inc(pool_did, seq.up())
            pool.wait_ge(pool_did, seq.n)
            pool.sem_inc(pool_did, -seq.reset())
            pool.sem_inc(consts_ready, 2)
            pool.wait_ge(setup_done, 1)

            def below(par):
                for h in range(2):
                    pool.wait_ge(above_ready, 1)
                    pool.sem_inc(above_ready, -1)
                    pool.tensor_tensor(work[:, h, :], work[:, h, :], S[par][:, h, :], ALU.add).then_inc(below_ready, 1)

            def mask(nxt):
                for h in range(2):
                    pool.wait_ge(s_out, 1)
                    pool.sem_inc(s_out, -1)
                    pool.sem_inc(bank_free[BANK[f"s_{h}"]], 1)
                pool.sem_inc(s_copied, 1)
                pool.wait_ge(sizes_ready, 1)
                pool.sem_inc(sizes_ready, -1)
                for h in range(2):
                    for c0, c1 in COLS:
                        diag = S[nxt][:, h, c0:c0 + P] if h == 0 else S[nxt][:, h, c1 - P:c1]
                        last = pool.affine_select(out=diag, in_=diag, compare_op=ALU.is_ge, fill=-BIG, base=0,
                                                  pattern=[[-1, P]], channel_multiplier=1)
                last.then_inc(s_masked, 1)

            def first_guess():
                pool.tensor_tensor(fit[:, :, :], guess[:, :, :],
                                   sizes[:, :, :].rearrange("p h t -> p (h t)").unsqueeze(1).broadcast_to([P, 5, 4]),
                                   ALU.mult).then_inc(pool_did, seq.up())
                pool.wait_ge(pool_did, seq.n)
                pool.sem_inc(pool_did, -seq.reset())
                pool.sem_inc(neg_t_ready, 1)

            def first_correction():
                pool.wait_ge(signs_ready, 1)
                pool.sem_inc(signs_ready, -1)
                pool.tensor_tensor(moved[:, :], fit[:, 2, :], signsum[0][:, :], ALU.mult).then_inc(pool_did, seq.up())
                pool.wait_ge(pool_did, seq.n)
                pool.tensor_tensor(neg_t[:, :], moved[:, :], fit[:, 1, :], ALU.add).then_inc(pool_did, seq.up())
                pool.wait_ge(pool_did, seq.n)
                pool.sem_inc(neg_t_ready, 1)
                pool.tensor_tensor(neg_t_next[:, :], neg_t[:, :], fit[:, 4, :], ALU.add).then_inc(pool_did, seq.up())
                pool.wait_ge(pool_did, seq.n)
                pool.sem_inc(pool_did, -seq.reset())

            def second_correction():
                pool.wait_ge(signs_ready, 1)
                pool.sem_inc(signs_ready, -1)
                pool.tensor_tensor(moved[:, :], fit[:, 3, :], signsum[1][:, :], ALU.mult).then_inc(pool_did, seq.up())
                pool.wait_ge(pool_did, seq.n)
                pool.tensor_tensor(threshold[:, :], moved[:, :], neg_t_next[:, :], ALU.subtract).then_inc(threshold_ready, 1)
                pool.sem_inc(pool_did, -seq.reset())

            def normalise(par, h):
                if h == 0:
                    pool.wait_ge(kept_ready, 1)
                    pool.sem_inc(kept_ready, -1)
                    pool.sem_inc(S_free, 1)
                    pool.sem_inc(E_free, 1)
                for t, (c0, c1) in enumerate(COLS):
                    u = 2 * h + t
                    probs = Pr[par][:, PROBS[h][t]:PROBS[h][t] + c1 - c0]
                    last = pool.tensor_scalar(probs, probs, rsumA[par][:, u:u + 1], 1.0, ALU.mult, ALU.mult)
                if h == 1:
                    last.then_inc(probs_ready, 1)

            def rstd_of(a0, present):
                cols = [a0 + i for i, p in enumerate(present) if p]
                if cols:
                    lo, hi = cols[0], cols[-1] + 1
                    pool.wait_ge(var_ready, 1)
                    pool.sem_inc(var_ready, -1)
                    pool.tensor_scalar(var[:, lo:hi, :], mv[:, lo:hi, :, 1], EPS, 1.0, ALU.add, ALU.mult).then_inc(pool_did, seq.up())
                    pool.wait_ge(pool_did, seq.n)
                    pool.tensor_tensor(rstd[:, lo:hi, :], var[:, lo:hi, :],
                                       minus_half[:, 0:(hi - lo) * T].rearrange("p (a t) -> p a t", t=T), ALU.pow).then_inc(pool_did, seq.up())
                    pool.wait_ge(pool_did, seq.n)
                    pool.sem_inc(pool_did, -seq.reset())

            def normalised(dst, src, i, done):
                for t in range(T):
                    last = pool.tensor_scalar(dst[:, t, :], src[:, t, :], mv[:, i, t, 0:1], rstd[:, i, t:t + 1], ALU.subtract, ALU.mult)
                last.then_inc(pool_did, seq.up())
                pool.wait_ge(pool_did, seq.n)
                pool.sem_inc(pool_did, -seq.reset())
                pool.sem_inc(done, 1)

            def spread_keys(h0, h1):
                pool.tensor_tensor(keys1[:, h0:h1, :], kT[:, :].unsqueeze(1).broadcast_to([P, h1 - h0, TOK]),
                                   hmask[:, h0:h1].unsqueeze(2).broadcast_to([P, h1 - h0, TOK]), ALU.mult).then_inc(keys1_ready, 1)

            def step(n, par, at, on):
                front = ("P" if at == STEPS - 1 else "A") in on
                if "A" in on:
                    below(par)
                if at == 0 and "B" in on:
                    spread_keys(2, 8)
                if at == 1 and "B" in on:
                    spread_keys(8, 16)
                if at == 2 and "B" in on:
                    pool.tensor_copy(x2res[:, :, :], x2[:, :, :]).then_inc(pool_did, seq.up())
                    pool.wait_ge(pool_did, seq.n)
                    pool.sem_inc(pool_did, -seq.reset())
                if front:
                    mask(1 - par)
                    first_guess()
                if at == 0:
                    rstd_of(0, ("F" in on, "C" in on))
                    if "F" in on:
                        pool.sem_inc(rstd_ready, 1)
                    if "C" in on:
                        normalised(x3, x3pre, 1, x3_ready)
                if at == 2:
                    rstd_of(2, ("F" in on, "D" in on))
                    if "D" in on:
                        pool.sem_inc(rstd_ready, 1)
                if at == STEPS - 1 and "F" in on:
                    pool.wait_ge(kT_ready, 1)
                    pool.sem_inc(kT_ready, -1)
                    spread_keys(0, 2)
                if front:
                    first_correction()
                if at == 2 and "F" in on:
                    normalised(x2, x2pre, 2, x2_ready)
                if "A" in on:
                    normalise(par, 0)
                if front:
                    second_correction()
                if "A" in on:
                    normalise(par, 1)

            def iteration(it, on):
                steps(pool, lambda n, par, at: step(n, par, at, on), on)

            iterations(pool, iteration)

        @block.scalar
        def _(act):
            act.preload_act_table_set("exp_and_others")
            seq = Count()

            def copy(dst, src, **kw):
                return act.activation(dst, src, ACT.Copy, **kw)

            act.wait_ge(turned, 1)
            copy(WoT[:, 0:512], bank[0][:, :])
            copy(WoT[:, 512:1024], bank[1][:, :])
            copy(mkT, bank[2][:, :])
            for r in range(2):
                copy(mvT[:, :, r, :], bank[3][:, :].rearrange("p (c m) -> p c m", c=CH))
            for i, (w, scale) in enumerate(((WrT, 1.0), (WkT, 1.0), (WvT, 1.0), (qW, float(D1) ** -0.5))):
                copy(w[:, :], bank[4][:, i * P:(i + 1) * P], scale=scale)
            for i, w in enumerate((kW, vW)):
                last = copy(w[:, :], bank[5][:, i * P:(i + 1) * P])
            last.then_inc(turned_out, 2)
            act.wait_ge(fold_full, 1)
            scale = float(DH) ** -0.5
            A_flat = A_all[:, :, :].rearrange("p k c -> p (k c)")
            for b in range(4):
                copy(A_flat[:, b * 512:(b + 1) * 512], bank[b][:, :], scale=scale)
            for s in range(STEPS):
                last = copy(keys[:, s, 0, TOK:TOK + P], bank[4 + s // 4][:, (s % 4) * P:(s % 4 + 1) * P], scale=scale)
            last.then_inc(fold_out, 1)
            act.wait_ge(fold_full, 2)
            B_flat = B_all[:, :, :].rearrange("p k c -> p (k c)")
            for b, mem in enumerate((bank[4], bank[5], acc_bank, pv_bank)):
                copy(B_flat[:, b * 512:(b + 1) * 512], bank[b][:, :])
                for r in range(2):
                    rows = slice(r * MEM, (r + 1) * MEM)
                    last = copy(UM[rows, 2 * b:2 * b + 2, :], mem[rows, :].rearrange("p (s r c) -> p s r c", s=2, r=2)[:, :, r, :])
            last.then_inc(act_did, seq.up())
            act.wait_ge(act_did, seq.n)
            act.sem_inc(act_did, -seq.reset())
            act.wait_ge(consts_ready, 3)
            act.wait_ge(w_small, 25 * 16)
            act.sem_inc(setup_done, 1)
            act.sem_inc(S_free, 2)
            act.sem_inc(E_free, 1)

            def exp1():
                act.wait_ge(negmax1_ready, 1)
                act.sem_inc(negmax1_ready, -1)
                for t in range(T):
                    for h in range(2):
                        last = act.activation(E1[:, t, h, :], psum(f"s1_{t}")[:, h * TOK:(h + 1) * TOK], ACT.Exp,
                                              bias=negmax1[:, t, h:h + 1])
                    last.then_inc(bank_free[BANK["s1_0"]] if t == 0 else E1_ready, 1)

            def scores_out(par):
                act.wait_ge(S_free, 1)
                act.sem_inc(S_free, -1)
                for h in range(2):
                    act.wait_ge(s_full, 1)
                    act.sem_inc(s_full, -1)
                    copy(S[1 - par][:, h, :], psum(f"s_{h}")[:, :]).then_inc(s_out, 1)

            def keys_out(n):
                act.wait_ge(pg_full, 1)
                act.sem_inc(pg_full, -1)
                copy(keys[:, n, :, 0:TOK], psum("pg")[:, :].rearrange("p (h j) -> p h j", h=2)).then_inc(bank_free[BANK["pg"]], 1)

            def values_out(it, n, par):
                act.wait_ge(pu_full, 1)
                act.sem_inc(pu_full, -1)
                act.sem_inc(A_free[par], 1)
                copy(vals[:, (STEPS * (it + 1) + n) % RING, :, :, :].rearrange("p t h c -> p (t h c)"), psum("pu")[:, :])\
                    .then_inc(bank_free[BANK["pu"]], 1)

            def probs_out():
                for i in range(2):
                    act.wait_ge(pt_full, 1)
                    act.sem_inc(pt_full, -1)
                    if i == 1:
                        act.sem_inc(P_free, 1)
                    copy(PT[:, 4 * i:4 * i + 4, :].rearrange("p u i -> p (u i)"), psum(f"pt_{i}")[:, :]).then_inc(pt_ready, 1)

            def hidden_out(e, par):
                for b in range(2):
                    act.wait_ge(h_full, 1)
                    act.sem_inc(h_full, -1)
                    if b == 1:
                        act.sem_inc(W1_free[par], 1)
                    for f in range(2):
                        last = act.activation(hT[b][:, f, :], psum(f"h_{b}")[:, f * TOK:(f + 1) * TOK], ACT.Relu,
                                              bias=b1c[:, e, 2 * b + f:2 * b + f + 1])
                    last.then_inc(h_ready, 1)

            def probs1_out():
                for h in range(2):
                    act.wait_ge(p1_full, 1)
                    act.sem_inc(p1_full, -1)
                    copy(E1T[h][:, :, :, :].rearrange("p a b i -> p (a b i)"), psum(f"p1_{h}")[:, :]).then_inc(p1_ready, 1)

            def exp_scores(par):
                act.wait_ge(negmax_ready, 1)
                act.sem_inc(negmax_ready, -1)
                act.wait_ge(E_free, 1)
                act.sem_inc(E_free, -1)
                for h in range(2):
                    for t, (c0, c1) in enumerate(COLS):
                        last = act.activation(E[:, h, c0:c1], S[par][:, h, c0:c1], ACT.Exp, bias=negmax[par][:, h, t:t + 1])
                last.then_inc(E_ready, 1)

            def count(nxt, neg_t, out):
                act.wait_ge(neg_t_ready, 1)
                act.sem_inc(neg_t_ready, -1)
                for h in range(2):
                    for t, (c0, c1) in enumerate(COLS):
                        u = 2 * h + t
                        last = act.activation(signs[:, h, c0:c1], S[nxt][:, h, c0:c1], ACT.Sign, bias=neg_t[:, u:u + 1],
                                              accum_out=out[:, u:u + 1])
                last.then_inc(signs_ready, 1)

            def bank_out(use, cols, dst, full, ready):
                act.wait_ge(full, 1)
                act.sem_inc(full, -1)
                src = psum(use)[0:dst.shape[0], 0:cols]
                if len(dst.shape) == 3:
                    src = src.rearrange("p (t e) -> p t e", t=T)
                copy(dst, src).then_inc(act_did, seq.up())
                act.wait_ge(act_did, seq.n)
                act.sem_inc(act_did, -seq.reset())
                act.sem_inc(ready, 1)
                act.sem_inc(bank_free[BANK[use]], 1)

            def step(it, n, par, at, on):
                front = ("P" if at == STEPS - 1 else "A") in on
                e = expert_of(n, at, on)
                if at == STEPS - 1 and "P" in on:
                    copy(xT[:, :], xT_next[:, :]).then_inc(xT_ready, 1)
                if at == 0 and "P" in on:
                    bank_out("xt", TOK, xT_next[:, :], xt_full, xt_ready)
                    if "L" in on:
                        act.sem_inc(xload_free, 1)
                if at == 1 and "F" in on:
                    bank_out("x1t", TOK, x1T[:, 1:1 + TOK], x1t_full, x1T_ready)
                if "B" in on:
                    exp1()
                if at == 2 and "F" in on:
                    act.wait_ge(kr_full, 1)
                    act.sem_inc(kr_full, -1)
                    act.activation(rk[:, :], psum("kr")[:, 0:TOK], ACT.Relu).then_inc(act_did, seq.up())
                    act.activation(th[:, :, :].rearrange("p t c -> p (t c)"), psum("kr")[:, TOK:2 * TOK], ACT.Tanh,
                                   scale=0.5).then_inc(act_did, seq.up())
                    act.wait_ge(act_did, seq.n)
                    act.activation(kact[:, :], rk[:, :], ACT.Square).then_inc(kact_ready, 1)
                    act.sem_inc(act_did, -seq.reset())
                    act.sem_inc(bank_free[BANK["kr"]], 1)
                if at == 2 and "C" in on:
                    act.wait_ge(lg_shifted, 1)
                    act.sem_inc(lg_shifted, -1)
                    act.activation(lg[:, 1, :, :], lg[:, 0, :, :], ACT.Exp).then_inc(lg_exp, 1)
                if at == 0 and "B" in on:
                    act.wait_ge(vv_full, 1)
                    act.sem_inc(vv_full, -1)
                    copy(vals1[:, :, :, 0:D1], psum("vv")[:, 0:TOK].rearrange("p (t h d) -> p t h d", t=T, h=H))\
                        .then_inc(bank_free[BANK["vv"]], 1)
                if e is not None:
                    hidden_out(e, par)
                if ("F" if at == 0 else "A") in on:
                    probs_out()
                if front:
                    scores_out(par)
                if "A" in on:
                    exp_scores(par)
                if at == 1 and "C" in on:
                    bank_out("x3t", TOK, x3T[:, :], x3t_full, x3T_ready)
                if "B" in on:
                    probs1_out()
                if at == 2 and "C" in on:
                    bank_out("gt", TOK, gT[:, :], gt_full, gT_ready)
                if "P" in on:
                    keys_out(n)
                if front:
                    count(1 - par, fit[:, 0, :], signsum[0])
                if "P" in on:
                    values_out(it, n, par)
                if at == 1 and {"A", "P"} <= on:
                    act.sem_inc(xres_free, 1)
                if front:
                    count(1 - par, neg_t, signsum[1])
                if at == 1 and "C" in on:
                    bank_out("lg", T * EXP, lg_raw[:, :, :], lg_full, lg_ready)
                if at == 2 and "F" in on:
                    bank_out("x2t", TOK, x2T[:, :], x2t_full, x2T_ready)

            def iteration(it, on):
                steps(act, lambda n, par, at: step(it, n, par, at, on), on)

            iterations(act, iteration)

        @block.vector
        def _(dve):
            seq = Count()
            dve.wait_ge(w_big, 14 * 16)
            pre_hk = preB.rearrange("p (h k) -> p h k", h=H)
            post_hk = postB.rearrange("p (k h) -> p h k", h=H)
            for half in range(2):
                rows = slice(half * DH, (half + 1) * DH)
                dve.tensor_copy(preX[rows, :, :], pre_hk[rows, half:H:2, :]).then_inc(dve_did, seq.up())
                dve.tensor_copy(postX[rows, :, :], post_hk[rows, half:H:2, :]).then_inc(dve_did, seq.up())
            dve.wait_ge(dve_did, seq.n)

            def make_slab(n, w, mix):
                if n >= 2:
                    dve.wait_ge(slab_free, n - 1)
                dve.tensor_tensor(slab[n % 2].rearrange("p (k c) -> p k c", k=H), w.unsqueeze(1).broadcast_to([P, H, P]),
                                  mix.unsqueeze(2).broadcast_to([P, H, P]), ALU.mult).then_inc(slab_ready, 1)

            for c in range(CH):
                make_slab(c, WqN[:, c, :], preX[:, c, :])
            dve.wait_ge(turned_out, 2)
            for w, wr in ((qW, qWr), (kW, kWr)):
                dve.tensor_scalar(wr[:, 0:P:2], w[:, 1:P:2], -1.0, None, ALU.mult).then_inc(dve_did, seq.up())
                dve.tensor_copy(wr[:, 1:P:2], w[:, 0:P:2]).then_inc(dve_did, seq.up())
            dve.wait_ge(dve_did, seq.n)
            dve.sem_inc(dve_did, -seq.reset())
            dve.sem_inc(consts_ready, 1)
            for c in range(CH):
                make_slab(CH + c, WoT[:, c * P:(c + 1) * P], postX[:, c, :])
            dve.wait_ge(setup_done, 1)
            dve.sem_inc(P_free, 2)
            dve.sem_inc(yout_free, 16)

            def max1_of():
                for t in range(T):
                    dve.wait_ge(s1_full, 1)
                    dve.sem_inc(s1_full, -1)
                    last = dve.tensor_reduce(negmax1[:, t, :], psum(f"s1_{t}")[:, :].rearrange("p (h j) -> p h j", h=2),
                                             AX.X, ALU.max, negate=True)
                last.then_inc(negmax1_ready, 1)

            units = [(2 * h + t, h, c0, c1) for h in range(2) for t, (c0, c1) in enumerate(COLS)]

            def count_above(par):
                dve.wait_ge(threshold_ready, 1)
                dve.sem_inc(threshold_ready, -1)
                for u, h, c0, c1 in units:
                    last = dve.scalar_tensor_tensor(out=work[:, h, c0:c1], in0=S[par][:, h, c0:c1], scalar=threshold[:, u:u + 1],
                                                    in1=taken[:, 0:1].broadcast_to([P, c1 - c0]), op0=ALU.is_ge, op1=ALU.mult,
                                                    accum_out=above[:, u:u + 1])
                    if u == 1:
                        last.then_inc(above_ready, 1)
                last.then_inc(dve_did, seq.up())
                dve.wait_ge(dve_did, seq.n)
                dve.sem_inc(above_ready, 1)
                dve.tensor_scalar(rank[:, :], above[:, :], 1 / TAKEN * -1.0, float(TOPK - 1), ALU.mult, ALU.add).then_inc(dve_did, seq.up())

            def upper_eight():
                ranked = seq.n
                got = {}
                for u, h, c0, c1 in units:
                    if u % 2 == 0:
                        dve.wait_ge(below_ready, 1)
                        dve.sem_inc(below_ready, -1)
                    dve.max(window[:, u, 0:8], work[:, h, c0:c1]).then_inc(dve_did, seq.up())
                    got[u] = seq.n
                    if u == 0:
                        dve.wait_ge(dve_did, ranked)
                        dve.tensor_scalar(deep[:, :], rank[:, :], WINDOW - 0.5, None, ALU.is_gt).then_inc(dve_did, seq.up())
                        compared = seq.n
                    if u == 1:
                        dve.wait_ge(dve_did, compared)
                        dve.scalar_tensor_tensor(out=missed[:, :], in0=rank[:, :], scalar=-0.5, in1=deep[:, :], op0=ALU.is_lt,
                                                 op1=ALU.add).then_inc(missed_ready, 1)
                for u, h, c0, c1 in units:
                    dve.wait_ge(dve_did, got[u])
                    dve.match_replace(work[:, h, c0:c1], window[:, u, 0:8], work[:, h, c0:c1], -BIG).then_inc(dve_did, seq.up())
                    got[u] = seq.n
                return got

            def lower_eight(got):
                def eight(u, h, c0, c1):
                    dve.wait_ge(dve_did, got[u])
                    dve.max(window[:, u, 8:WINDOW], work[:, h, c0:c1]).then_inc(dve_did, seq.up())
                    got[u] = seq.n

                def choose(u):
                    dve.wait_ge(dve_did, got[u])
                    dve.scalar_tensor_tensor(out=chosen[:, u, :], in0=place[:, :], scalar=rank[:, u:u + 1], in1=window[:, u, :],
                                             op0=ALU.is_equal, op1=ALU.mult, accum_out=kth[:, u:u + 1]).then_inc(dve_did, seq.up())

                eight(*units[0])
                for u in range(1, len(units)):
                    eight(*units[u])
                    choose(u - 1)
                choose(len(units) - 1)

            def all_eights(par):
                for r in range(TOPK // 8):
                    src = S[par] if r <= 1 else work
                    if r > 0:
                        for u, h, c0, c1 in units:
                            dve.match_replace(work[:, h, c0:c1], top[:, u, :], src[:, h, c0:c1], -BIG).then_inc(dve_did, seq.up())
                        dve.wait_ge(dve_did, seq.n)
                        src = work
                    for u, h, c0, c1 in units:
                        dve.max(top[:, u, :], src[:, h, c0:c1]).then_inc(dve_did, seq.up())
                    dve.wait_ge(dve_did, seq.n)
                dve.tensor_copy(kth[:, :], top[:, :, 7]).then_inc(dve_did, seq.up())
                dve.wait_ge(dve_did, seq.n)
                dve.sem_inc(dve_did, -seq.reset())

            def count_missed():
                dve.wait_ge(missed_full, 1)
                dve.sem_inc(missed_full, -1)
                dve.tensor_reduce(missed_n[:, :], psum("miss")[0:1, 0:4], AX.X, ALU.max).then_inc(dve_did, seq.up())

            def repair(par):
                if seq.n:
                    dve.wait_ge(dve_did, seq.n)
                    dve.sem_inc(dve_did, -seq.reset())
                n_missed = dve.value_load(missed_n[0:1, 0:1])
                with dve.If(n_missed > 0):
                    all_eights(par)

            def sum_sizes(nxt):
                dve.wait_ge(s_copied, 1)
                dve.sem_inc(s_copied, -1)
                for t, (c0, c1) in enumerate(COLS):
                    last = dve.tensor_reduce(sizes[:, :, t], S[nxt][:, :, c0:c1:SAMPLE], AX.X, ALU.add, apply_absolute_value=True)
                last.then_inc(sizes_ready, 1)

            def maxima(nxt):
                dve.wait_ge(s_masked, 1)
                dve.sem_inc(s_masked, -1)
                for t, (c0, c1) in enumerate(COLS):
                    last = dve.tensor_reduce(negmax[nxt][:, :, t], S[nxt][:, :, c0:c1], AX.X, ALU.max, negate=True)
                last.then_inc(negmax_ready, 1)

            def keep(par):
                dve.wait_ge(E_ready, 1)
                dve.sem_inc(E_ready, -1)
                dve.wait_ge(P_free, 1)
                dve.sem_inc(P_free, -1)
                for u, h, c0, c1 in units:
                    dve.scalar_tensor_tensor(out=Pr[par][:, PROBS[h][u % T]:PROBS[h][u % T] + c1 - c0], in0=S[par][:, h, c0:c1], scalar=kth[:, u:u + 1],
                                             in1=E[:, h, c0:c1], op0=ALU.is_ge, op1=ALU.mult,
                                             accum_out=psumA[:, u:u + 1]).then_inc(dve_did, seq.up())
                dve.wait_ge(dve_did, seq.n)
                dve.reciprocal(rsumA[par][:, :], psumA[:, :]).then_inc(kept_ready, 1)
                dve.wait_ge(dve_did, seq.n)
                dve.sem_inc(dve_did, -seq.reset())

            def add_expert(e):
                dve.wait_ge(y_full, 1)
                dve.sem_inc(y_full, -1)
                for t in range(T):
                    dve.scalar_tensor_tensor(out=yacc[:, t, :], in0=psum("y")[:, t * P:(t + 1) * P],
                                             scalar=gates[:, t, bass.ds(e, 1)], in1=yacc[:, t, :],
                                             op0=ALU.mult, op1=ALU.add).then_inc(dve_did, seq.up())
                dve.wait_ge(dve_did, seq.n)
                dve.sem_inc(dve_did, -seq.reset())
                dve.sem_inc(bank_free[BANK["y"]], 1)

            def statistics(src, i):
                for t in range(T):
                    dve.bn_stats(stats[:, i, t, :], src[:, t, :]).then_inc(dve_did, seq.up())
                dve.wait_ge(dve_did, seq.n)
                for t in range(T):
                    dve.bn_aggr(mv[:, i, t, :], stats[:, i, t, :]).then_inc(dve_did, seq.up())

            def over_experts(x):
                return x.unsqueeze(2).broadcast_to([P, T, EXP])

            def shift_logits():
                dve.wait_ge(lg_ready, 1)
                dve.sem_inc(lg_ready, -1)
                dve.tensor_reduce(lgs[:, 0, :], lg_raw[:, :, :], AX.X, ALU.max).then_inc(dve_did, seq.up())
                dve.wait_ge(dve_did, seq.n)
                dve.tensor_tensor(lg[:, 0, :, :], lg_raw[:, :, :], over_experts(lgs[:, 0, :]), ALU.subtract).then_inc(lg_shifted, 1)

            def route():
                dve.wait_ge(lg_exp, 1)
                dve.sem_inc(lg_exp, -1)
                dve.tensor_reduce(lgs[:, 1, :], lg[:, 1, :, :], AX.X, ALU.add).then_inc(dve_did, seq.up())
                dve.wait_ge(dve_did, seq.n)
                dve.reciprocal(lgs[:, 2, :], lgs[:, 1, :]).then_inc(dve_did, seq.up())
                dve.wait_ge(dve_did, seq.n)
                dve.tensor_tensor(lg[:, 2, :, :], lg[:, 1, :, :], over_experts(lgs[:, 2, :]), ALU.mult).then_inc(dve_did, seq.up())
                dve.wait_ge(dve_did, seq.n)
                for t in range(T):
                    dve.scalar_tensor_tensor(out=lg[:, 3, t, :], in0=lg[:, 2, t, :], scalar=lgs[:, 2, t:t + 1], in1=first[:, :],
                                             op0=ALU.is_ge, op1=ALU.mult).then_inc(dve_did, seq.up())
                dve.wait_ge(dve_did, seq.n)
                dve.tensor_reduce(lgs[:, 3, :], lg[:, 3, :, :], AX.X, ALU.max).then_inc(dve_did, seq.up())
                dve.wait_ge(dve_did, seq.n)
                for t in range(T):
                    last = dve.scalar_tensor_tensor(out=gates[:, t, :], in0=lg[:, 3, t, :], scalar=lgs[:, 3, t:t + 1],
                                                    in1=lg[:, 2, t, :], op0=ALU.is_ge, op1=ALU.mult)
                last.then_inc(gates_ready, 1)

            def start_sum():
                dve.wait_ge(base_full, 1)
                dve.sem_inc(base_full, -1)
                dve.tensor_tensor(yacc[:, :, :], psum("base")[:, 0:TOK].rearrange("p (t c) -> p t c", t=T), x3[:, :, :],
                                  ALU.add).then_inc(dve_did, seq.up())
                dve.wait_ge(dve_did, seq.n)
                dve.sem_inc(dve_did, -seq.reset())
                dve.sem_inc(bank_free[BANK["base"]], 1)

            def end_attention1():
                dve.wait_ge(pv_full, 1)
                dve.sem_inc(pv_full, -1)
                dve.reciprocal(rsum1[:, :, :], pv[:, :, :, D1]).then_inc(dve_did, seq.up())
                dve.wait_ge(dve_did, seq.n)
                o1_h = o1[:, :, :].rearrange("p t (h d) -> p t h d", h=H)
                dve.tensor_tensor(o1_h, pv[:, :, :, 0:D1], rsum1[:, :, :].unsqueeze(3).broadcast_to([P, T, H, D1]),
                                  ALU.mult).then_inc(dve_did, seq.up())
                dve.wait_ge(dve_did, seq.n)
                dve.sem_inc(pv_free, 1)
                dve.tensor_tensor(x3pre[:, :, :], o1[:, :, :], x2res[:, :, :], ALU.add).then_inc(dve_did, seq.up())
                dve.wait_ge(dve_did, seq.n)
                statistics(x3pre, 1)

            def mix_tokens():
                dve.wait_ge(x1T_ready, 1)
                dve.sem_inc(x1T_ready, -1)
                dve.tensor_tensor(dT[:, :], x1T[:, 1:1 + TOK], x1T[:, 0:TOK], ALU.subtract).then_inc(dve_did, seq.up())
                dve.wait_ge(dve_did, seq.n)
                for dst, mu in ((xrT, mu_r), (xkT, mu_k)):
                    last = dve.scalar_tensor_tensor(out=dst[:, :], in0=dT[:, :], scalar=mu[:, 0:1], in1=x1T[:, 0:TOK],
                                                    op0=ALU.mult, op1=ALU.add)
                last.then_inc(mixed_ready, 1)

            def end_channel_mix():
                dve.wait_ge(v_full, 1)
                dve.sem_inc(v_full, -1)
                v = psum("v")[:, 0:TOK].rearrange("p (t c) -> p t c", t=T)
                dve.scalar_tensor_tensor(out=x2pre[:, :, :], in0=th[:, :, :], scalar=1.0, in1=v, op0=ALU.add, op1=ALU.mult).then_inc(dve_did, seq.up())
                dve.wait_ge(dve_did, seq.n)
                dve.sem_inc(bank_free[BANK["v"]], 1)
                dve.scalar_tensor_tensor(out=x2pre[:, :, :], in0=x2pre[:, :, :], scalar=0.5, in1=x1[:, :, :],
                                         op0=ALU.mult, op1=ALU.add).then_inc(dve_did, seq.up())
                dve.wait_ge(dve_did, seq.n)
                statistics(x2pre, 2)

            def rotate():
                for i, (use, full, dst) in enumerate((("q", q_full, qT), ("k", k_full, kT))):
                    dve.wait_ge(full, 1)
                    dve.sem_inc(full, -1)
                    for j, table in enumerate((cosT, sinT)):
                        dve.tensor_tensor(rope[:, 2 * i + j, :], psum(use)[:, j * TOK:(j + 1) * TOK], table[:, :], ALU.mult).then_inc(dve_did, seq.up())
                    dve.wait_ge(dve_did, seq.n)
                    dve.sem_inc(bank_free[BANK[use]], 1)
                    last = dve.tensor_tensor(dst[:, :], rope[:, 2 * i, :], rope[:, 2 * i + 1, :], ALU.add)
                last.then_inc(kT_ready, 1)

            def step(n, par, at, on):
                front = ("P" if at == STEPS - 1 else "A") in on
                e = expert_of(n, at, on)
                if "B" in on:
                    max1_of()
                if "A" in on:
                    count_above(par)
                if at == 0 and "C" in on:
                    end_attention1()
                if at == 1 and "F" in on:
                    mix_tokens()
                if at == 2 and "C" in on:
                    shift_logits()
                if at == 2 and "D" in on:
                    statistics(yacc, 3)
                if at == 2 and "C" in on:
                    route()
                if "A" in on:
                    got = upper_eight()
                    count_missed()
                    missed_counted = seq.n
                if front:
                    sum_sizes(1 - par)
                if "A" in on:
                    dve.wait_ge(dve_did, missed_counted)
                    dve.sem_inc(bank_free[BANK["miss"]], 1)
                if at == 0 and "F" in on:
                    dve.wait_ge(acc_full, 1)
                    dve.sem_inc(acc_full, -1)
                    statistics(acc, 0)
                if at == 2 and "F" in on:
                    end_channel_mix()
                if (at == 0 and on & {"F", "C"}) or (at == 2 and on & {"F", "D"}):
                    dve.wait_ge(dve_did, seq.n)
                    dve.sem_inc(var_ready, 1)
                if "A" in on:
                    lower_eight(got)
                if at == STEPS - 1 and "F" in on:
                    rotate()
                if front:
                    maxima(1 - par)
                if "A" in on:
                    repair(par)
                if at == 0 and "F" in on:
                    dve.wait_ge(rstd_ready, 1)
                    dve.sem_inc(rstd_ready, -1)
                    for t in range(T):
                        last = dve.tensor_scalar(x1[:, t, :], acc[:, t, :], mv[:, 0, t, 0:1], rstd[:, 0, t:t + 1],
                                                 ALU.subtract, ALU.mult)
                    last.then_inc(x1_ready, 1)
                if at == 2 and "D" in on:
                    dve.wait_ge(rstd_ready, 1)
                    dve.sem_inc(rstd_ready, -1)
                    dve.wait_ge(yout_free, 16)
                    dve.sem_inc(yout_free, -16)
                    for t in range(T):
                        dve.tensor_scalar(yout[:, t, :], yacc[:, t, :], mv[:, 3, t, 0:1], rstd[:, 3, t:t + 1],
                                          ALU.subtract, ALU.mult).then_inc(dve_did, seq.up())
                    dve.wait_ge(dve_did, seq.n)
                    dve.sem_inc(yout_full, 1)
                if "A" in on:
                    keep(par)
                if at == 2 and "C" in on:
                    start_sum()
                if e is not None:
                    add_expert(e)
                if seq.n:
                    dve.wait_ge(dve_did, seq.n)
                    dve.sem_inc(dve_did, -seq.reset())

            def iteration(it, on):
                steps(dve, lambda n, par, at: step(n, par, at, on), on)

            iterations(dve, iteration)

        @block.tensor
        def _(pe):
            pe.wait_ge(consts_ready, 2)
            pe.wait_ge(w_big, 14 * 16)
            for c in range(CH):
                pe.transpose(bank[c // 4][:, (c % 4) * P:(c % 4 + 1) * P], WoN[:, c, :], ident[:, :])
                pe.transpose(bank[2][:, c * MEM:(c + 1) * MEM], mkN[:, c * P:(c + 1) * P], ident[0:MEM, 0:MEM])
                pe.transpose(bank[3][:, c * MEM:(c + 1) * MEM], mvN[:, c * P:(c + 1) * P], ident[0:MEM, 0:MEM])
            for i, (b, k) in enumerate(((4, 0), (4, 1), (4, 2), (4, 3), (5, 0), (5, 1))):
                last = pe.transpose(bank[b][:, k * P:(k + 1) * P], smallN[:, i * P:(i + 1) * P], ident[:, :])
            last.then_inc(turned, 1)
            pe.wait_ge(turned_out, 2)
            for c in range(CH):
                pe.wait_ge(slab_ready, c + 1)
                for b in range(4):
                    pe.matmul(bank[b][:, :], WkN[:, c, :], slab[c % 2][:, b * 512:(b + 1) * 512], start=(c == 0), stop=(c == CH - 1))
                for k in range(H):
                    last = pe.matmul(bank[4 + k // 8][:, (k % 8) * MEM:(k % 8 + 1) * MEM], slab[c % 2][:, k * P:(k + 1) * P],
                                     mkT[:, c * MEM:(c + 1) * MEM], start=(c == 0 and k % 8 == 0), stop=(c == CH - 1),
                                     skip_group_check=True)
                last.then_inc(slab_free, 1)
            pe.drain().then_inc(fold_full, 1)
            pe.wait_ge(fold_out, 1)
            for c in range(CH):
                pe.wait_ge(slab_ready, CH + c + 1)
                for b, mem in enumerate((bank[4], bank[5], acc_bank, pv_bank)):
                    sl = slab[c % 2][:, b * 512:(b + 1) * 512]
                    pe.matmul(bank[b][:, :], WvN[:, c, :], sl, start=(c == 0), stop=(c == CH - 1))
                    last = pe.matmul(mem[:, :], mvT[:, c, :, :], sl, start=(c == 0), stop=(c == CH - 1))
                last.then_inc(slab_free, 1)
            pe.drain().then_inc(fold_full, 1)
            pe.wait_ge(setup_done, 1)
            for f in bank_free:
                pe.sem_inc(f, 1)

            def take_bank(use):
                pe.wait_ge(bank_free[BANK[use]], 1)
                pe.sem_inc(bank_free[BANK[use]], -1)
                return psum(use)

            def give_bank(use):
                pe.sem_inc(bank_free[BANK[use]], 1)

            keys_flat = keys[:, :, :, :].rearrange("p s a j -> p s (a j)")

            def scores1(n):
                for t in range(T):
                    b = take_bank(f"s1_{t}")
                    pe.matmul(b[:, :].rearrange("p (h j) -> p h j", h=2), qT[:, t * P:(t + 1) * P],
                              keys1[:, bass.ds(2 * n, 2), :], start=True, stop=True).then_inc(s1_full, 1)

            def scores(n, h):
                b = take_bank(f"s_{h}")
                for t, (c0, c1) in enumerate(COLS):
                    last = pe.matmul(b[:, c0:c1], xT[:, t * P:(t + 1) * P], keys_flat[:, n, KEYS[h][t][0]:KEYS[h][t][1]],
                                     start=True, stop=True)
                last.then_inc(s_full, 1)

            def project(n, par):
                pe.wait_ge(A_full[par], 16)
                pe.sem_inc(A_full[par], -16)
                b = take_bank("pg")
                for t in range(T):
                    pe.matmul(b[:, t * P:(t + 1) * P], A_st[par][:, 0, :], xT_next[:, (1 - t) * P:(2 - t) * P], start=True, stop=True)
                last = pe.matmul(b[:, TOK:2 * TOK], A_st[par][:, 1, :], xT_next[:, :], start=True, stop=True)
                last.then_inc(pg_full, 1)
                b = take_bank("pu")
                for t in range(T):
                    last = pe.matmul(b[:, t * TOK:(t + 1) * TOK].rearrange("p (h c) -> p h c", h=2),
                                     xT_next[:, t * P:(t + 1) * P], B_all[:, bass.ds(2 * n, 2), :], start=True, stop=True)
                last.then_inc(pu_full, 1)

            def turn_probs(prev):
                pe.wait_ge(probs_ready, 1)
                pe.sem_inc(probs_ready, -1)
                starts = (*MEM_AT, *TOKENS_AT[0], *TOKENS_AT[1])
                for i in range(2):
                    b = take_bank(f"pt_{i}")
                    for j in range(4):
                        c0 = starts[4 * i + j]
                        last = pe.transpose(b[:, j * P:(j + 1) * P], Pr[prev][:, c0:c0 + P], ident[:, :])
                    last.then_inc(pt_full, 1)

            def attend(n, ring, last_of_batch=False):
                terms = [(t, UM[:, n, :]) for t in range(T)]
                terms += [(t, vals[:, ring, jt, h, :]) for h in range(2) for t, jt in ((0, 0), (1, 0), (1, 1))]
                for i, (t, v) in enumerate(terms):
                    if i % 4 == 0:
                        pe.wait_ge(pt_ready, 1)
                        pe.sem_inc(pt_ready, -1)
                        give_bank(f"pt_{i // 4}")
                    last = pe.matmul(acc[:, t, :], PT[:, i, :], v, start=False, stop=last_of_batch and i in (5, 7),
                                     skip_group_check=True)
                if last_of_batch:
                    last.then_inc(acc_full, 1)

            def hidden(par):
                pe.wait_ge(W1_full[par], 16)
                pe.sem_inc(W1_full[par], -16)
                for i in range(2):
                    b = take_bank(f"h_{i}")
                    for f in range(2):
                        c = 2 * i + f
                        last = pe.matmul(b[:, f * TOK:(f + 1) * TOK], W1_st[par][:, c * P:(c + 1) * P], x3T[:, :], start=True, stop=True)
                    last.then_inc(h_full, 1)

            def turn_probs1():
                for h in range(2):
                    b = take_bank(f"p1_{h}")
                    for jt in range(T):
                        for t in range(T):
                            last = pe.transpose(b[:, (2 * jt + t) * P:(2 * jt + t + 1) * P], E1[:, t, h, jt * P:(jt + 1) * P], ident[:, :])
                    last.then_inc(p1_full, 1)

            def attend1(n, last_of_batch):
                for h in range(2):
                    pe.wait_ge(p1_ready, 1)
                    pe.sem_inc(p1_ready, -1)
                    give_bank(f"p1_{h}")
                    for t in range(T):
                        for jt in range(T):
                            last = pe.matmul(pv[:, t, 2 * n + h, :], E1T[h][:, jt, t, :], vals1[:, jt, 2 * n + h, :],
                                             start=(jt == 0), stop=(jt == T - 1))
                if last_of_batch:
                    last.then_inc(pv_full, 1)

            def experts_out(e):
                b = take_bank("y")
                for t in range(T):
                    for f in range(FF // P):
                        last = pe.matmul(b[:, t * P:(t + 1) * P], hT[f // 2][:, f % 2, t * P:(t + 1) * P], W2[:, e, f, :],
                                         start=(f == 0), stop=(f == FF // P - 1))
                last.then_inc(y_full, 1)

            def turn(use, src, full):
                b = take_bank(use)
                for t in range(T):
                    last = pe.transpose(b[:, t * P:(t + 1) * P], src[:, t, :], ident[:, :])
                last.then_inc(full, 1)

            def per_tile(b, c0, lhsT, w):
                for t in range(T):
                    last = pe.matmul(b[:, c0 + t * P:c0 + (t + 1) * P], lhsT[:, t * P:(t + 1) * P], w[:, :], start=True, stop=True)
                return last

            def step(it, n, par, at, on):
                last = at == STEPS - 1
                e = expert_of(n, at, on)
                if at == 0 and "P" in on:
                    pe.wait_ge(xload_full, 16)
                    pe.sem_inc(xload_full, -16)
                    turn("xt", xload, xt_full)
                if at == 0 and "B" in on:
                    pe.wait_ge(keys1_ready, 1)
                    pe.sem_inc(keys1_ready, -1)
                    scores1(0)
                if at == 1 and "F" in on:
                    pe.wait_ge(x1_ready, 1)
                    pe.sem_inc(x1_ready, -1)
                    turn("x1t", x1, x1t_full)
                if e is not None:
                    hidden(par)
                if ("F" if at == 0 else "A") in on:
                    turn_probs(1 - par)
                if last and "P" in on:
                    pe.wait_ge(xT_ready, 1)
                    pe.sem_inc(xT_ready, -1)
                for h in range(2):
                    if h == 1 and "B" in on:
                        pe.wait_ge(E1_ready, 1)
                        pe.sem_inc(E1_ready, -1)
                        give_bank("s1_1")
                    if ("P" if last else "A") in on:
                        scores(0 if last else n + 1, h)
                    if e is not None:
                        pe.wait_ge(h_ready, 1)
                        pe.sem_inc(h_ready, -1)
                        give_bank(f"h_{h}")
                if "A" in on:
                    pe.wait_ge(missed_ready, 1)
                    pe.sem_inc(missed_ready, -1)
                    pe.matmul(take_bank("miss")[0:1, 0:4], ones[:, 0:1], missed[:, :], start=True, stop=True).then_inc(missed_full, 1)
                if at == 1 and "A" in on:
                    pe.wait_ge(xres_full, 16)
                    pe.sem_inc(xres_full, -16)
                    pe.matmul(acc_bank[:, 0:TOK], ident[:, :], xres[:, :, :].rearrange("p t c -> p (t c)"), start=True, stop=False,
                              skip_group_check=True)
                    for t in range(T):
                        pe.matmul(acc[:, t, :], ones[0:1, :], brow[:, :], start=False, stop=False, skip_group_check=True)
                if at == 0 and "F" in on:
                    attend(STEPS - 1, (STEPS * it - 1) % RING, last_of_batch=True)
                if at != 0 and "A" in on:
                    attend(n - 1, (STEPS * it + n - 1) % RING)
                if at == 1 and "C" in on:
                    pe.wait_ge(x3_ready, 1)
                    pe.sem_inc(x3_ready, -1)
                    turn("x3t", x3, x3t_full)
                if at == 2 and "F" in on:
                    pe.wait_ge(kact_ready, 1)
                    pe.sem_inc(kact_ready, -1)
                    per_tile(take_bank("v"), 0, kact, WvT).then_inc(v_full, 1)
                if "B" in on:
                    turn_probs1()
                if at == 2 and "C" in on:
                    pe.wait_ge(gates_ready, 1)
                    pe.sem_inc(gates_ready, -1)
                    b = take_bank("gt")
                    for t in range(T):
                        turned_gates = pe.transpose(b[0:EXP, t * P:(t + 1) * P], gates[:, t, :], ident[:, :])
                    turned_gates.then_inc(gt_full, 1)
                if last and "F" in on:
                    pe.wait_ge(x2T_ready, 1)
                    pe.sem_inc(x2T_ready, -1)
                    for use, w, wr, full in (("q", qW, qWr, q_full), ("k", kW, kWr, k_full)):
                        b = take_bank(use)
                        pe.matmul(b[:, 0:TOK], w[:, :], x2T[:, :], start=True, stop=True)
                        pe.matmul(b[:, TOK:2 * TOK], wr[:, :], x2T[:, :], start=True, stop=True).then_inc(full, 1)
                if "P" in on:
                    if at == 0:
                        pe.wait_ge(xt_ready, 1)
                        pe.sem_inc(xt_ready, -1)
                    project(n, par)
                if not last and "B" in on:
                    if at in (0, 2):
                        pe.wait_ge(keys1_ready, 1)
                        pe.sem_inc(keys1_ready, -1)
                    scores1(n + 1)
                if e is not None:
                    experts_out(e)
                if at == 2 and "C" in on:
                    pe.wait_ge(gT_ready, 1)
                    pe.sem_inc(gT_ready, -1)
                    per_tile(take_bank("base"), 0, gT, b2).then_inc(base_full, 1)
                if at == 0 and "C" in on:
                    pe.wait_ge(pv_free, 1)
                    pe.sem_inc(pv_free, -1)
                if "B" in on:
                    attend1(n, last)
                if at == 1 and "C" in on:
                    pe.wait_ge(x3T_ready, 1)
                    pe.sem_inc(x3T_ready, -1)
                    b = take_bank("lg")
                    for t in range(T):
                        pe.matmul(b[:, t * EXP:(t + 1) * EXP], x3T[:, t * P:(t + 1) * P], rW[:, :], start=True, stop=False)
                        logits = pe.matmul(b[:, t * EXP:(t + 1) * EXP], ones[0:1, :], rb[:, :], start=False, stop=True)
                    logits.then_inc(lg_full, 1)
                if at == 1 and "F" in on:
                    pe.wait_ge(mixed_ready, 1)
                    pe.sem_inc(mixed_ready, -1)
                    b = take_bank("kr")
                    pe.matmul(b[:, 0:TOK], WkT[:, :], xkT[:, :], start=True, stop=True)
                    per_tile(b, TOK, xrT, WrT).then_inc(kr_full, 1)
                if at == 2 and "F" in on:
                    pe.wait_ge(x2_ready, 1)
                    pe.sem_inc(x2_ready, -1)
                    turn("x2t", x2, x2t_full)
                if last and "F" in on:
                    per_tile(take_bank("vv"), 0, x2T, vW).then_inc(vv_full, 1)

            def iteration(it, on):
                steps(pe, lambda n, par, at: step(it, n, par, at, on), on)

            iterations(pe, iteration)


INPUTS = ("L0_attn_x", "L0_attn_Wq", "L0_attn_Wk", "L0_attn_Wv", "L0_attn_pre_proj", "L0_attn_post_proj", "L0_attn_mem_k",
          "L0_attn_mem_v", "L0_attn_Wout", "L0_attn_bout", "L0_ffn_W_r", "L0_ffn_W_k", "L0_ffn_W_v", "L0_ffn_mu_r",
          "L0_ffn_mu_k", "L1_attn_Wq", "L1_attn_Wk", "L1_attn_Wv", "L1_ffn_router_W", "L1_ffn_router_b", "L1_ffn_W1",
          "L1_ffn_b1", "L1_ffn_W2", "L1_ffn_b2")


def kernel(**inputs):
    import numpy as np
    import concourse.bacc as bacc
    from concourse.bass_utils import run_bass_kernel_spmd

    arrays = {n: np.ascontiguousarray(inputs[n]) for n in INPUTS}
    pos = np.arange(TOK, dtype=np.float32)
    inv = np.power(np.float32(10000.0), -2.0 * np.arange(D1 // 2, dtype=np.float32) / D1).astype(np.float32)
    angle = np.tile(np.repeat(inv[:, None] * pos[None, :], 2, axis=0), (H, 1))
    arrays["cosT"] = np.cos(angle).astype(np.float32)
    arrays["sinT"] = np.sin(angle).astype(np.float32)
    arrays["guess"] = threshold_tables()
    nc = bacc.Bacc("TRN2", target_bir_lowering=False, num_devices=1)
    a = {n: nc.dram_tensor(f"{n}_dram", v.shape, F32, kind="ExternalInput").ap() for n, v in arrays.items()}
    shape = arrays["L0_attn_x"].shape
    a["out"] = nc.dram_tensor("out_dram", shape, F32, kind="ExternalOutput").ap()
    build(nc, a, shape[0])
    r = run_bass_kernel_spmd(nc, [{f"{n}_dram": v for n, v in arrays.items()}], core_ids=[0])
    return r.results[0]["out_dram"]
```
